# Optimizing a Trainium2 kernel written in Bass

```python
import numpy as np
import jax
import jax.numpy as jnp

def _softmax(x, axis=-1):
    return jax.nn.softmax(x, axis=axis)

def _gelu(x):
    return jax.nn.gelu(x, approximate=True)

def _silu(x):
    return jax.nn.silu(x)

def _sigmoid(x):
    return jax.nn.sigmoid(x)

def _layernorm(x, axis=-1, eps=1e-05):
    m = jnp.mean(x, axis=axis, keepdims=True)
    v = jnp.var(x, axis=axis, keepdims=True)
    return (x - m) / jnp.sqrt(v + eps)

def _scatter_add(tgt, idx, src, axis=0):
    return tgt.at[idx].add(src)

def _segment_sum(src, seg, n):
    return jax.ops.segment_sum(src, seg, n)
kernel_name = 'mk_decoder_preln_d1_seqx_r8_245d09'

def setup_inputs(seed: int=0):
    np.random.seed(seed)
    _w = jnp.asarray

    def _rec_inputs():
        import jax
        import jax.numpy as jnp
        _rk = jax.random.key(seed)
        x = 7.22e-05 + 1 * jax.random.normal(jax.random.fold_in(_rk, 1), (8, 256, 128), jnp.float32)
        _lenS = 256 - jax.random.randint(jax.random.fold_in(_rk, 7), (8,), 0, max(1, 256 // 4) + 1, jnp.int32)
        _lenS2 = 512 - jax.random.randint(jax.random.fold_in(_rk, 8), (8,), 0, max(1, 512 // 4) + 1, jnp.int32)
        _ctx_1024P = jax.random.normal(jax.random.fold_in(_rk, 11), (8, 16, 128), jnp.float32)
        _ctx_1024c = jax.random.dirichlet(jax.random.fold_in(_rk, 511), 0.3 * jnp.ones((16,), jnp.float32), (8, 512))
        _ctx_1024t = jnp.einsum('bsk,bkd->bsd', _ctx_1024c, _ctx_1024P)
        _ctx_1024t = _ctx_1024t * jax.lax.rsqrt(jnp.mean(jnp.square(_ctx_1024t)) + 1e-12) * 0.953939
        ctx_1024 = 4.13588e-05 + 0.999923 * (_ctx_1024t + 0.3 * jax.random.normal(jax.random.fold_in(_rk, 611), (8, 512, 128), jnp.float32))
        _validS = jnp.arange(256)[None, :] < _lenS[:, None]
        _validS2 = jnp.arange(512)[None, :] < _lenS2[:, None]
        _causal = jnp.tril(jnp.ones((256, 256), dtype=bool))
        mask_Bx1xSxS2_bf1 = jnp.ones((8, 1, 256, 512), dtype=bool)
        return (x, ctx_1024, mask_Bx1xSxS2_bf1)
    x, ctx_1024, mask_Bx1xSxS2_bf1 = _rec_inputs()

    def _L0_attn_setup():
        import jax, jax.numpy as jnp
        import numpy as np
        B, N, DM, H = (1, 256, 128, 16)
        CURV = 1.0
        key = jax.random.key(seed)
        ks = jax.random.split(key, 5)
        s = 1.0 / np.sqrt(DM)
        x = jax.random.normal(ks[0], (B, N, DM), dtype=jnp.float32)
        Wq = jax.random.uniform(ks[1], (DM, DM), jnp.float32, -s, s)
        Wk = jax.random.uniform(ks[2], (DM, DM), jnp.float32, -s, s)
        Wv = jax.random.uniform(ks[3], (DM, DM), jnp.float32, -s, s)
        Wo = jax.random.uniform(ks[4], (DM, DM), jnp.float32, -s, s)
        return {'x': x, 'Wq': Wq, 'Wk': Wk, 'Wv': Wv, 'Wo': Wo}
    _L0_attn_all = _L0_attn_setup()
    _L0_attn_in = {k: v for k, v in _L0_attn_all.items() if k in ('Wq', 'Wk', 'Wv', 'Wo')}
    del _L0_attn_all

    def _L0_xattn_setup():
        import jax, jax.numpy as jnp
        import numpy as np
        D_MODEL = 128
        H = 16
        D_K = D_MODEL // H
        key = jax.random.key(seed)
        ks = jax.random.split(key, 12)
        B, S = (4, 256)
        scale = 1.0 / np.sqrt(D_MODEL)
        inp = {'q': jax.random.normal(ks[0], (B, S, D_MODEL), jnp.float32), 'k': jax.random.normal(ks[1], (B, S, D_MODEL), jnp.float32), 'v': jax.random.normal(ks[2], (B, S, D_MODEL), jnp.float32), 'mask': jnp.ones((B, 1, S, S), dtype=bool), 'Wq': jax.random.normal(ks[3], (D_MODEL, D_MODEL), jnp.float32) * scale, 'bq': jax.random.normal(ks[4], (D_MODEL,), jnp.float32) * 0.01, 'Wk': jax.random.normal(ks[5], (D_MODEL, D_MODEL), jnp.float32) * scale, 'bk': jax.random.normal(ks[6], (D_MODEL,), jnp.float32) * 0.01, 'Wv': jax.random.normal(ks[7], (D_MODEL, D_MODEL), jnp.float32) * scale, 'bv': jax.random.normal(ks[8], (D_MODEL,), jnp.float32) * 0.01, 'Wo': jax.random.normal(ks[9], (D_MODEL, D_MODEL), jnp.float32) * scale, 'bo': jax.random.normal(ks[10], (D_MODEL,), jnp.float32) * 0.01}
        return inp
    _L0_xattn_all = _L0_xattn_setup()
    _L0_xattn_in = {k: v for k, v in _L0_xattn_all.items() if k in ('Wq', 'bq', 'Wk', 'bk', 'Wv', 'bv', 'Wo', 'bo')}
    del _L0_xattn_all

    def _L0_ffn_setup():
        import jax, jax.numpy as jnp
        import numpy as np
        B, L, D = (4, 64, 128)
        E, TOP_K = (16, 4)
        F = 4 * D
        key = jax.random.key(seed)
        ks = jax.random.split(key, 6)
        scale = 0.02
        return {'x': jax.random.normal(ks[0], (B, L, D), jnp.float32), 'keys': jax.random.normal(ks[1], (E, D), jnp.float32), 'w1': jax.random.normal(ks[2], (E, F, D), jnp.float32) * scale, 'b1': jnp.zeros((E, F), jnp.float32), 'w2': jax.random.normal(ks[3], (E, D, F), jnp.float32) * scale, 'b2': jnp.zeros((E, D), jnp.float32), 'rw': jax.random.normal(ks[4], (E, D), jnp.float32) * scale, 'rb': jnp.zeros((E,), jnp.float32)}
    _L0_ffn_all = _L0_ffn_setup()
    _L0_ffn_in = {k: v for k, v in _L0_ffn_all.items() if k in ('keys', 'w1', 'b1', 'w2', 'b2', 'rw', 'rb')}
    del _L0_ffn_all
    return {'x': x, 'ctx_1024': ctx_1024, 'mask_Bx1xSxS2_bf1': mask_Bx1xSxS2_bf1, 'L0_attn_Wq': _L0_attn_in['Wq'], 'L0_attn_Wk': _L0_attn_in['Wk'], 'L0_attn_Wv': _L0_attn_in['Wv'], 'L0_attn_Wo': _L0_attn_in['Wo'], 'L0_xattn_Wq': _L0_xattn_in['Wq'], 'L0_xattn_bq': _L0_xattn_in['bq'], 'L0_xattn_Wk': _L0_xattn_in['Wk'], 'L0_xattn_bk': _L0_xattn_in['bk'], 'L0_xattn_Wv': _L0_xattn_in['Wv'], 'L0_xattn_bv': _L0_xattn_in['bv'], 'L0_xattn_Wo': _L0_xattn_in['Wo'], 'L0_xattn_bo': _L0_xattn_in['bo'], 'L0_ffn_keys': _L0_ffn_in['keys'], 'L0_ffn_w1': _L0_ffn_in['w1'], 'L0_ffn_b1': _L0_ffn_in['b1'], 'L0_ffn_w2': _L0_ffn_in['w2'], 'L0_ffn_b2': _L0_ffn_in['b2'], 'L0_ffn_rw': _L0_ffn_in['rw'], 'L0_ffn_rb': _L0_ffn_in['rb']}

def reference(x, ctx_1024, mask_Bx1xSxS2_bf1, L0_attn_Wq, L0_attn_Wk, L0_attn_Wv, L0_attn_Wo, L0_xattn_Wq, L0_xattn_bq, L0_xattn_Wk, L0_xattn_bk, L0_xattn_Wv, L0_xattn_bv, L0_xattn_Wo, L0_xattn_bo, L0_ffn_keys, L0_ffn_w1, L0_ffn_b1, L0_ffn_w2, L0_ffn_b2, L0_ffn_rw, L0_ffn_rb):
    import jax
    import jax.numpy as jnp

    def _L0_attn_ref(x, Wq, Wk, Wv, Wo):
        import jax, jax.numpy as jnp
        import numpy as np
        B, N, DM, H = (1, 256, 128, 16)
        CURV = 1.0
        b, n, d = x.shape
        hd = d // H

        def split_heads(t):
            return t.reshape(b, n, H, hd).transpose(0, 2, 1, 3)
        q = split_heads(x @ Wq.T)
        k = split_heads(x @ Wk.T)
        v = split_heads(x @ Wv.T)
        q_norm_sq = jnp.sum(q * q, axis=-1, keepdims=True)
        k_norm_sq = jnp.sum(k * k, axis=-1)[:, :, None, :]
        qk = jnp.einsum('bhnd,bhmd->bhnm', q, k)
        diff_sq = jnp.maximum(q_norm_sq + k_norm_sq - 2.0 * qk, 0.0)
        denom = jnp.maximum((1.0 - CURV * q_norm_sq) * (1.0 - CURV * k_norm_sq), 1e-06)
        cosh_arg = jnp.maximum(1.0 + 2.0 * CURV * diff_sq / denom, 1.0)
        distance = jnp.where(cosh_arg > 1.0, jnp.arccosh(jnp.maximum(cosh_arg, 1.0 + 1e-12)), 0.0)
        attn = jax.nn.softmax(-distance, axis=-1)
        out = jnp.einsum('bhnm,bhmd->bhnd', attn, v)
        out = out.transpose(0, 2, 1, 3).reshape(b, n, d)
        return out @ Wo.T

    def _L0_xattn_ref(q, k, v, mask, Wq, bq, Wk, bk, Wv, bv, Wo, bo):
        import jax, jax.numpy as jnp
        import numpy as np
        D_MODEL = 128
        H = 16
        D_K = D_MODEL // H
        B, S, _ = q.shape
        qh = (q @ Wq.T + bq).reshape(B, S, H, D_K).transpose(0, 2, 1, 3)
        kh = (k @ Wk.T + bk).reshape(B, -1, H, D_K).transpose(0, 2, 1, 3)
        vh = (v @ Wv.T + bv).reshape(B, -1, H, D_K).transpose(0, 2, 1, 3)
        scores = jnp.einsum('bhqd,bhkd->bhqk', qh, kh) / np.sqrt(D_K)
        scores = jnp.where(mask, scores, -1000000000.0)
        weights = jax.nn.softmax(scores, axis=-1)
        out = jnp.einsum('bhqk,bhkd->bhqd', weights, vh)
        out = out.transpose(0, 2, 1, 3).reshape(B, S, D_MODEL)
        return out @ Wo.T + bo

    def _L0_ffn_ref(x, keys, w1, b1, w2, b2, rw, rb):
        import jax, jax.numpy as jnp
        import numpy as np
        B, L, D = (4, 64, 128)
        E, TOP_K = (16, 4)
        F = 4 * D
        diff = x[:, :, None, :] - keys
        dist2 = jnp.sum(diff * diff, axis=-1)
        logits = -dist2 + jnp.einsum('bld,ed->ble', x, rw) + rb
        topv, topi = jax.lax.top_k(logits, TOP_K)
        w = jax.nn.softmax(topv, axis=-1)
        hidden = jax.nn.gelu(jnp.einsum('bld,efd->blef', x, w1) + b1, approximate=False)
        exp_out = jnp.einsum('blef,edf->bled', hidden, w2) + b2
        sel = jnp.take_along_axis(exp_out, topi[..., None], axis=2)
        fused = jnp.sum(w[..., None] * sel, axis=2)
        return fused
    x = x + _L0_attn_ref(_layernorm(x, axis=-1), L0_attn_Wq, L0_attn_Wk, L0_attn_Wv, L0_attn_Wo)
    x = x + _L0_xattn_ref(_layernorm(x, axis=-1), ctx_1024, ctx_1024, mask_Bx1xSxS2_bf1, L0_xattn_Wq, L0_xattn_bq, L0_xattn_Wk, L0_xattn_bk, L0_xattn_Wv, L0_xattn_bv, L0_xattn_Wo, L0_xattn_bo)
    x = x + _L0_ffn_ref(_layernorm(x, axis=-1), L0_ffn_keys, L0_ffn_w1, L0_ffn_b1, L0_ffn_w2, L0_ffn_b2, L0_ffn_rw, L0_ffn_rb)
    return x

_drawn_inputs = setup_inputs


def setup_inputs(seed=0):
    import zlib

    import numpy as np

    out = dict(_drawn_inputs(seed))
    spreads = {'L0_ffn_b1': (0.0, 0.381), 'L0_ffn_b2': (0.0, 0.1), 'L0_ffn_rb': (0.0, 2.0)}
    factors = {'L0_xattn_bq': 23.878,
     'L0_xattn_bk': 64.0,
     'L0_xattn_bv': 5.473,
     'L0_xattn_bo': 5.457,
     'L0_ffn_rw': 8.0}
    for name, (base, spread) in spreads.items():
        noise = np.random.default_rng([zlib.crc32(name.encode()), seed]).standard_normal(out[name].shape)
        drawn = base * np.exp(spread * noise) if base else spread * noise
        out[name] = jnp.asarray(drawn.astype(out[name].dtype))
    for name, factor in factors.items():
        out[name] = (out[name] * factor).astype(out[name].dtype)
    return out
```

```python
from contextlib import ExitStack

import numpy as np
import concourse.bass as bass
from concourse import mybir

F32 = mybir.dt.float32
F32R = mybir.dt.float32r
BF16 = mybir.dt.bfloat16
U8 = mybir.dt.uint8
ALU = mybir.AluOpType
ACT = mybir.ActivationFunctionType
AX = mybir.AxisListType.X

P = 128
B, N, D = 8, 256, 128
M = 512
H, HD = 16, 8
TN, TM = N // P, M // P
NT = B * TN
R, G = 4, H // 4
GP = G // 2
E, TOPK, FF = 16, 4, 512
FC = FF // P
EPS = 1e-5
BIG = float(2.0 ** 100)
DENOM_MIN = 1e-6
SCALE = 1.0 / float(np.sqrt(HD))

WEIGHTS = ("wqT_s", "wkT_s", "wvT_s", "woT_s")
WEIGHTS_X = ("wqT_x", "wkT_x", "wvT_x", "woT_x", "bq_x", "bk_x", "bv_x", "bo_x")


def wait(eng, sem, value, apart=None):
    if not isinstance(value, int) or value > 0:
        eng.wait_ge(sem, value)
        if apart is not None:
            eng.sem_inc(apart, 1)


class Chain:

    def __init__(self, eng, sem, apart=None):
        self.apart = apart
        self.eng, self.sem, self.base, self.n, self.loop0, self.per = eng, sem, 0, 0, None, None

    def step(self, ins):
        ins.then_inc(self.sem, 1)
        self.n += 1

    def sync(self):
        wait(self.eng, self.sem, self.base + self.n, None if isinstance(self.base, int) else self.apart)

    def link(self, ins):
        self.step(ins)
        self.sync()

    def enter(self, b, per):
        if self.loop0 is None:
            self.loop0 = self.base + self.n
        self.base, self.n, self.per = b * per + self.loop0, 0, per

    def leave(self, b):
        assert self.n == self.per, (self.n, self.per)
        self.base, self.n = (b + 1) * self.per + self.loop0, 0

    def end(self, batches):
        self.base, self.n, self.loop0 = self.loop0 + batches * self.per, 0, None


def decoder_block(nc, a, out):
    with ExitStack() as ctx:
        def sb(name, shape, dt=F32):
            return ctx.enter_context(nc.sbuf_tensor(name, shape, dt))

        def sem(name):
            return ctx.enter_context(nc.semaphore(name))

        X = sb("X", [P, NT, D])
        ident = sb("ident", [P, P])
        ident_bf = sb("ident_bf", [P, P], BF16)
        sel = sb("sel", [P, R * 9])
        bn_st = sb("bn_st", [P, NT, 6])
        bn_mv = sb("bn_mv", [P, NT, 2])
        ln_sd = sb("ln_sd", [P, NT])
        ln_rs = sb("ln_rs", [P, NT])
        eps_c = sb("eps_c", [P, 1])
        rec = sb("rec", [P, TN, H])
        On = sb("On", [P, TN, D])
        OnT = sb("OnT", [P, N])
        OT = sb("OT", [P, 2, N])
        HIq = sb("HIq", [P, NT, D], F32R)
        LOq = sb("LOq", [P, NT, D])

        def arena(phase):
            top = ctx.enter_context(ExitStack())
            return top, lambda name, shape, dt=F32: top.enter_context(
                nc.sbuf_tensor(f"{phase}_{name}", [P] + list(shape), dt))

        def ps(name, shape):
            return ctx.enter_context(nc.psum_tensor(name, [P] + shape, F32))

        slot = [ps(f"slot{i}", [2, 512]) for i in range(2)]
        tps = [ps(f"tps{i}", [512]) for i in range(2)]
        ops = ps("ops", [2, N])
        bps = ps("bps", [512])

        apart_g, apart_a, apart_s = sem("apart_g"), sem("apart_a"), sem("apart_s")
        x_in, w_in, cst = sem("x_in"), sem("w_in"), sem("cst")
        dve_step, act_step, pool_step = sem("dve_step"), sem("act_step"), sem("pool_step")
        ln_var, ln_dev, xn_rdy = sem("ln_var"), sem("ln_dev"), sem("xn_rdy")
        xt_full, xt_rdy = sem("xt_full"), sem("xt_rdy")
        qkv_full, qkv_used = sem("qkv_full"), sem("qkv_used")
        sq_rdy, s_prep, s_const = sem("sq_rdy"), sem("s_prep"), sem("s_const")
        s_feat, s_tfull, s_tused, s_vf = sem("s_feat"), sem("s_tfull"), sem("s_tused"), sem("s_vf")
        u_full, u_used = sem("u_full"), sem("u_used")
        g_rdy, y_rdy, z_rdy = sem("g_rdy"), sem("y_rdy"), sem("z_rdy")
        root_rdy, f_rdy, w_rdy = sem("root_rdy"), sem("f_rdy"), sem("w_rdy")
        ln_rdy = sem("ln_rdy")
        o_full, o_rdy = sem("o_full"), sem("o_rdy")
        b_full, b_used, s_done = sem("b_full"), sem("b_used"), sem("s_done")

        def ln_vector(dve, ch, XN, k):
            for t in range(NT):
                ch.step(dve.bn_stats(bn_st[:, t, :], X[:, t, :]))
            ch.sync()
            for t in range(NT):
                i = dve.bn_aggr(bn_mv[:, t, :], bn_st[:, t, :])
                if t < NT - 1:
                    ch.step(i)
            i.then_inc(ln_var, 1)
            ch.sync()
            dve.wait_ge(ln_dev, k + 1)
            ch.link(dve.reciprocal(ln_rs[:, :], ln_sd[:, :]))
            for t in range(NT):
                dve.tensor_scalar(XN[:, t, :], X[:, t, :], bn_mv[:, t, 0:1], ln_rs[:, t:t + 1],
                                  ALU.subtract, ALU.mult).then_inc(xn_rdy, 1)

        def ln_scalar(act, k):
            act.wait_ge(ln_var, k + 1)
            act.activation(ln_sd[:, :], bn_mv[:, :, 1], ACT.Sqrt, bias=eps_c[:, 0:1]).then_inc(ln_dev, 1)

        def ln_tensor(pe, XN, k):
            for t in range(NT):
                pe.wait_ge(xn_rdy, k * NT + t + 1)
                i = pe.transpose(slot[t // 8][:, t // 4 % 2, t % 4 * P:(t % 4 + 1) * P], XN[:, t, :], ident[:, :])
                if t % 4 == 3:
                    i.then_inc(xt_full, 1)

        def ln_copy(act, xnT, k):
            for q in range(4):
                act.wait_ge(xt_full, 4 * k + q + 1)
                act.copy(xnT[:, 512 * q:512 * q + 512], slot[q // 2][:, q % 2, :]).then_inc(xt_rdy, 1)

        topS, sS = arena("S")
        Y = sS("Y", [2, H, 2 * N])
        prepS = Y[:, :, :, :].rearrange("p a h n -> p (a h n)")
        at = [0]

        def over_Y(shape, names, **sizes):
            n = int(np.prod(shape))
            at[0] += n
            v = prepS[:, at[0] - n:at[0]]
            return v.rearrange(f"p ({names}) -> p {names}", **sizes) if sizes else v

        XN = over_Y([NT, D], "t d", t=NT)
        xnT = over_Y([NT * P], "")
        QKV = over_Y([NT, 3 * D], "t d", t=NT)
        SQ = over_Y([NT, 2 * D], "t d", t=NT)
        NRM = over_Y([NT, 2 * H], "t h", t=NT)
        A0 = over_Y([NT, 2 * H], "t h", t=NT)
        A1 = over_Y([NT, 2 * H], "t h", t=NT)
        A2 = over_Y([NT, 2 * H], "t h", t=NT)
        Zr = sS("Zr", [4, 2 * N])
        gb = sS("gb", [2, 2 * N])
        VS = sS("VS", [NT, D])
        HIk, LOk = sS("HIk", [NT, D], F32R), sS("LOk", [NT, D])
        NH, NL = sS("NH", [NT, 2 * H], F32R), sS("NL", [NT, 2 * H])
        QG, KG = sS("QG", [NT, H, 8]), sS("KG", [NT, H, 8])
        UQ, UK = sS("UQ", [TN, H, 32]), sS("UK", [TN, H, 32])
        GQ, GK = sS("GQ", [TN, H, 8]), sS("GK", [TN, 4, H, 8])
        UQT, UKT = sS("UQT", [2, G, N], F32R), sS("UKT", [2, G, N], F32R)
        GQT, GKT = sS("GQT", [2, N], F32R), sS("GKT", [2, 4, N], F32R)
        VF = sS("VF", [2, TN, H, 32])
        wqkv = sS("wqkv", [3 * D])
        wo_s = sS("wo_s", [D])
        STI = 7

        topS.close()

        topX, sX = arena("X")
        XNx = sX("XN", [NT, D])
        xnTx = sX("xnT", [NT * P])
        QX = sX("QX", [NT, D])
        wq_x, wkv_x, wo_x = sX("wq", [D]), sX("wkv", [2 * D]), sX("wo", [D])
        bq_x, bkv_x, bo_x = sX("bq", [D]), sX("bkv", [2 * D]), sX("bo", [D])
        CT = sX("CT", [2, TM, D])
        ctxT = sX("ctxT", [M])
        KV = sX("KV", [TM, D])
        QF, KF = sX("QF", [TN, H, 32]), sX("KF", [TM, H, 32])
        QFT, QFT2 = sX("QFT", [G, N], F32R), sX("QFT2", [G, N], F32R)
        KFT = sX("KFT", [2, G, M], F32R)
        VX = sX("VX", [2, TM, H, 32])
        M8, MT8 = sX("M8", [2, TN, M], U8), sX("MT8", [2, TM, N], U8)
        MB, MBT = sX("MB", [2, TN, M], BF16), sX("MBT", [2, TM, N], BF16)
        MX = sX("MX", [TN, H])
        W = sX("W", [4, TM, N])
        XTI, XTA = 11, 9
        topX.close()
        qx_full, qx_used, q_prep = sem("qx_full"), sem("qx_used"), sem("q_prep")
        wx_in, x_const = sem("wx_in"), sem("x_const")
        c_in, m_in = [sem("c_in0"), sem("c_in1")], [sem("m_in0"), sem("m_in1")]
        x_tfull, x_tact, x_tdve = sem("x_tfull"), sem("x_tact"), sem("x_tdve")
        k_rdy, mb_rdy, f_x, q2_rdy = sem("k_rdy"), sem("mb_rdy"), sem("f_x"), sem("q2_rdy")
        mx_full, mx_rdy, e_full, e_rdy = sem("mx_full"), sem("mx_rdy"), sem("e_full"), sem("e_rdy")
        pv_head, xo_rdy, xb_full, xb_used = sem("pv_head"), sem("xo_rdy"), sem("xb_full"), sem("xb_used")

        topF, sF = arena("F")
        XNf, xnTf = sF("XN", [NT, D]), sF("xnT", [NT * P])
        keysT, rwT, rb_b = sF("keysT", [E]), sF("rwT", [E]), sF("rb", [E])
        kw, ksq, lc = sF("kw", [E]), sF("ksq", [E]), sF("lc", [E])
        ones = sF("ones", [P])
        iota_i, iota_f = sF("iota_i", [E], mybir.dt.int32), sF("iota_f", [E])
        LG, EX, PICK, EQ = (sF(n, [NT, E]) for n in ("LG", "EX", "PICK", "EQ"))
        TOP, TOPI, TOPF = sF("TOP", [NT, 8]), sF("TOPI", [NT, 8], mybir.dt.uint32), sF("TOPF", [NT, 8])
        SM, RS = sF("SM", [NT]), sF("RS", [NT])
        WT, WTT = sF("WT", [NT, E]), sF("WTT", [NT * P])
        B1, b2_sb = sF("B1", [E, FC]), sF("b2", [D])
        W1, W2 = sF("W1", [2, FF]), sF("W2", [2, FC, D])
        HB = sF("HB", [2, FC, 512])
        TB = NT // 4
        topF.close()
        rw_in, rt_const, kw_rdy, ks_full, lg_full = sem("rw_in"), sem("rt_const"), sem("kw_rdy"), sem("ks_full"), sem("lg_full")
        ex_in, ex_rdy, wt_rdy = sem("ex_in"), sem("ex_rdy"), sem("wt_rdy")
        wtt_full, wtt_rdy, bo_full, bo_used = sem("wtt_full"), sem("wtt_rdy"), sem("bo_full"), sem("bo_used")
        ew_in = [sem("ew_in0"), sem("ew_in1")]
        h_full, h_rdy, y_full, y_used = sem("h_full"), sem("h_rdy"), sem("y_full"), sem("y_used")
        out_done = sem("out_done")

        block = ctx.enter_context(nc.Block())

        @block.sync
        def _(sp):
            x_t = a["x"].rearrange("b (t p) d -> p (b t) d", p=P)
            for q in range(4):
                sp.dma_start(X[:, 4 * q:4 * q + 4, :], x_t[:, 4 * q:4 * q + 4, :]).then_inc(x_in, 16)
            for j, n in enumerate(WEIGHTS[:3]):
                sp.dma_start(wqkv[:, j * D:(j + 1) * D], a[n]).then_inc(w_in, 16)
            sp.dma_start(wo_s[:, :], a["woT_s"]).then_inc(w_in, 16)
            sp.wait_ge(b_used, 3 * B + 1)
            sp.dma_start(wq_x[:, :], a["wqT_x"]).then_inc(wx_in, 16)
            sp.dma_start(wkv_x[:, 0:D], a["wkT_x"]).then_inc(wx_in, 16)
            sp.dma_start(wkv_x[:, D:2 * D], a["wvT_x"]).then_inc(wx_in, 16)
            sp.dma_start(wo_x[:, :], a["woT_x"]).then_inc(wx_in, 16)
            for dst, n in ((bq_x[:, :], "bq_x"), (bkv_x[:, 0:D], "bk_x"), (bkv_x[:, D:2 * D], "bv_x"),
                           (bo_x[:, :], "bo_x")):
                sp.dma_start(dst, a[n].partition_broadcast(P)).then_inc(wx_in, 16)
            ctx_t = a["ctx"].rearrange("b (t p) d -> b p t d", p=P)
            m_t = a["mask"].rearrange("b (t p) m -> b p t m", p=P)
            mT_t = a["maskT"].rearrange("b (t p) q -> b p t q", p=P)

            def load(b, p):
                wait(sp, x_tfull, (b - 2) * XTI + 1, apart_s)
                sp.dma_start(CT[:, p], ctx_t[b]).then_inc(c_in[p], 16)
                wait(sp, mb_rdy, (b - 1) * 2, apart_s)
                sp.dma_start(M8[:, p], m_t[b]).then_inc(m_in[p], 16)
                sp.dma_start(MT8[:, p], mT_t[b]).then_inc(m_in[p], 16)

            for b in range(2):
                load(b, b)
            with sp.Fori(1, B // 2) as i:
                for p in range(2):
                    load(i * 2 + p, p)
            sp.wait_ge(xb_used, 3 * B)
            for dst, src in ((keysT[:, :], a["keysT"]), (rwT[:, :], a["rwT"]), (rb_b[:, :], a["rb"].partition_broadcast(P)),
                             (B1[:], a["b1"]), (b2_sb[0:E, :], a["b2"])):
                sp.dma_start(dst, src).then_inc(rw_in, 16)
            w2_t = a["w2T"].rearrange("e (c p) d -> e p c d", p=P)

            def load_expert(e, p):
                wait(sp, y_full, (e - 1) * TB, apart_s)
                sp.dma_start(W1[:, p], a["w1T"][e]).then_inc(ew_in[p], 16)
                sp.dma_start(W2[:, p], w2_t[e]).then_inc(ew_in[p], 16)

            for e in range(2):
                load_expert(e, e)
            with sp.Fori(1, E // 2) as i:
                for p in range(2):
                    load_expert(i * 2 + p, p)
            o_t = out.rearrange("b (t p) d -> p (b t) d", p=P)
            sp.wait_ge(y_used, E * NT)
            sp.dma_start(o_t, X[:, :, :]).then_inc(out_done, 16)
            sp.wait_ge(out_done, 16)

        def batches(eng, front, body, back):
            front(0, 0)
            body(0, 0, True, False)
            with eng.Fori(0, (B - 2) // 2) as i:
                for k in range(2):
                    body(i * 2 + (k + 1), (k + 1) % 2, True, True)
            body(B - 1, (B - 1) % 2, False, True)
            back(B - 1, (B - 1) % 2)

        @block.gpsimd
        def _(g):
            ch = Chain(g, pool_step, apart_g)
            ch.step(g.memset(eps_c[:, :], EPS))
            ch.link(g.memset(ident[:, :], 0.0))
            ch.link(g.affine_select(out=ident[:, :], in_=ident[:, :], compare_op=ALU.not_equal, fill=1.0,
                                    base=0, pattern=[[-1, P]], channel_multiplier=1))
            ch.step(g.tensor_copy(ident_bf[:, :], ident[:, :]))
            for r in range(R):
                ch.step(g.tensor_copy(sel[:, 9 * r:9 * r + 9], ident[:, 32 * r:32 * r + 9]))
            for t in (UQ, UK, GQ, GK, VF):
                ch.step(g.memset(t[:], 0.0))
            ch.sync()
            ch.step(g.memset(UQ[:, :, :, 26:28], 1.0))
            ch.step(g.memset(UK[:, :, :, 24:26], 1.0))
            for p in range(2):
                ch.step(g.memset(VF[:, p, :, :, 8:9], 1.0))
            ch.sync()
            g.sem_inc(cst, 1)

            def per_head(x, bt, tt):
                return x[:, bt, :][:, tt].rearrange("p (h d) -> p h d", d=HD)

            HQ, HK, NHf = HIq[:].bitcast(F32), HIk[:].bitcast(F32), NH[:].bitcast(F32)

            def front(b, p):
                ch.enter(b, 26)
                bt = bass.ts(b, TN)
                wait(g, s_tfull, b * STI, apart_g)
                for tt in range(TN):
                    for dst, src in ((UQ[:, tt, :, 0:8], per_head(HQ, bt, tt)),
                                     (UQ[:, tt, :, 8:16], per_head(HQ, bt, tt)),
                                     (UQ[:, tt, :, 16:24], per_head(LOq, bt, tt)),
                                     (UK[:, tt, :, 0:8], per_head(HK, bt, tt)),
                                     (UK[:, tt, :, 8:16], per_head(LOk, bt, tt)),
                                     (UK[:, tt, :, 16:24], per_head(HK, bt, tt)),
                                     (GQ[:, tt], QG[:, bt][:, tt])):
                        ch.step(g.tensor_copy(dst, src))
                    for v in range(4):
                        ch.step(g.tensor_copy(GK[:, tt, v, v::4, :], KG[:, bt][:, tt, v::4, :]))
                for dst, src in ((UQ[:, :, :, 24], NHf[:, bt, 0:H]), (UQ[:, :, :, 25], NL[:, bt, 0:H]),
                                 (UK[:, :, :, 26], NHf[:, bt, H:2 * H]), (UK[:, :, :, 27], NL[:, bt, H:2 * H])):
                    ch.step(g.tensor_copy(dst, src))
                ch.sync()
                g.sem_inc(s_feat, 1)
                ch.leave(b)
                wait(g, o_full, (b - 1) * GP, apart_g)
                for tt in range(TN):
                    g.tensor_copy(VF[:, p, tt, :, 0:8], per_head(VS, bt, tt)).then_inc(s_vf, 1)

            def body(b, p, with_front, with_back):
                for h in range(H):
                    if h == 2 and with_front:
                        front(b + 1, 1 - p)
                    g.wait_ge(root_rdy, b * H + h + 1)
                    g.tensor_tensor(Y[:, p, h], Y[:, p, h], Zr[:, h % 4], ALU.add).then_inc(f_rdy, 1)

            g.wait_ge(s_prep, 1)
            batches(g, front, body, lambda b, p: None)
            ch.end(B)

            g.wait_ge(b_used, 3 * B + 1)
            for t in (QF, KF, VX):
                ch.step(g.memset(t[:], 0.0))
            ch.sync()
            ch.step(g.memset(KF[:, :, :, 24:26], 1.0))
            for p in range(2):
                ch.step(g.memset(VX[:, p, :, :, 8:9], 1.0))
            ch.sync()
            g.sem_inc(x_const, 1)

            def heads(x):
                return x.rearrange("p t (h d) -> p t h d", d=HD)

            def front(b, p):
                ch.enter(b, 8)
                bt = bass.ts(b, TN)
                wait(g, x_tfull, b * XTI, apart_g)
                for tt in range(TN):
                    for dst, src in ((QF[:, tt, :, 0:8], per_head(HQ, bt, tt)),
                                     (QF[:, tt, :, 8:16], per_head(HQ, bt, tt)),
                                     (QF[:, tt, :, 16:24], per_head(LOq, bt, tt))):
                        ch.step(g.tensor_copy(dst, src))
                wait(g, k_rdy, (b + 1) * 2, apart_g)
                ch.link(g.tensor_copy(KF[:].bitcast(F32R)[:, :, :, 0:8], heads(KV[:, :, :])))
                ch.step(g.tensor_copy(KF[:, :, :, 16:24], KF[:, :, :, 0:8]))
                g.tensor_tensor(KF[:, :, :, 8:16], heads(KV[:, :, :]), KF[:, :, :, 0:8], ALU.subtract).then_inc(f_x, 1)
                ch.leave(b)
                ch.sync()
                g.wait_ge(f_x, b * 2 + 1)
                g.sem_inc(f_x, 1)

            g.wait_ge(q_prep, 1)
            front(0, 0)
            with g.Fori(0, (B - 2) // 2) as i:
                for k in range(2):
                    front(i * 2 + (k + 1), (k + 1) % 2)
            front(B - 1, (B - 1) % 2)
            ch.end(B)

            g.wait_ge(xb_used, 3 * B)
            ch.step(g.memset(ones[:, :], 1.0))
            ch.link(g.iota(iota_i[:, :], pattern=[[1, E]], base=0, channel_multiplier=0))
            ch.link(g.tensor_copy(iota_f[:, :], iota_i[:, :]))
            g.sem_inc(rt_const, 1)

        @block.scalar
        def _(act):
            act.wait_ge(cst, 1)
            ln_scalar(act, 0)
            ln_copy(act, xnT, 0)
            for t in range(NT):
                act.wait_ge(qkv_full, t + 1)
                act.copy(QKV[:, t, :], tps[t % 2][:, 0:3 * D]).then_inc(qkv_used, 1)
            act.wait_ge(qkv_used, NT)
            act.activation(SQ[:, :, :], QKV[:, :, 0:2 * D], ACT.Square).then_inc(sq_rdy, 1)

            def front_copy(b, p, n):
                act.wait_ge(s_tfull, b * STI + n + 1)
                if n == 0:
                    wait(act, u_full, (b - 1) * H)
                src = tps[n % 2]
                if n < 4:
                    dst = (UQT, UKT)[n // 2][:, p, n % 2 * 2:n % 2 * 2 + 2, :]
                elif n == 4:
                    dst = GQT[:, p, :]
                    src = src[:, 0:N]
                else:
                    dst = GKT[:, p, (n - 5) * 2:(n - 5) * 2 + 2, :]
                act.copy(dst, src if n == 4 else src[:, :].rearrange("p (g n) -> p g n", g=2)).then_inc(s_tused, 1)

            def front(b, p):
                for n in range(STI):
                    front_copy(b, p, n)

            def body(b, p, with_front, with_back):
                for h in range(H):
                    act.wait_ge(z_rdy, b * H + h + 1)
                    act.activation(Zr[:, h % 4], Zr[:, h % 4], ACT.Sqrt).then_inc(root_rdy, 1)
                    if with_back and h in (2, 6):
                        out_copy(b - 1, h // 4)
                    if with_front and h >= H - STI:
                        front_copy(b + 1, 1 - p, h - (H - STI))
                for g in range(G):
                    v = Y[:, p, R * g:R * g + R, :]
                    act.wait_ge(f_rdy, b * H + R * g + R)
                    act.activation(v, v, ACT.Ln, bias=1.0).then_inc(ln_rdy, 1)
                    act.wait_ge(ln_rdy, b * G + g + 1)
                    act.activation(v, v, ACT.Exp, scale=-1.0).then_inc(w_rdy, 1)

            def out_copy(b, q):
                act.wait_ge(o_full, b * GP + q + 1)
                if q:
                    act.wait_ge(b_full, b * 4 + 1)
                act.copy(OT[:, :, :], ops[:, :, :]).then_inc(o_rdy, 1)

            def back(b, p):
                for q in range(GP):
                    out_copy(b, q)

            batches(act, front, body, back)

            ln_scalar(act, 1)
            ln_copy(act, xnTx, 1)

            def act_item(b, p, n):
                act.wait_ge(x_tfull, b * XTI + (n + 1 if n == 0 else n + 3))
                dst, src = ((ctxT[:, :], tps[0][:, :]),
                            (KFT[:, p, 0, :], tps[1][:, :]), (KFT[:, p, 1, :], tps[0][:, :]),
                            (KFT[:, p, 2, :], tps[1][:, :]), (KFT[:, p, 3, :], tps[0][:, :]),
                            (QFT[:, 0:2, :], tps[1][:, :]), (QFT[:, 2:4, :], tps[0][:, :]),
                            (QFT2[:, 0:2, :], tps[1][:, :]), (QFT2[:, 2:4, :], tps[0][:, :]))[n]
                if n >= 5:
                    src = src.rearrange("p (g n) -> p g n", g=2)
                act.copy(dst, src).then_inc(x_tact, 1)

            def front(b, p):
                for n in range(7):
                    act_item(b, p, n)

            def body(b, p, with_front):
                for h in range(H):
                    act.wait_ge(e_full, b * H + h + 1)
                    wait(act, pv_head, b * H + h - 3)
                    act.activation(W[:, h % 4, :, :].rearrange("p (c t) n -> p c (t n)", c=2), slot[h % 2][:, :, :],
                                   ACT.Exp, scale=SCALE).then_inc(e_rdy, 1)
                    if h == 8:
                        out_copy(b, 0)
                    if with_front and h in (2, 8, 10, 12, 14):
                        act_item(b + 1, 1 - p, max(h // 2 - 3, 0))
                out_copy(b, 1)
                if with_front:
                    for n in (5, 6, 7, 8):
                        act_item(b + 1, 1 - p, n)

            def out_copy(b, q):
                act.wait_ge(pv_head, b * H + 8 * (q + 1))
                wait(act, xb_full, b * 4 + q)
                act.copy(OT[:, :, :], ops[:, :, :]).then_inc(xo_rdy, 1)

            front(0, 0)
            for n in (7, 8):
                act_item(0, 0, n)
            body(0, 0, True)
            with act.Fori(0, (B - 2) // 2) as i:
                for k in range(2):
                    body(i * 2 + (k + 1), (k + 1) % 2, True)
            body(B - 1, (B - 1) % 2, False)

            ln_scalar(act, 2)
            ln_copy(act, xnTf, 2)
            act.wait_ge(ex_in, 1)
            act.activation(EX[:], EX[:], ACT.Exp).then_inc(ex_rdy, 1)
            for q in range(4):
                act.wait_ge(wtt_full, q + 1)
                act.copy(WTT[0:E, 512 * q:512 * q + 512], slot[q // 2][0:E, q % 2, :]).then_inc(wtt_rdy, 1)

            def gelus(e, tb):
                k = e * TB + tb
                for c in range(FC):
                    if c == 0:
                        wait(act, y_full, k - 1)
                    wait(act, h_full, k * FC + c + 1, apart_a)
                    act.activation(HB[:, tb % 2, c, :], slot[c // 2][:, c % 2, :], ACT.Gelu,
                                   bias=B1[:, bass.ts(e, 1), c]).then_inc(h_rdy, 1)

            for tb in range(TB):
                gelus(0, tb)
            with act.Fori(1, E) as e:
                for tb in range(TB):
                    gelus(e, tb)

        @block.tensor
        def _(pe):
            pe.wait_ge(cst, 1)
            ln_tensor(pe, XN, 0)
            pe.wait_ge(w_in, 64)
            for t in range(NT):
                pe.wait_ge(xt_rdy, t // 4 + 1)
                if t >= 2:
                    pe.wait_ge(qkv_used, t - 1)
                pe.matmul(tps[t % 2][:, 0:3 * D], xnT[:, t * P:(t + 1) * P], wqkv[:, :],
                          start=True, stop=True).then_inc(qkv_full, 1)
            pe.wait_ge(qkv_used, NT)

            def front_item(b, p, n):
                if n == 0:
                    pe.wait_ge(s_feat, b + 1)
                wait(pe, s_tused, b * STI + n - 1)
                dst = tps[n % 2]
                if n < 4:
                    src = (UQ, UK)[n // 2]
                    parts = [(j, tt, src[:, tt, R * (n % 2 * 2 + j):R * (n % 2 * 2 + j + 1), :])
                             for j in range(2) for tt in range(TN)]
                elif n == 4:
                    parts = [(0, tt, GQ[:, tt]) for tt in range(TN)]
                else:
                    parts = [(j, tt, GK[:, tt, (n - 5) * 2 + j]) for j in range(2) for tt in range(TN)]
                for j, tt, src in parts:
                    ins = pe.transpose(dst[:, j * N + tt * P:j * N + (tt + 1) * P],
                                       src.rearrange("p h f -> p (h f)"), ident[:, :])
                ins.then_inc(s_tfull, 1)

            def front(b, p):
                for n in range(STI):
                    front_item(b, p, n)

            def scores(b, p, h):
                g, r = h // R, slice(32 * (h % R), 32 * (h % R) + 32)
                rg = slice(32 * (h // 4), 32 * (h // 4) + 32)
                if h == 0:
                    pe.wait_ge(s_tused, (b + 1) * STI)
                wait(pe, u_used, b * H + h - 1)
                for kt in range(TN):
                    pe.matmul(slot[h % 2][:, 0, kt * N:(kt + 1) * N], UKT[r, p, g, kt * P:(kt + 1) * P],
                              UQT[r, p, g, :], start=True, stop=True)
                for kt in range(TN):
                    ins = pe.matmul(slot[h % 2][:, 1, kt * N:(kt + 1) * N],
                                    GKT[rg, p, h % 4, kt * P:(kt + 1) * P], GQT[rg, p, :], start=True, stop=True)
                ins.then_inc(u_full, 1)

            def product(b, p, g):
                if g == 0:
                    pe.wait_ge(s_vf, (b + 1) * TN)
                pe.wait_ge(w_rdy, b * G + g + 1)
                if g == 2:
                    pe.wait_ge(o_rdy, b * GP + 1)
                for r in range(R):
                    h = R * g + r
                    for kt in range(TN):
                        ins = pe.matmul(ops[32 * r:32 * r + 32, g % 2, :], VF[:, p, kt, h, :],
                                        Y[:, p, h, kt * N:(kt + 1) * N], start=(kt == 0), stop=(kt == TN - 1))
                if g % 2:
                    ins.then_inc(o_full, 1)

            def turn(b, q):
                if q == 0:
                    pe.wait_ge(b_used, b * 3 + 1)
                pe.wait_ge(o_rdy, b * GP + q + 1)
                for g in (0, 1):
                    for tt in range(TN):
                        ins = pe.matmul(bps[:, tt * 144 + (2 * q + g) * 36:tt * 144 + (2 * q + g + 1) * 36],
                                        OT[:, g, tt * P:(tt + 1) * P], sel[:, :], start=True, stop=True)
                ins.then_inc(b_full, 1)

            def back_at(b, p, k):
                if k < G:
                    product(b, p, k)
                if k == 2:
                    turn(b, 0)
                if k == G:
                    turn(b, 1)
                if k == G + 1:
                    pe.wait_ge(b_used, b * 3 + 2)
                    for tt in range(TN):
                        ins = pe.transpose(bps[:, tt * P:(tt + 1) * P], On[:, tt, :], ident[:, :])
                    ins.then_inc(b_full, 1)
                if k == G + 2:
                    pe.wait_ge(b_used, b * 3 + 3)
                    for tt in range(TN):
                        ins = pe.matmul(bps[:, tt * P:(tt + 1) * P], OnT[:, tt * P:(tt + 1) * P], wo_s[:, :],
                                        start=True, stop=True)
                    ins.then_inc(b_full, 1)

            def body(b, p, with_front, with_back):
                for h in range(H):
                    scores(b, p, h)
                    if with_back and h % 2 == 0 and h // 2 < G + 3:
                        back_at(b - 1, 1 - p, h // 2)
                    if with_front and h >= H - STI:
                        front_item(b + 1, 1 - p, h - (H - STI))

            def back(b, p):
                for k in range(G + 3):
                    back_at(b, p, k)

            batches(pe, front, body, back)

            ln_tensor(pe, XNx, 1)
            pe.wait_ge(wx_in, 16 * 8)
            for q in range(4):
                pe.wait_ge(xt_rdy, 4 + q + 1)
                wait(pe, qx_used, q - 1)
                for t in range(4):
                    ins = pe.matmul(tps[q % 2][:, t * P:(t + 1) * P], xnTx[:, (4 * q + t) * P:(4 * q + t + 1) * P],
                                    wq_x[:, :], start=True, stop=True)
                ins.then_inc(qx_full, 1)
            pe.wait_ge(qx_used, 4)

            def item(b, p, n):
                prior = ((x_tact, b * 9), (x_tact, b * 9), (x_tact, b * 9 + 1), (x_tdve, b * 2 + 1),
                         (x_tdve, b * 2 + 2)) + tuple((x_tact, b * 9 + k) for k in range(2, 8))
                wait(pe, *prior[n])
                dst = tps[n % 2]
                if n == 0:
                    for p_ in range(2):
                        if p_ == p:
                            pe.wait_ge(c_in[p], in_loop_count(b, p))
                    for t in range(TM):
                        ins = pe.transpose(dst[:, t * P:(t + 1) * P], CT[:, p, t, :], ident[:, :])
                elif n < 3:
                    pe.wait_ge(x_tact, b * 9 + 1)
                    for j in range(2):
                        t = (n - 1) * 2 + j
                        ins = pe.matmul(dst[:, j * N:(j + 1) * N], ctxT[:, t * P:(t + 1) * P], wkv_x[:, :],
                                        start=True, stop=True)
                elif n < 7:
                    if n == 3:
                        pe.wait_ge(f_x, b * 2 + 2)
                    for t in range(TM):
                        ins = pe.transpose(dst[:, t * P:(t + 1) * P],
                                           KF[:, t, R * (n - 3):R * (n - 2), :].rearrange("p h f -> p (h f)"),
                                           ident[:, :])
                else:
                    if n == 9:
                        pe.wait_ge(q2_rdy, b + 1)
                    for j in range(2):
                        gg = (n - 7) % 2 * 2 + j
                        for t in range(TN):
                            ins = pe.transpose(dst[:, j * N + t * P:j * N + (t + 1) * P],
                                               QF[:, t, R * gg:R * gg + R, :].rearrange("p h f -> p (h f)"),
                                               ident[:, :])
                ins.then_inc(x_tfull, 1)

            def maxima(b, p, h):
                g, r = h // R, slice(32 * (h % R), 32 * (h % R) + 32)
                if h == 0:
                    pe.wait_ge(x_tact, b * 9 + 7)
                    pe.wait_ge(mb_rdy, (b + 1) * 2)
                if h < 2:
                    wait(pe, e_rdy, b * H)
                else:
                    pe.wait_ge(mx_rdy, b * H + h - 1)
                for t in range(TN):
                    pe.matmul(slot[h % 2][:, t, :], QFT[r, g, t * P:(t + 1) * P], KFT[r, p, g, :],
                              start=True, stop=False)
                for t in range(TN):
                    ins = pe.matmul(slot[h % 2][:, t, :], ident_bf[:, :], MB[:, p, t, :], start=False, stop=True)
                ins.then_inc(mx_full, 1)

            def scores(b, p, h):
                g, r = h // R, slice(32 * (h % R), 32 * (h % R) + 32)
                if h == 0:
                    pe.wait_ge(x_tact, b * 9 + 9)
                if h < 2:
                    pe.wait_ge(mx_rdy, (b + 1) * H)
                else:
                    pe.wait_ge(e_rdy, b * H + h - 1)
                for t in range(TM):
                    pe.matmul(slot[h % 2][:, t // 2, t % 2 * N:(t % 2 + 1) * N], KFT[r, p, g, t * P:(t + 1) * P],
                              QFT2[r, g, :], start=True, stop=False)
                    ins = pe.matmul(slot[h % 2][:, t // 2, t % 2 * N:(t % 2 + 1) * N], ident_bf[:, :], MBT[:, p, t, :],
                                    start=False, stop=True)
                ins.then_inc(e_full, 1)

            def product(b, p, h):
                pe.wait_ge(e_rdy, b * H + h + 1)
                if h % 8 == 0:
                    wait(pe, xo_rdy, b * GP + h // 8)
                r, half = slice(32 * (h % R), 32 * (h % R) + 32), h // R % 2
                for t in range(TM):
                    ins = pe.matmul(ops[r, half, :], VX[:, p, t, h, :], W[:, h % 4, t, :],
                                    start=(t == 0), stop=(t == TM - 1))
                ins.then_inc(pv_head, 1)

            def turn(b, q):
                if q == 0:
                    wait(pe, xb_used, b * 3)
                pe.wait_ge(xo_rdy, b * GP + q + 1)
                for g in (0, 1):
                    for tt in range(TN):
                        ins = pe.matmul(bps[:, tt * 144 + (2 * q + g) * 36:tt * 144 + (2 * q + g + 1) * 36],
                                        OT[:, g, tt * P:(tt + 1) * P], sel[:, :], start=True, stop=True)
                ins.then_inc(xb_full, 1)

            def body(b, p, with_front):
                for h in range(H):
                    scores(b, p, h)
                    if h:
                        product(b, p, h - 1)
                    if h == 11:
                        turn(b, 0)
                    if with_front and h % 2 == 0 and h > 0:
                        item(b + 1, 1 - p, h // 2 - 1)
                product(b, p, H - 1)
                if with_front:
                    for n in (7, 8):
                        item(b + 1, 1 - p, n)
                turn(b, 1)
                for h in range(H):
                    if with_front:
                        maxima(b + 1, 1 - p, h)
                    if h == 4:
                        pe.wait_ge(xb_used, b * 3 + 1)
                        for tt in range(TN):
                            ins = pe.transpose(bps[:, tt * P:(tt + 1) * P], On[:, tt, :], ident[:, :])
                        ins.then_inc(xb_full, 1)
                    if h == 8:
                        pe.wait_ge(xb_used, b * 3 + 2)
                        for tt in range(TN):
                            ins = pe.matmul(bps[:, tt * P:(tt + 1) * P], OnT[:, tt * P:(tt + 1) * P], wo_x[:, :],
                                            start=True, stop=True)
                        ins.then_inc(xb_full, 1)
                if with_front:
                    for n in (9, 10):
                        item(b + 1, 1 - p, n)

            def in_loop_count(b, p):
                if isinstance(b, int):
                    return 16 * (b // 2 + 1)
                return b * 8 + (16 if p == 0 else 8)

            for n in range(9):
                item(0, 0, n)
            for h in range(H):
                maxima(0, 0, h)
            for n in (9, 10):
                item(0, 0, n)
            body(0, 0, True)
            with pe.Fori(0, (B - 2) // 2) as i:
                for k in range(2):
                    body(i * 2 + (k + 1), (k + 1) % 2, True)
            body(B - 1, (B - 1) % 2, False)

            ln_tensor(pe, XNf, 2)
            pe.wait_ge(kw_rdy, 2)
            pe.wait_ge(rt_const, 1)
            pe.matmul(tps[0][:, 0:E], ones[:, :], ksq[:, :], start=True, stop=True).then_inc(ks_full, 1)
            for t in range(NT):
                pe.wait_ge(xt_rdy, 8 + t // 4 + 1)
                ins = pe.matmul(tps[1][:, t * E:(t + 1) * E], xnTf[:, t * P:(t + 1) * P], kw[:, :], start=True, stop=True)
            ins.then_inc(lg_full, 1)
            pe.wait_ge(wt_rdy, 1)
            for t in range(NT):
                ins = pe.transpose(slot[t // 8][0:E, t // 4 % 2, t % 4 * P:(t % 4 + 1) * P], WT[:, t, :], ident[:, :])
                if t % 4 == 3:
                    ins.then_inc(wtt_full, 1)
            pe.wait_ge(rw_in, 16 * 5)
            for q in range(4):
                pe.wait_ge(wtt_rdy, q + 1)
                wait(pe, bo_used, q - 1)
                for t in range(4 * q, 4 * q + 4):
                    ins = pe.matmul(tps[q % 2][:, t % 4 * P:(t % 4 + 1) * P], WTT[0:E, t * P:(t + 1) * P], b2_sb[0:E, :],
                                    start=True, stop=True)
                ins.then_inc(bo_full, 1)
            pe.wait_ge(wtt_rdy, 4)
            pe.wait_ge(bo_used, 4)

            def hidden(i, j):
                p, tb = j // TB, j % TB
                if tb == 0:
                    pe.wait_ge(ew_in[p], i * 32 + 32)
                for c in range(FC):
                    k = (i * 2 * TB + j) * FC
                    if isinstance(i, int) and i == 0 and j == 0:
                        pass
                    else:
                        pe.wait_ge(h_rdy, k + c - FC + 1)
                    pe.matmul(slot[c // 2][:, c % 2, :], W1[:, p, c * P:(c + 1) * P], xnTf[:, tb * 512:(tb + 1) * 512],
                              start=True, stop=True).then_inc(h_full, 1)

            def outputs(i, j):
                p, tb = j // TB, j % TB
                k = i * 2 * TB + j
                pe.wait_ge(h_rdy, (k + 1) * FC)
                if not (isinstance(i, int) and i == 0 and j < 2):
                    pe.wait_ge(y_used, (k - 1) * 4)
                for tt in range(4):
                    for c in range(FC):
                        ins = pe.matmul(tps[j % 2][:, tt * P:(tt + 1) * P], HB[:, j % 2, c, tt * P:(tt + 1) * P],
                                        W2[:, p, c, :], start=(c == 0), stop=(c == FC - 1))
                ins.then_inc(y_full, 1)

            hidden(0, 0)
            J = 2 * TB
            for j in range(J):
                hidden(0, j + 1) if j + 1 < J else hidden(1, 0)
                outputs(0, j)
            with pe.Fori(1, E // 2 - 1) as i:
                for j in range(J):
                    hidden(i, j + 1) if j + 1 < J else hidden(i + 1, 0)
                    outputs(i, j)
            for j in range(J):
                if j + 1 < J:
                    hidden(E // 2 - 1, j + 1)
                outputs(E // 2 - 1, j)

        @block.vector
        def _(dve):
            ch = Chain(dve, dve_step)
            dve.sem_inc(b_used, 1)
            dve.wait_ge(x_in, 64)
            dve.wait_ge(cst, 1)
            ln_vector(dve, ch, XN, 0)
            dve.wait_ge(sq_rdy, 1)
            ch.step(dve.tensor_reduce(NRM, SQ.rearrange("p t (h d) -> p (t h) d", d=HD), AX, ALU.add))
            Q, K, V = (QKV[:, :, j * D:(j + 1) * D] for j in range(3))
            ch.step(dve.tensor_copy(HIq[:], Q))
            ch.step(dve.tensor_scalar(HIk[:], K, -2.0, None, ALU.mult))
            ch.step(dve.tensor_copy(VS[:], V))
            ch.sync()
            ch.step(dve.tensor_tensor(LOq[:], Q, HIq[:].bitcast(F32), ALU.subtract))
            ch.step(dve.scalar_tensor_tensor(out=LOk[:], in0=K, scalar=-2.0, in1=HIk[:].bitcast(F32),
                                             op0=ALU.mult, op1=ALU.subtract))
            ch.step(dve.tensor_copy(NH[:], NRM))
            ch.step(dve.tensor_scalar(A0, NRM, -1.0, 1.0, ALU.mult, ALU.add))
            ch.sync()
            ch.step(dve.tensor_tensor(NL[:], NRM, NH[:].bitcast(F32), ALU.subtract))
            ch.link(dve.tensor_scalar(A1, A0, 0.0, None, ALU.is_equal))
            ch.link(dve.tensor_tensor(A2, A0, A1, ALU.add))
            ch.step(dve.tensor_scalar(A1, A1, -1.0, 1.0, ALU.mult, ALU.add))
            ch.link(dve.reciprocal(NRM, A2))
            ch.link(dve.tensor_tensor(A1, A1, NRM, ALU.mult))
            qa, ka = slice(0, H), slice(H, 2 * H)
            ch.step(dve.memset(QG[:], 0.0))
            ch.step(dve.memset(KG[:], 0.0))
            ch.sync()
            ch.step(dve.tensor_copy(QG[:].bitcast(F32R)[:, :, :, 0], A1[:, :, qa]))
            ch.step(dve.tensor_scalar(QG[:, :, :, 3], A0[:, :, qa], 0.0, None, ALU.is_ge))
            ch.step(dve.tensor_scalar(QG[:, :, :, 4], A0[:, :, qa], 0.0, None, ALU.is_le))
            ch.step(dve.tensor_scalar(KG[:].bitcast(F32R)[:, :, :, 0], A1[:, :, ka], 2.0, None, ALU.mult))
            ch.step(dve.tensor_scalar(KG[:, :, :, 3], A0[:, :, ka], 0.0, BIG, ALU.is_le, ALU.mult))
            ch.step(dve.tensor_scalar(KG[:, :, :, 4], A0[:, :, ka], 0.0, BIG, ALU.is_ge, ALU.mult))
            ch.sync()
            ch.step(dve.tensor_copy(QG[:, :, :, 1], QG[:, :, :, 0]))
            ch.step(dve.tensor_tensor(QG[:, :, :, 2], A1[:, :, qa], QG[:, :, :, 0], ALU.subtract))
            ch.step(dve.scalar_tensor_tensor(out=KG[:, :, :, 1], in0=A1[:, :, ka], scalar=2.0, in1=KG[:, :, :, 0],
                                             op0=ALU.mult, op1=ALU.subtract))
            ch.step(dve.tensor_copy(KG[:, :, :, 2], KG[:, :, :, 0]))
            ch.sync()
            dve.sem_inc(s_prep, 1)

            def back_at(b, k):
                if k == 0:
                    ch.enter(b, 1)
                    dve.wait_ge(b_full, b * 4 + 2)
                    o = bps[:, 0:2 * 144].rearrange("p (a n) -> p a n", n=9)
                    ch.link(dve.reciprocal(rec[:].rearrange("p t h -> p (t h)"), o[:, :, 8]))
                    dve.tensor_tensor(On[:].rearrange("p t (h d) -> p (t h) d", d=HD), o[:, :, 0:8],
                                      rec[:].rearrange("p t h -> p (t h)").unsqueeze(2).broadcast_to([P, TN * H, HD]),
                                      ALU.mult).then_inc(b_used, 1)
                elif k == 1:
                    dve.wait_ge(b_full, b * 4 + 3)
                    dve.tensor_copy(OnT[:, :], bps[:, 0:N]).then_inc(b_used, 1)
                else:
                    dve.wait_ge(b_full, b * 4 + 4)
                    xb = X[:, bass.ts(b, TN), :]
                    dve.tensor_tensor(xb, bps[:, 0:N].rearrange("p (t d) -> p t d", t=TN), xb,
                                      ALU.add).then_inc(b_used, 1)
                    ch.leave(b)

            def body(b, p, with_front, with_back):
                for h in range(H):
                    n = b * H + h
                    dve.wait_ge(u_full, n + 1)
                    wait(dve, u_used, n - 1)
                    dve.tensor_scalar(gb[:, h % 2], slot[h % 2][:, 1, :], 2.0 / DENOM_MIN, None,
                                      ALU.min).then_inc(g_rdy, 1)
                    dve.wait_ge(g_rdy, n + 1)
                    dve.scalar_tensor_tensor(out=Y[:, p, h], in0=slot[h % 2][:, 0, :], scalar=0.0,
                                             in1=gb[:, h % 2], op0=ALU.max, op1=ALU.mult).then_inc(u_used, 1)
                    dve.wait_ge(u_used, n + 1)
                    wait(dve, f_rdy, n - 3)
                    dve.scalar_tensor_tensor(out=Zr[:, h % 4], in0=Y[:, p, h], scalar=2.0, in1=Y[:, p, h],
                                             op0=ALU.add, op1=ALU.mult).then_inc(z_rdy, 1)
                    if with_back and h in (9, 11, 13):
                        back_at(b - 1, (h - 9) // 2)

            def back(b, p):
                for k in range(3):
                    back_at(b, k)

            batches(dve, lambda b, p: None, body, back)
            ch.end(B)

            dve.wait_ge(b_used, 3 * B + 1)
            ln_vector(dve, ch, XNx, 1)
            dve.wait_ge(wx_in, 16 * 8)
            for q in range(4):
                dve.wait_ge(qx_full, q + 1)
                dve.tensor_tensor(QX[:, 4 * q:4 * q + 4, :], tps[q % 2][:, :].rearrange("p (t d) -> p t d", d=D),
                                  bq_x[:, :].unsqueeze(1).broadcast_to([P, 4, D]), ALU.add).then_inc(qx_used, 1)
            dve.wait_ge(qx_used, 4)
            dve.wait_ge(xn_rdy, 2 * NT)
            ch.link(dve.tensor_copy(HIq[:], QX[:]))
            ch.step(dve.tensor_tensor(LOq[:], QX[:], HIq[:].bitcast(F32), ALU.subtract))
            ch.step(dve.tensor_tensor(X[:], X[:], bo_x[:, :].unsqueeze(1).broadcast_to([P, NT, D]), ALU.add))
            ch.sync()
            dve.sem_inc(q_prep, 1)
            dve.wait_ge(x_const, 1)

            def front(b, p):
                for n in range(2):
                    dve.wait_ge(x_tfull, b * XTI + n + 2)
                    if n == 0:
                        wait(dve, f_x, b * 2)
                    src = tps[(n + 1) % 2][:, :].rearrange("p (t c) -> p t c", c=2 * D)
                    dve.tensor_tensor(KV[:, 2 * n:2 * n + 2, :], src[:, :, 0:D],
                                      bkv_x[:, 0:D].unsqueeze(1).broadcast_to([P, 2, D]), ALU.add).then_inc(k_rdy, 1)
                    for t in range(2):
                        i = dve.tensor_tensor(VX[:, p, 2 * n + t, :, 0:8],
                                              src[:, t, D:2 * D].rearrange("p (h d) -> p h d", d=HD),
                                              bkv_x[:, D:2 * D].rearrange("p (h d) -> p h d", d=HD), ALU.add)
                        if t == 0:
                            ch.step(i)
                    i.then_inc(x_tdve, 1)
                masks(b, p)

            def masks(b, p):
                dve.wait_ge(m_in[p], 32 * (b // 2 + 1) if isinstance(b, int) else b * 16 + (32 if p == 0 else 16))
                dve.tensor_scalar(MB[:, p], M8[:, p], 1.0, BIG, ALU.subtract, ALU.mult).then_inc(mb_rdy, 1)
                dve.tensor_scalar(MBT[:, p], MT8[:, p], 1.0, BIG, ALU.subtract, ALU.mult).then_inc(mb_rdy, 1)

            def maximum(b, h):
                dve.wait_ge(mx_full, b * H + h + 1)
                dve.tensor_reduce(MX[:, :, h], slot[h % 2][:, :, :], AX, ALU.max).then_inc(mx_rdy, 1)

            def shift(b):
                dve.wait_ge(x_tfull, b * XTI + 9)
                dve.wait_ge(mx_rdy, (b + 1) * H)
                ch.link(dve.tensor_scalar(QF[:].bitcast(F32R)[:, :, :, 24], MX[:], -1.0, None, ALU.mult))
                ch.link(dve.scalar_tensor_tensor(out=QF[:, :, :, 25], in0=MX[:], scalar=-1.0, in1=QF[:, :, :, 24],
                                                 op0=ALU.mult, op1=ALU.subtract))
                dve.sem_inc(q2_rdy, 1)

            def back_at(b, k):
                if k == 0:
                    dve.wait_ge(xb_full, b * 4 + 2)
                    o = bps[:, 0:2 * 144].rearrange("p (a n) -> p a n", n=9)
                    ch.link(dve.reciprocal(rec[:].rearrange("p t h -> p (t h)"), o[:, :, 8]))
                    dve.tensor_tensor(On[:].rearrange("p t (h d) -> p (t h) d", d=HD), o[:, :, 0:8],
                                      rec[:].rearrange("p t h -> p (t h)").unsqueeze(2).broadcast_to([P, TN * H, HD]),
                                      ALU.mult).then_inc(xb_used, 1)
                elif k == 1:
                    dve.wait_ge(xb_full, b * 4 + 3)
                    dve.tensor_copy(OnT[:, :], bps[:, 0:N]).then_inc(xb_used, 1)
                else:
                    dve.wait_ge(xb_full, b * 4 + 4)
                    xb = X[:, bass.ts(b, TN), :]
                    dve.tensor_tensor(xb, bps[:, 0:N].rearrange("p (t d) -> p t d", t=TN), xb,
                                      ALU.add).then_inc(xb_used, 1)

            def body(b, p, with_front):
                ch.enter(b, 5)
                if with_front:
                    front(b + 1, 1 - p)
                for h in range(H):
                    if with_front:
                        maximum(b + 1, h)
                    if h in (2, 6, 10):
                        back_at(b, (h - 2) // 4)
                if with_front:
                    shift(b + 1)
                    ch.leave(b)

            front(0, 0)
            for h in range(H):
                maximum(0, h)
            shift(0)
            body(0, 0, True)
            with dve.Fori(0, (B - 2) // 2) as i:
                for k in range(2):
                    body(i * 2 + (k + 1), (k + 1) % 2, True)
            body(B - 1, (B - 1) % 2, False)
            ch.base, ch.n = ch.loop0 + (B - 1) * ch.per + 1, 0
            ch.loop0 = None

            dve.wait_ge(xb_used, 3 * B)
            ln_vector(dve, ch, XNf, 2)
            dve.wait_ge(rw_in, 16 * 5)
            dve.scalar_tensor_tensor(out=kw[:, :], in0=keysT[:, :], scalar=2.0, in1=rwT[:, :],
                                     op0=ALU.mult, op1=ALU.add).then_inc(kw_rdy, 1)
            dve.tensor_tensor(ksq[:, :], keysT[:, :], keysT[:, :], ALU.mult).then_inc(kw_rdy, 1)
            dve.wait_ge(ks_full, 1)
            ch.link(dve.tensor_tensor(lc[:, :], rb_b[:, :], tps[0][:, 0:E], ALU.subtract))
            dve.wait_ge(lg_full, 1)
            ch.link(dve.tensor_tensor(LG[:], tps[1][:, 0:NT * E].rearrange("p (t e) -> p t e", e=E),
                                      lc[:, :].unsqueeze(1).broadcast_to([P, NT, E]), ALU.add))
            for t in range(NT):
                ch.step(dve.max(TOP[:, t, :], LG[:, t, :]))
            ch.sync()
            for t in range(NT):
                ch.step(dve.max_index(TOPI[:, t, :], TOP[:, t, :], LG[:, t, :]))
            ch.step(dve.tensor_tensor(EX[:], LG[:], TOP[:, :, 0:1].broadcast_to([P, NT, E]), ALU.subtract))
            ch.sync()
            dve.sem_inc(ex_in, 1)
            ch.link(dve.tensor_copy(TOPF[:], TOPI[:]))
            dve.wait_ge(rt_const, 1)
            iota_b = iota_f[:, :].unsqueeze(1).broadcast_to([P, NT, E])
            for j in range(TOPK):
                dst = EQ if j else PICK
                ch.link(dve.tensor_tensor(dst[:], iota_b, TOPF[:, :, j:j + 1].broadcast_to([P, NT, E]), ALU.is_equal))
                if j:
                    ch.link(dve.tensor_tensor(PICK[:], PICK[:], EQ[:], ALU.add))
            dve.wait_ge(ex_rdy, 1)
            ch.link(dve.tensor_tensor(EX[:], EX[:], PICK[:], ALU.mult))
            ch.link(dve.tensor_reduce(SM[:, :], EX[:], AX, ALU.add))
            ch.link(dve.reciprocal(RS[:, :], SM[:, :]))
            dve.tensor_tensor(WT[:], EX[:], RS[:, :].unsqueeze(2).broadcast_to([P, NT, E]), ALU.mult).then_inc(wt_rdy, 1)
            dve.wait_ge(wt_rdy, 1)
            for q in range(4):
                dve.wait_ge(bo_full, q + 1)
                dve.wait_ge(xn_rdy, 3 * NT)
                xq = X[:, 4 * q:4 * q + 4, :]
                dve.tensor_tensor(xq, tps[q % 2][:, :].rearrange("p (t d) -> p t d", d=D), xq, ALU.add).then_inc(bo_used, 1)
            dve.wait_ge(bo_used, 4)

            def add(e, k, tb, prior):
                dve.wait_ge(y_full, k + 1)
                if prior:
                    dve.wait_ge(y_used, (k - TB) * 4 + 4)
                for tt in range(4):
                    t = tb * 4 + tt
                    dve.scalar_tensor_tensor(out=X[:, t, :], in0=tps[tb % 2][:, tt * P:(tt + 1) * P],
                                             scalar=WT[:, t, bass.ts(e, 1)], in1=X[:, t, :],
                                             op0=ALU.mult, op1=ALU.add).then_inc(y_used, 1)

            for tb in range(TB):
                add(0, tb, tb, False)
            with dve.Fori(1, E) as e:
                for tb in range(TB):
                    add(e, e * TB + tb, tb, True)


_IN = {"x": "x", "wqT_s": "L0_attn_Wq", "wkT_s": "L0_attn_Wk", "wvT_s": "L0_attn_Wv", "woT_s": "L0_attn_Wo",
       "wqT_x": "L0_xattn_Wq", "wkT_x": "L0_xattn_Wk", "wvT_x": "L0_xattn_Wv", "woT_x": "L0_xattn_Wo",
       "bq_x": "L0_xattn_bq", "bk_x": "L0_xattn_bk", "bv_x": "L0_xattn_bv", "bo_x": "L0_xattn_bo",
       "ctx": "ctx_1024", "keysT": "L0_ffn_keys", "rwT": "L0_ffn_rw", "rb": "L0_ffn_rb",
       "w1T": "L0_ffn_w1", "b1": "L0_ffn_b1", "w2T": "L0_ffn_w2", "b2": "L0_ffn_b2"}


def lay_out(inputs):
    a = {k: np.asarray(inputs[v]) for k, v in _IN.items()}
    for k in a:
        if "T_" in k or k.endswith("T"):
            a[k] = a[k].swapaxes(-1, -2)
    mask = np.asarray(inputs["mask_Bx1xSxS2_bf1"]).reshape(B, N, M).view(np.uint8)
    a["b1"] = a["b1"].reshape(E, FC, P).transpose(2, 0, 1)
    a["mask"], a["maskT"] = mask, mask.transpose(0, 2, 1)
    return {k: np.ascontiguousarray(v) for k, v in a.items()}


def kernel(**inputs):
    import concourse.bacc as bacc
    from concourse.bass_utils import run_bass_kernel_spmd
    nc = bacc.Bacc("TRN2", target_bir_lowering=False, num_devices=1)
    arrays = lay_out(inputs)
    a = {k: nc.dram_tensor(k, v.shape, mybir.dt.from_np(v.dtype), kind="ExternalInput").ap()
         for k, v in arrays.items()}
    out = nc.dram_tensor("out", (B, N, D), F32, kind="ExternalOutput").ap()
    decoder_block(nc, a, out)
    r = run_bass_kernel_spmd(nc, [arrays], core_ids=[0])
    return r.results[0]["out"]
```

```python
from contextlib import ExitStack

import numpy as np
import concourse.bass as bass
from concourse import mybir

F32 = mybir.dt.float32
F32R = mybir.dt.float32r
BF16 = mybir.dt.bfloat16
U8 = mybir.dt.uint8
ALU = mybir.AluOpType
ACT = mybir.ActivationFunctionType
AX = mybir.AxisListType.X

P = 128
B, N, D = 8, 256, 128
M = 512
H, HD = 16, 8
TN, TM = N // P, M // P
NT = B * TN
R, G = 4, H // 4
GP = G // 2
E, TOPK, FF = 16, 4, 512
FC = FF // P
EPS = 1e-5
BIG = float(2.0 ** 100)
DENOM_MIN = 1e-6
SCALE = 1.0 / float(np.sqrt(HD))

WEIGHTS = ("wqT_s", "wkT_s", "wvT_s", "woT_s")
WEIGHTS_X = ("wqT_x", "wkT_x", "wvT_x", "woT_x", "bq_x", "bk_x", "bv_x", "bo_x")


def wait(eng, sem, value, apart=None):
    if not isinstance(value, int) or value > 0:
        eng.wait_ge(sem, value)
        if apart is not None:
            eng.sem_inc(apart, 1)


class Chain:

    def __init__(self, eng, sem, apart=None):
        self.apart = apart
        self.eng, self.sem, self.base, self.n, self.loop0, self.per = eng, sem, 0, 0, None, None

    def step(self, ins):
        ins.then_inc(self.sem, 1)
        self.n += 1

    def sync(self):
        wait(self.eng, self.sem, self.base + self.n, None if isinstance(self.base, int) else self.apart)

    def link(self, ins):
        self.step(ins)
        self.sync()

    def enter(self, b, per):
        if self.loop0 is None:
            self.loop0 = self.base + self.n
        self.base, self.n, self.per = b * per + self.loop0, 0, per

    def leave(self, b):
        assert self.n == self.per, (self.n, self.per)
        self.base, self.n = (b + 1) * self.per + self.loop0, 0

    def end(self, batches):
        self.base, self.n, self.loop0 = self.loop0 + batches * self.per, 0, None


def decoder_block(nc, a, out):
    with ExitStack() as ctx:
        def sb(name, shape, dt=F32):
            return ctx.enter_context(nc.sbuf_tensor(name, shape, dt))

        def sem(name):
            return ctx.enter_context(nc.semaphore(name))

        X = sb("X", [P, NT, D])
        ident = sb("ident", [P, P])
        ident_bf = sb("ident_bf", [P, P], BF16)
        sel = sb("sel", [P, R * 9])
        bn_st = sb("bn_st", [P, NT, 6])
        bn_mv = sb("bn_mv", [P, NT, 2])
        ln_sd = sb("ln_sd", [P, NT])
        ln_rs = sb("ln_rs", [P, NT])
        eps_c = sb("eps_c", [P, 1])
        rec = sb("rec", [P, TN, H])
        On = sb("On", [P, TN, D])
        OnT = sb("OnT", [P, N])
        OT = sb("OT", [P, 2, N])
        HIq = sb("HIq", [P, NT, D], F32R)
        LOq = sb("LOq", [P, NT, D])

        def arena(phase):
            top = ctx.enter_context(ExitStack())
            return top, lambda name, shape, dt=F32: top.enter_context(
                nc.sbuf_tensor(f"{phase}_{name}", [P] + list(shape), dt))

        def ps(name, shape):
            return ctx.enter_context(nc.psum_tensor(name, [P] + shape, F32))

        slot = [ps(f"slot{i}", [2, 512]) for i in range(2)]
        tps = [ps(f"tps{i}", [512]) for i in range(2)]
        ops = ps("ops", [2, N])
        bps = ps("bps", [512])

        apart_g, apart_a, apart_s, apart_v = sem("apart_g"), sem("apart_a"), sem("apart_s"), sem("apart_v")
        x_in, w_in, cst = sem("x_in"), sem("w_in"), sem("cst")
        dve_step, act_step, pool_step = sem("dve_step"), sem("act_step"), sem("pool_step")
        ln_var, ln_dev, xn_rdy = sem("ln_var"), sem("ln_dev"), sem("xn_rdy")
        xt_full, xt_rdy = sem("xt_full"), sem("xt_rdy")
        qkv_full, qkv_used = sem("qkv_full"), sem("qkv_used")
        sq_rdy, s_prep, s_const = sem("sq_rdy"), sem("s_prep"), sem("s_const")
        s_feat, s_norm, s_tfull, s_tused, s_vf = sem("s_feat"), sem("s_norm"), sem("s_tfull"), sem("s_tused"), sem("s_vf")
        u_full, u_used = sem("u_full"), sem("u_used")
        g_rdy, y_rdy, z_rdy = sem("g_rdy"), sem("y_rdy"), sem("z_rdy")
        root_rdy, f_rdy, w_rdy = sem("root_rdy"), sem("f_rdy"), sem("w_rdy")
        ln_rdy = sem("ln_rdy")
        o_full, o_rdy = sem("o_full"), sem("o_rdy")
        b_full, b_used, s_done = sem("b_full"), sem("b_used"), sem("s_done")

        def ln_vector(dve, ch, XN, k):
            for t in range(NT):
                ch.step(dve.bn_stats(bn_st[:, t, :], X[:, t, :]))
            ch.sync()
            for t in range(NT):
                i = dve.bn_aggr(bn_mv[:, t, :], bn_st[:, t, :])
                if t < NT - 1:
                    ch.step(i)
            i.then_inc(ln_var, 1)
            ch.sync()
            dve.wait_ge(ln_dev, k + 1)
            ch.link(dve.reciprocal(ln_rs[:, :], ln_sd[:, :]))
            for t in range(NT):
                dve.tensor_scalar(XN[:, t, :], X[:, t, :], bn_mv[:, t, 0:1], ln_rs[:, t:t + 1],
                                  ALU.subtract, ALU.mult).then_inc(xn_rdy, 1)

        def ln_scalar(act, k):
            act.wait_ge(ln_var, k + 1)
            act.activation(ln_sd[:, :], bn_mv[:, :, 1], ACT.Sqrt, bias=eps_c[:, 0:1]).then_inc(ln_dev, 1)

        def ln_tensor(pe, XN, k):
            for t in range(NT):
                pe.wait_ge(xn_rdy, k * NT + t + 1)
                i = pe.transpose(slot[t // 8][:, t // 4 % 2, t % 4 * P:(t % 4 + 1) * P], XN[:, t, :], ident[:, :])
                if t % 4 == 3:
                    i.then_inc(xt_full, 1)

        def ln_copy(act, xnT, k):
            for q in range(4):
                act.wait_ge(xt_full, 4 * k + q + 1)
                act.copy(xnT[:, 512 * q:512 * q + 512], slot[q // 2][:, q % 2, :]).then_inc(xt_rdy, 1)

        topS, sS = arena("S")
        Y = sS("Y", [2, H, 2 * N])
        prepS = Y[:, :, :, :].rearrange("p a h n -> p (a h n)")
        at = [0]

        def over_Y(shape, names, **sizes):
            n = int(np.prod(shape))
            at[0] += n
            v = prepS[:, at[0] - n:at[0]]
            return v.rearrange(f"p ({names}) -> p {names}", **sizes) if sizes else v

        XN = over_Y([NT, D], "t d", t=NT)
        xnT = over_Y([NT * P], "")
        QKV = over_Y([NT, 3 * D], "t d", t=NT)
        SQ = over_Y([NT, 2 * D], "t d", t=NT)
        NRM = over_Y([NT, 2 * H], "t h", t=NT)
        A0 = over_Y([NT, 2 * H], "t h", t=NT)
        A1 = over_Y([NT, 2 * H], "t h", t=NT)
        A2 = over_Y([NT, 2 * H], "t h", t=NT)
        ZR = 8
        VW = 16
        Zr = sS("Zr", [ZR, 2 * N])
        gb = sS("gb", [2, 2 * N])
        VS = sS("VS", [NT, D])
        HIk, LOk = sS("HIk", [NT, D], F32R), sS("LOk", [NT, D])
        NH, NL = sS("NH", [NT, 2 * H], F32R), sS("NL", [NT, 2 * H])
        QG, KG = sS("QG", [NT, H, 5]), sS("KG", [NT, H, 5])
        UQ, UK = sS("UQ", [TN, H, 32]), sS("UK", [TN, H, 32])
        GQ, GK = sS("GQ", [TN, H, 8]), sS("GK", [TN, 4, H, 8])
        UQT, UKT = sS("UQT", [2, G, N], F32R), sS("UKT", [2, G, N], F32R)
        GQT, GKT = sS("GQT", [2, N], F32R), sS("GKT", [2, 4, N], F32R)
        VF = sS("VF", [2, TN, H, VW])
        wqkv = sS("wqkv", [3 * D])
        wo_s = sS("wo_s", [D])
        STI = 7

        topS.close()

        topX, sX = arena("X")
        XNx = sX("XN", [NT, D])
        xnTx = sX("xnT", [NT * P])
        QX = sX("QX", [NT, D])
        wq_x, wkv_x, wo_x = sX("wq", [D]), sX("wkv", [2 * D]), sX("wo", [D])
        bq_x, bkv_x, bo_x = sX("bq", [D]), sX("bkv", [2 * D]), sX("bo", [D])
        CT = sX("CT", [2, TM, D])
        ctxT = sX("ctxT", [M])
        KV = sX("KV", [TM, D])
        QF, KF = sX("QF", [TN, H, 32]), sX("KF", [TM, H, 32])
        QFT, QFT2 = sX("QFT", [G, N], F32R), sX("QFT2", [G, N], F32R)
        KFT = sX("KFT", [2, G, M], F32R)
        VX = sX("VX", [2, TM, H, 32])
        M8, MT8 = sX("M8", [2, TN, M], U8), sX("MT8", [2, TM, N], U8)
        MB, MBT = sX("MB", [2, TN, M], BF16), sX("MBT", [2, TM, N], BF16)
        MX = sX("MX", [TN, H])
        W = sX("W", [4, TM, N])
        VST = sX("VST", [TM, D])
        junk = sX("junk", [TN, M], BF16)
        topX.close()
        qx_full, qx_used, q_prep = sem("qx_full"), sem("qx_used"), sem("q_prep")
        wx_in, x_const = sem("wx_in"), sem("x_const")
        c_in, m_in, mt_in = ([sem(f"{n}_in{i}") for i in range(2)] for n in ("c", "m", "mt"))
        x_tfull, x_tact, x_tdve = sem("x_tfull"), sem("x_tact"), sem("x_tdve")
        k_rdy, kf_rdy, qf_rdy, q2_rdy = sem("k_rdy"), sem("kf_rdy"), sem("qf_rdy"), sem("q2_rdy")
        qmax_rdy, rec_rdy = sem("qmax_rdy"), sem("rec_rdy")
        mb_rdy, mbt_rdy, vx_rdy = sem("mb_rdy"), sem("mbt_rdy"), sem("vx_rdy")
        mx_full, mx_rdy, e_full, e_rdy = sem("mx_full"), sem("mx_rdy"), sem("e_full"), sem("e_rdy")
        pv_head, xo_rdy, xb_full, xb_used = sem("pv_head"), sem("xo_rdy"), sem("xb_full"), sem("xb_used")

        topF, sF = arena("F")
        XNf, xnTf = sF("XN", [NT, D]), sF("xnT", [NT * P])
        keysT, rwT, rb_b = sF("keysT", [E]), sF("rwT", [E]), sF("rb", [E])
        kw, ksq, lc = sF("kw", [E]), sF("ksq", [E]), sF("lc", [E])
        ones = sF("ones", [P])
        iota_i, iota_f = sF("iota_i", [E], mybir.dt.int32), sF("iota_f", [E])
        LG, EX, PICK, EQ = (sF(n, [NT, E]) for n in ("LG", "EX", "PICK", "EQ"))
        TOP, TOPI, TOPF = sF("TOP", [NT, 8]), sF("TOPI", [NT, 8], mybir.dt.uint32), sF("TOPF", [NT, 8])
        SM, RS = sF("SM", [NT]), sF("RS", [NT])
        WT, WTT = sF("WT", [NT, E]), sF("WTT", [NT * P])
        B1, b2_sb = sF("B1", [E, FC]), sF("b2", [D])
        W1, W2 = sF("W1", [2, FF]), sF("W2", [2, FC, D])
        HB = sF("HB", [2, FC, 512])
        TB = NT // 4
        topF.close()
        rw_in, rt_const, kw_rdy, ks_full, lg_full = sem("rw_in"), sem("rt_const"), sem("kw_rdy"), sem("ks_full"), sem("lg_full")
        ex_in, ex_rdy, wt_rdy = sem("ex_in"), sem("ex_rdy"), sem("wt_rdy")
        wtt_full, wtt_rdy, bo_full, bo_used = sem("wtt_full"), sem("wtt_rdy"), sem("bo_full"), sem("bo_used")
        ew_in = [sem("ew_in0"), sem("ew_in1")]
        h_full, h_rdy, y_full, y_used = sem("h_full"), sem("h_rdy"), sem("y_full"), sem("y_used")
        out_done = sem("out_done")

        X_FIRST = [(n, 0) for n in range(10)] + [(n, 1) for n in (0, 1, 2, 3, 4, 7, 5)]
        X_BODY = ((10, 0, 1), (6, 1, 2), (0, 2, 3), (1, 2, 5), (8, 1, 6), (2, 2, 7), (9, 1, 10),
                  (3, 2, 12), (4, 2, 13), (7, 2, 14), (5, 2, 15))
        XI = len(X_BODY)

        def by(items):
            d = sum(it[0] in (1, 2) for it in items)
            return len(items) - d, d

        def x_before(b):
            return X_FIRST + [(n, c + i) for i in range(b) for n, c, _ in X_BODY if c + i < B]

        (X_A0, X_D0), (XA, XD) = by(X_FIRST), by(X_BODY)

        def x_acts(b):
            return by(x_before(b))[0] if isinstance(b, int) else b * XA + X_A0

        class XItem:

            def __init__(self, i, b=None, p=0):
                if b is None:
                    (self.n, self.c), before, base = X_FIRST[i], X_FIRST[:i], (0, 0, 0)
                elif isinstance(b, int):
                    self.n, self.c = X_BODY[i][0], b + X_BODY[i][1]
                    before = x_before(b) + [x for x in X_BODY[:i] if x[1] + b < B]
                    base = (0, 0, 0)
                else:
                    self.n, self.c = X_BODY[i][0], b + X_BODY[i][1]
                    before = X_FIRST + list(X_BODY) * p + list(X_BODY[:i])
                    base = tuple((b - p) * x for x in (XI, XA, XD))
                self.p = self.c % 2 if b is None else (p + X_BODY[i][1]) % 2
                self.bank = tps[len(before) % 2]
                last, (acts, dves) = before[-2:], by(before)
                self.k, self.act = base[0] + len(before), base[1] + acts
                if len(last) < 2:
                    self.bank_free = (x_tact, 0)
                elif last[0][0] in (1, 2):
                    self.bank_free = (x_tdve, base[2] + dves - (last[1][0] in (1, 2)))
                else:
                    self.bank_free = (x_tact, base[1] + acts - (last[1][0] not in (1, 2)))

        def x_items(b, h, nxt, nxt2):
            return [i for i, (n, c, at) in enumerate(X_BODY) if at == h and (c == 0 or (nxt, nxt2)[c - 1])]

        def x_batches(eng, body):
            body(0, 0, True, True)
            with eng.Fori(0, 2) as i:
                for k in (1, 2):
                    body(i * 2 + k, k % 2, True, True)
            body(B - 3, 1, True, True)
            body(B - 2, 0, True, False)
            body(B - 1, 1, False, False)

        block = ctx.enter_context(nc.Block())

        @block.sync
        def _(sp):
            x_t = a["x"].rearrange("b (t p) d -> p (b t) d", p=P)
            for q in range(4):
                sp.dma_start(X[:, 4 * q:4 * q + 4, :], x_t[:, 4 * q:4 * q + 4, :]).then_inc(x_in, 16)
            for j, n in enumerate(WEIGHTS[:3]):
                sp.dma_start(wqkv[:, j * D:(j + 1) * D], a[n]).then_inc(w_in, 16)
            sp.dma_start(wo_s[:, :], a["woT_s"]).then_inc(w_in, 16)
            sp.wait_ge(b_used, 3 * B + 1)
            sp.dma_start(wq_x[:, :], a["wqT_x"]).then_inc(wx_in, 16)
            sp.dma_start(wkv_x[:, 0:D], a["wkT_x"]).then_inc(wx_in, 16)
            sp.dma_start(wkv_x[:, D:2 * D], a["wvT_x"]).then_inc(wx_in, 16)
            sp.dma_start(wo_x[:, :], a["woT_x"]).then_inc(wx_in, 16)
            for dst, n in ((bq_x[:, :], "bq_x"), (bkv_x[:, 0:D], "bk_x"), (bkv_x[:, D:2 * D], "bv_x"),
                           (bo_x[:, :], "bo_x")):
                sp.dma_start(dst, a[n].partition_broadcast(P)).then_inc(wx_in, 16)
            ctx_t = a["ctx"].rearrange("b (t p) d -> b p t d", p=P)
            m_t = a["mask"].rearrange("b (t p) m -> b p t m", p=P)
            mT_t = a["maskT"].rearrange("b (t p) q -> b p t q", p=P)

            def load(c, p):
                if isinstance(c, int):
                    done = {0: 0, 1: 0, 2: 1, 3: len(X_FIRST) - 6}[c]
                else:
                    done = c * XI + (len(X_FIRST) + 3 - 4 * XI)
                wait(sp, x_tfull, done, apart_s)
                sp.dma_start(CT[:, p], ctx_t[c]).then_inc(c_in[p], 16)
                wait(sp, mb_rdy, c - 1, apart_s)
                sp.dma_start(M8[:, p], m_t[c]).then_inc(m_in[p], 16)
                wait(sp, mbt_rdy, c - 1, apart_s)
                sp.dma_start(MT8[:, p], mT_t[c]).then_inc(mt_in[p], 16)

            for c in range(4):
                load(c, c % 2)
            with sp.Fori(2, B // 2) as i:
                for p in range(2):
                    load(i * 2 + p, p)
            sp.wait_ge(xb_used, 3 * B)
            for dst, src in ((keysT[:, :], a["keysT"]), (rwT[:, :], a["rwT"]), (rb_b[:, :], a["rb"].partition_broadcast(P)),
                             (B1[:], a["b1"]), (b2_sb[0:E, :], a["b2"])):
                sp.dma_start(dst, src).then_inc(rw_in, 16)
            w2_t = a["w2T"].rearrange("e (c p) d -> e p c d", p=P)

            def load_expert(e, p):
                wait(sp, y_full, (e - 1) * TB, apart_s)
                sp.dma_start(W1[:, p], a["w1T"][e]).then_inc(ew_in[p], 16)
                sp.dma_start(W2[:, p], w2_t[e]).then_inc(ew_in[p], 16)

            for e in range(2):
                load_expert(e, e)
            with sp.Fori(1, E // 2) as i:
                for p in range(2):
                    load_expert(i * 2 + p, p)
            o_t = out.rearrange("b (t p) d -> p (b t) d", p=P)
            sp.wait_ge(y_used, E * NT)
            sp.dma_start(o_t, X[:, :, :]).then_inc(out_done, 16)
            sp.wait_ge(out_done, 16)

        def batches(eng, front, body, back):
            front(0, 0)
            body(0, 0, True, False, False)
            body(1, 1, True, True, False)
            with eng.Fori(1, B // 2 - 1) as i:
                for k in range(2):
                    body(i * 2 + k, k, True, True, True)
            body(B - 2, 0, True, True, True)
            body(B - 1, 1, False, True, True)
            back(B - 1, 1)

        @block.gpsimd
        def _(g):
            ch = Chain(g, pool_step, apart_g)
            ch.step(g.memset(eps_c[:, :], EPS))
            ch.link(g.memset(ident[:, :], 0.0))
            ch.link(g.affine_select(out=ident[:, :], in_=ident[:, :], compare_op=ALU.not_equal, fill=1.0,
                                    base=0, pattern=[[-1, P]], channel_multiplier=1))
            ch.step(g.tensor_copy(ident_bf[:, :], ident[:, :]))
            for r in range(R):
                ch.step(g.tensor_copy(sel[:, 9 * r:9 * r + 9], ident[:, 32 * r:32 * r + 9]))
            for t in (UQ, UK, GQ, GK, VF):
                ch.step(g.memset(t[:], 0.0))
            ch.sync()
            ch.step(g.memset(UQ[:, :, :, 26:28], 1.0))
            ch.step(g.memset(UK[:, :, :, 24:26], 1.0))
            for p in range(2):
                ch.step(g.memset(VF[:, p, :, :, 8:9], 1.0))
            ch.sync()
            g.sem_inc(cst, 1)

            def per_head(x, bt, tt):
                return x[:, bt, :][:, tt].rearrange("p (h d) -> p h d", d=HD)

            HQ, HK = HIq[:].bitcast(F32), HIk[:].bitcast(F32)

            def copies(b):
                bt, tiles = bass.ts(b, TN), range(TN)
                return ([(UQ[:, tt, :, c:c + 8], per_head(src, bt, tt))
                         for tt in tiles for c, src in ((0, HQ), (8, HQ), (16, LOq))],
                        [(UK[:, tt, :, c:c + 8], per_head(src, bt, tt))
                         for tt in tiles for c, src in ((0, HK), (8, LOk), (16, HK))])

            PARTS = 4

            def front_part(b, k):
                if k == 0:
                    ch.enter(b, 12)
                    wait(g, s_tfull, b * STI, apart_g)
                for dst, src in copies(b)[k // 2][k % 2 * 3:k % 2 * 3 + 3]:
                    ch.step(g.tensor_copy(dst, src))
                if k % 2:
                    ch.sync()
                    g.sem_inc(s_feat, 1)
                if k == PARTS - 1:
                    ch.leave(b)

            def front_values(b, p):
                wait(g, o_full, (b - 1) * GP, apart_g)
                for tt in range(TN):
                    g.tensor_copy(VF[:, p, tt, :, 0:8], per_head(VS, bass.ts(b, TN), tt)).then_inc(s_vf, 1)

            def front(b, p):
                for k in range(PARTS):
                    front_part(b, k)
                front_values(b, p)

            def body(b, p, with_front, with_back, with_end):
                for h in range(H):
                    if with_front and h < PARTS:
                        front_part(b + 1, h)
                    if with_front and h == 15:
                        front_values(b + 1, 1 - p)
                    g.wait_ge(root_rdy, b * H + h + 1)
                    g.tensor_tensor(Y[:, p, h], Y[:, p, h], Zr[:, h % ZR], ALU.add).then_inc(f_rdy, 1)

            g.wait_ge(s_prep, 1)
            batches(g, front, body, lambda b, p: None)
            ch.end(B)

            g.wait_ge(b_used, 3 * B + 1)
            for t in (QF, KF, VX):
                ch.step(g.memset(t[:], 0.0))
            ch.sync()
            ch.step(g.memset(KF[:, :, :, 24:26], 1.0))
            for p in range(2):
                ch.step(g.memset(VX[:, p, :, :, 8:9], 1.0))
            ch.sync()
            g.sem_inc(x_const, 1)

            def heads(x):
                return x.rearrange("p t (h d) -> p t h d", d=HD)

            def q_features(c, half):
                cols, hs = slice(64 * half, 64 * half + 64), slice(8 * half, 8 * half + 8)
                for tt in range(TN):
                    for f, src in ((0, HQ), (8, HQ), (16, LOq)):
                        g.tensor_copy(QF[:, tt, hs, f:f + 8],
                                      src[:, bass.ts(c, TN)][:, tt, cols].rearrange("p (h d) -> p h d", d=HD)
                                      ).then_inc(qf_rdy, 1)

            def k_features(c):
                wait(g, k_rdy, c * 2 + 2, apart_g)
                g.tensor_copy(KF[:].bitcast(F32R)[:, :, :, 0:8], heads(KV[:, :, :])).then_inc(kf_rdy, 1)
                wait(g, kf_rdy, c * 3 + 1, apart_g)
                g.tensor_copy(KF[:, :, :, 16:24], KF[:, :, :, 0:8]).then_inc(kf_rdy, 1)
                g.tensor_tensor(KF[:, :, :, 8:16], heads(KV[:, :, :]), KF[:, :, :, 0:8], ALU.subtract).then_inc(kf_rdy, 1)

            g.wait_ge(q_prep, 1)
            q_features(0, 0)
            q_features(0, 1)
            k_features(0)
            g.wait_ge(x_tfull, 10)
            q_features(1, 0)
            k_features(1)

            def body(b, p, nxt, nxt2):
                if nxt:
                    wait(g, x_tfull, XItem(0, b).k + 1, apart_g)
                    q_features(b + 1, 1)
                if nxt2:
                    wait(g, x_tfull, XItem(1, b).k + 1, apart_g)
                    k_features(b + 2)
                    wait(g, x_tfull, XItem(6, b).k + 1, apart_g)
                    q_features(b + 2, 0)

            x_batches(g, body)

            g.wait_ge(xb_used, 3 * B)
            ch.step(g.memset(ones[:, :], 1.0))
            ch.link(g.iota(iota_i[:, :], pattern=[[1, E]], base=0, channel_multiplier=0))
            ch.link(g.tensor_copy(iota_f[:, :], iota_i[:, :]))
            g.sem_inc(rt_const, 1)

        @block.scalar
        def _(act):
            act.wait_ge(cst, 1)
            ln_scalar(act, 0)
            ln_copy(act, xnT, 0)
            for t in range(NT):
                act.wait_ge(qkv_full, t + 1)
                act.copy(QKV[:, t, :], tps[t % 2][:, 0:3 * D]).then_inc(qkv_used, 1)
            act.wait_ge(qkv_used, NT)
            act.activation(SQ[:, :, :], QKV[:, :, 0:2 * D], ACT.Square).then_inc(sq_rdy, 1)

            def front_copy(b, p, n):
                act.wait_ge(s_tfull, b * STI + n + 1)
                if n == 0:
                    wait(act, u_full, (b - 1) * H)
                src = tps[n % 2]
                if n < 4:
                    dst = (UQT, UKT)[n % 2][:, p, n // 2 * 2:n // 2 * 2 + 2, :]
                elif n == 4:
                    dst = GQT[:, p, :]
                    src = src[:, 0:N]
                else:
                    dst = GKT[:, p, (n - 5) * 2:(n - 5) * 2 + 2, :]
                act.copy(dst, src if n == 4 else src[:, :].rearrange("p (g n) -> p g n", g=2)).then_inc(s_tused, 1)

            def front(b, p):
                for n in range(STI):
                    front_copy(b, p, n)

            def body(b, p, with_front, with_back, with_end):
                for h in range(H):
                    if h % 8 == 4 and (h > 4 or with_back):
                        act.preload_act_table_set("sqrt_and_others")
                    act.wait_ge(z_rdy, b * H + h + 1)
                    act.activation(Zr[:, h % ZR], Zr[:, h % ZR], ACT.Sqrt).then_inc(root_rdy, 1)
                    if h == 3 and with_back:
                        weights(b - 1, 1 - p, 1, lambda k: None)
                        out_copy(b - 1, 0)
                    if with_front and h in (7, 8, 9, 11):
                        front_copy(b + 1, 1 - p, (7, 8, 9, 11).index(h))
                    if h == 11:
                        weights(b, p, 0, lambda k: (with_back and k == 3 and out_copy(b - 1, 1),
                                                    with_front and k < 3 and front_copy(b + 1, 1 - p, 4 + k)))

            def weights(b, p, half, between):
                act.preload_act_table_set("natural_log_exp_and_others")
                for j in range(2):
                    g = 2 * half + j
                    v = Y[:, p, R * g:R * g + R, :]
                    act.wait_ge(f_rdy, b * H + R * g + R)
                    act.activation(v, v, ACT.Ln, bias=1.0).then_inc(ln_rdy, 1)
                    between(2 * j)
                    act.wait_ge(ln_rdy, b * G + g + 1)
                    act.activation(v, v, ACT.Exp, scale=-1.0).then_inc(w_rdy, 1)
                    between(2 * j + 1)

            def out_copy(b, q):
                act.wait_ge(o_full, b * GP + q + 1)
                wait(act, b_full, b * 4 + 1 if q else b * 4 - 2)
                act.copy(OT[:, :, :], ops[:, :, :]).then_inc(o_rdy, 1)

            def back(b, p):
                weights(b, p, 1, lambda k: None)
                for q in range(GP):
                    out_copy(b, q)

            batches(act, front, body, back)

            ln_scalar(act, 1)
            ln_copy(act, xnTx, 1)

            def copy_item(it):
                n, p, src = it.n, it.p, it.bank[:, :]
                wait(act, x_tfull, it.k + 1, apart_a)
                if n >= 7:
                    src = src.rearrange("p (g n) -> p g n", g=2)
                dst = ctxT[:, :] if n == 0 else KFT[:, p, n - 3, :] if n < 7 else \
                    (QFT if n < 9 else QFT2)[:, (n - 7) % 2 * 2:(n - 7) % 2 * 2 + 2, :]
                act.copy(dst, src).then_inc(x_tact, 1)

            def out_copy(b, q):
                wait(act, pv_head, b * H + 8 * (q + 1), apart_a)
                wait(act, xb_full, b * 4 + 1 if q else b * 4 - 2, apart_a)
                act.copy(OT[:, :, :], ops[:, :, :]).then_inc(xo_rdy, 1)

            def body(b, p, nxt, nxt2):
                for h in range(H):
                    for j in range(2):
                        k = (b * H + h) * 2 + j
                        wait(act, e_full, k + 1, apart_a)
                        if not (isinstance(b, int) and b == 0 and h < 4):
                            wait(act, pv_head, b * H + h - 3, apart_a)
                        act.activation(W[:, h % 4, 2 * j:2 * j + 2, :].rearrange("p t n -> p (t n)"), slot[0][:, j, :],
                                       ACT.Exp, scale=SCALE).then_inc(e_rdy, 1)
                    if h == 0 and not (isinstance(b, int) and b == 0):
                        out_copy(b - 1, 1)
                    if h == 8:
                        out_copy(b, 0)
                    for i in x_items(b, h, nxt, nxt2):
                        if X_BODY[i][0] not in (1, 2):
                            copy_item(XItem(i, b, p))

            for i, (n, c) in enumerate(X_FIRST):
                if n not in (1, 2):
                    copy_item(XItem(i))
            x_batches(act, body)
            out_copy(B - 1, 1)

            ln_scalar(act, 2)
            ln_copy(act, xnTf, 2)
            act.wait_ge(ex_in, 1)
            act.activation(EX[:], EX[:], ACT.Exp).then_inc(ex_rdy, 1)
            for q in range(4):
                act.wait_ge(wtt_full, q + 1)
                act.copy(WTT[0:E, 512 * q:512 * q + 512], slot[q // 2][0:E, q % 2, :]).then_inc(wtt_rdy, 1)

            def gelus(e, tb):
                k = e * TB + tb
                for c in range(FC):
                    if c == 0:
                        wait(act, y_full, k - 1)
                    wait(act, h_full, k * FC + c + 1, apart_a)
                    act.activation(HB[:, tb % 2, c, :], slot[c // 2][:, c % 2, :], ACT.Gelu,
                                   bias=B1[:, bass.ts(e, 1), c]).then_inc(h_rdy, 1)

            for tb in range(TB):
                gelus(0, tb)
            with act.Fori(1, E) as e:
                for tb in range(TB):
                    gelus(e, tb)

        @block.tensor
        def _(pe):
            pe.wait_ge(cst, 1)
            ln_tensor(pe, XN, 0)
            pe.wait_ge(w_in, 64)
            for t in range(NT):
                pe.wait_ge(xt_rdy, t // 4 + 1)
                if t >= 2:
                    pe.wait_ge(qkv_used, t - 1)
                pe.matmul(tps[t % 2][:, 0:3 * D], xnT[:, t * P:(t + 1) * P], wqkv[:, :],
                          start=True, stop=True).then_inc(qkv_full, 1)
            pe.wait_ge(qkv_used, NT)

            def front_item(b, p, n):
                if n == 0:
                    pe.wait_ge(s_norm, (b + 1) * 14)
                if n < 2:
                    pe.wait_ge(s_feat, b * 2 + n + 1)
                wait(pe, s_tused, b * STI + n - 1)
                dst = tps[n % 2]
                if n < 4:
                    src = (UQ, UK)[n % 2]
                    parts = [(j, tt, src[:, tt, R * (n // 2 * 2 + j):R * (n // 2 * 2 + j + 1), :])
                             for j in range(2) for tt in range(TN)]
                elif n == 4:
                    parts = [(0, tt, GQ[:, tt]) for tt in range(TN)]
                else:
                    parts = [(j, tt, GK[:, tt, (n - 5) * 2 + j]) for j in range(2) for tt in range(TN)]
                for j, tt, src in parts:
                    ins = pe.transpose(dst[:, j * N + tt * P:j * N + (tt + 1) * P],
                                       src.rearrange("p h f -> p (h f)"), ident[:, :])
                ins.then_inc(s_tfull, 1)

            END_AT = (1, 6, 8)
            FRONT_AT = (7, 8, 10, 11, 12, 13)
            BACK_AT = (2, 3, 4, 5, 12, 13, 14, 15)

            def front(b, p):
                for n in range(STI - 1):
                    front_item(b, p, n)

            def scores(b, p, h):
                g, r = h // R, slice(32 * (h % R), 32 * (h % R) + 32)
                rg = slice(32 * (h // 4), 32 * (h // 4) + 32)
                if h in (0, 2):
                    pe.wait_ge(s_tused, b * STI + STI - (h == 0))
                wait(pe, u_used, b * H + h - 1)
                for kt in range(TN):
                    pe.matmul(slot[h % 2][:, 0, kt * N:(kt + 1) * N], UKT[r, p, g, kt * P:(kt + 1) * P],
                              UQT[r, p, g, :], start=True, stop=True)
                for kt in range(TN):
                    ins = pe.matmul(slot[h % 2][:, 1, kt * N:(kt + 1) * N],
                                    GKT[rg, p, h % 4, kt * P:(kt + 1) * P], GQT[rg, p, :], start=True, stop=True)
                ins.then_inc(u_full, 1)

            def product(b, p, j):
                g = j // 2
                if j == 0:
                    pe.wait_ge(s_vf, (b + 1) * TN)
                if j % 2 == 0:
                    pe.wait_ge(w_rdy, b * G + g + 1)
                if j == 4:
                    pe.wait_ge(o_rdy, b * GP + 1)
                for r in (j % 2 * 2, j % 2 * 2 + 1):
                    h = R * g + r
                    for kt in range(TN):
                        ins = pe.matmul(ops[32 * r:32 * r + VW, g % 2, :], VF[:, p, kt, h, :],
                                        Y[:, p, h, kt * N:(kt + 1) * N], start=(kt == 0), stop=(kt == TN - 1))
                if j % 4 == 3:
                    ins.then_inc(o_full, 1)

            def turn(b, q):
                if q == 0:
                    pe.wait_ge(b_used, b * 3 + 1)
                pe.wait_ge(o_rdy, b * GP + q + 1)
                for g in (0, 1):
                    for tt in range(TN):
                        ins = pe.matmul(bps[:, tt * 144 + (2 * q + g) * 36:tt * 144 + (2 * q + g + 1) * 36],
                                        OT[:, g, tt * P:(tt + 1) * P], sel[:, :], start=True, stop=True)
                ins.then_inc(b_full, 1)

            def back_at(b, p, k):
                product(b, p, k)
                if k == 5:
                    turn(b, 0)

            def end_at(b, k):
                if k == 0:
                    turn(b, 1)
                if k == 1:
                    pe.wait_ge(b_used, b * 3 + 2)
                    for tt in range(TN):
                        ins = pe.transpose(bps[:, tt * P:(tt + 1) * P], On[:, tt, :], ident[:, :])
                    ins.then_inc(b_full, 1)
                if k == 2:
                    pe.wait_ge(b_used, b * 3 + 3)
                    for tt in range(TN):
                        ins = pe.matmul(bps[:, tt * P:(tt + 1) * P], OnT[:, tt * P:(tt + 1) * P], wo_s[:, :],
                                        start=True, stop=True)
                    ins.then_inc(b_full, 1)

            def body(b, p, with_front, with_back, with_end):
                for h in range(H):
                    scores(b, p, h)
                    if h == 0:
                        front_item(b, p, STI - 1)
                    if with_end and h in END_AT:
                        end_at(b - 2, END_AT.index(h))
                    for k, at in enumerate(BACK_AT):
                        if with_back and h == at:
                            back_at(b - 1, 1 - p, k)
                    if with_front:
                        for n in range(STI - 1):
                            if h == FRONT_AT[n]:
                                front_item(b + 1, 1 - p, n)

            def back(b, p):
                for k in range(3):
                    end_at(b - 1, k)
                for k in range(2 * G):
                    back_at(b, p, k)
                for k in range(3):
                    end_at(b, k)

            batches(pe, front, body, back)

            ln_tensor(pe, XNx, 1)
            pe.wait_ge(wx_in, 16 * 8)
            for q in range(4):
                pe.wait_ge(xt_rdy, 4 + q + 1)
                wait(pe, qx_used, q - 1)
                for t in range(4):
                    ins = pe.matmul(tps[q % 2][:, t * P:(t + 1) * P], xnTx[:, (4 * q + t) * P:(4 * q + t + 1) * P],
                                    wq_x[:, :], start=True, stop=True)
                ins.then_inc(qx_full, 1)
            pe.wait_ge(qx_used, 4)

            def data_count(c, p, once):
                return 16 * once * (c // 2 + 1) if isinstance(c, int) else c * (8 * once) + 8 * once * (2 - p)

            def item(it):
                n, p, c, dst = it.n, it.p, it.c, it.bank
                wait(pe, *it.bank_free)
                if n == 0:
                    pe.wait_ge(c_in[p], data_count(c, p, 1))
                    for t in range(TM):
                        ins = pe.transpose(dst[:, t * P:(t + 1) * P], CT[:, p, t, :], ident[:, :])
                elif n < 3:
                    if n == 1:
                        wait(pe, x_tact, it.act)
                    for j in range(2):
                        t = (n - 1) * 2 + j
                        ins = pe.matmul(dst[:, j * N:(j + 1) * N], ctxT[:, t * P:(t + 1) * P], wkv_x[:, :],
                                        start=True, stop=True)
                elif n < 7:
                    if n == 3:
                        pe.wait_ge(kf_rdy, c * 3 + 3)
                    for t in range(TM):
                        ins = pe.transpose(dst[:, t * P:(t + 1) * P],
                                           KF[:, t, R * (n - 3):R * (n - 2), :].rearrange("p h f -> p (h f)"),
                                           ident[:, :])
                else:
                    half = (n - 7) % 2
                    if n < 9:
                        pe.wait_ge(qf_rdy, (c * 2 + half + 1) * 6)
                    else:
                        pe.wait_ge(q2_rdy, c * 2 + half + 1)
                    for j in range(2):
                        for t in range(TN):
                            ins = pe.transpose(dst[:, j * N + t * P:j * N + (t + 1) * P],
                                               QF[:, t, R * (half * 2 + j):R * (half * 2 + j + 1), :]
                                               .rearrange("p h f -> p (h f)"), ident[:, :])
                ins.then_inc(x_tfull, 1)

            def maxima(c, p, h, t):
                g, r = h // R, slice(32 * (h % R), 32 * (h % R) + 32)
                k = (c * H + h) * 2 + t
                if not (isinstance(c, int) and c == 0 and h == 0):
                    pe.wait_ge(mx_rdy, k - 1)
                pe.matmul(slot[1][:, t, :], QFT[r, g, t * P:(t + 1) * P], KFT[r, p, g, :],
                          start=True, stop=True).then_inc(mx_full, 1)

            def scores(b, p, h, j):
                g, r = h // R, slice(32 * (h % R), 32 * (h % R) + 32)
                if not (isinstance(b, int) and b == 0 and h == 0):
                    pe.wait_ge(e_rdy, (b * H + h - 1) * 2 + j + 1)
                for t in (2 * j, 2 * j + 1):
                    cols = slice(t % 2 * N, (t % 2 + 1) * N)
                    pe.matmul(slot[0][:, j, cols], KFT[r, p, g, t * P:(t + 1) * P], QFT2[r, g, :],
                              start=True, stop=False)
                    ins = pe.matmul(slot[0][:, j, cols], ident_bf[:, :], MBT[:, p, t, :], start=False, stop=True)
                ins.then_inc(e_full, 1)

            def product(b, p, h):
                pe.wait_ge(e_rdy, (b * H + h + 1) * 2)
                if h == 0:
                    pe.wait_ge(vx_rdy, b + 1)
                if h % 8 == 0:
                    wait(pe, xo_rdy, b * GP + h // 8)
                r, half = slice(32 * (h % R), 32 * (h % R) + 32), h // R % 2
                for t in range(TM):
                    ins = pe.matmul(ops[r, half, :], VX[:, p, t, h, :], W[:, h % 4, t, :],
                                    start=(t == 0), stop=(t == TM - 1))
                ins.then_inc(pv_head, 1)

            def turn(b, q):
                if q == 0:
                    wait(pe, xb_used, b * 3)
                pe.wait_ge(xo_rdy, b * GP + q + 1)
                for g in (0, 1):
                    for tt in range(TN):
                        ins = pe.matmul(bps[:, tt * 144 + (2 * q + g) * 36:tt * 144 + (2 * q + g + 1) * 36],
                                        OT[:, g, tt * P:(tt + 1) * P], sel[:, :], start=True, stop=True)
                ins.then_inc(xb_full, 1)

            def end_at(b, k):
                if k == 0:
                    turn(b, 1)
                if k == 1:
                    pe.wait_ge(xb_used, b * 3 + 1)
                    for tt in range(TN):
                        ins = pe.transpose(bps[:, tt * P:(tt + 1) * P], On[:, tt, :], ident[:, :])
                    ins.then_inc(xb_full, 1)
                if k == 2:
                    pe.wait_ge(xb_used, b * 3 + 2)
                    for tt in range(TN):
                        ins = pe.matmul(bps[:, tt * P:(tt + 1) * P], OnT[:, tt * P:(tt + 1) * P], wo_x[:, :],
                                        start=True, stop=True)
                    ins.then_inc(xb_full, 1)

            def body(b, p, nxt, nxt2):
                first = isinstance(b, int) and b == 0
                for h in range(H):
                    if h == 0:
                        pe.wait_ge(x_tact, x_acts(b))
                        pe.wait_ge(mbt_rdy, b + 1)
                    if h == 8:
                        pe.wait_ge(x_tact, x_acts(b) + (4 if nxt2 else 3 if nxt else 1))
                    for j in range(2):
                        scores(b, p, h, j)
                        if nxt:
                            maxima(b + 1, 1 - p, h, j)
                    if h:
                        product(b, p, h - 1)
                    elif not first:
                        product(b - 1, 1 - p, H - 1)
                    if h == 11:
                        turn(b, 0)
                    if not first and h in (2, 5, 9):
                        end_at(b - 1, (2, 5, 9).index(h))
                    for i in x_items(b, h, nxt, nxt2):
                        item(XItem(i, b, p))

            for i in range(9):
                item(XItem(i))
            pe.wait_ge(x_tact, 7)
            for h in range(H):
                for t in range(TN):
                    maxima(0, 0, h, t)
            for i in range(9, len(X_FIRST)):
                item(XItem(i))
            x_batches(pe, body)
            product(B - 1, 1, H - 1)
            for k in range(3):
                end_at(B - 1, k)

            ln_tensor(pe, XNf, 2)
            pe.wait_ge(kw_rdy, 2)
            pe.wait_ge(rt_const, 1)
            pe.matmul(tps[0][:, 0:E], ones[:, :], ksq[:, :], start=True, stop=True).then_inc(ks_full, 1)
            for t in range(NT):
                pe.wait_ge(xt_rdy, 8 + t // 4 + 1)
                ins = pe.matmul(tps[1][:, t * E:(t + 1) * E], xnTf[:, t * P:(t + 1) * P], kw[:, :], start=True, stop=True)
            ins.then_inc(lg_full, 1)
            pe.wait_ge(wt_rdy, 1)
            for t in range(NT):
                ins = pe.transpose(slot[t // 8][0:E, t // 4 % 2, t % 4 * P:(t % 4 + 1) * P], WT[:, t, :], ident[:, :])
                if t % 4 == 3:
                    ins.then_inc(wtt_full, 1)
            pe.wait_ge(rw_in, 16 * 5)
            for q in range(4):
                pe.wait_ge(wtt_rdy, q + 1)
                wait(pe, bo_used, q - 1)
                for t in range(4 * q, 4 * q + 4):
                    ins = pe.matmul(tps[q % 2][:, t % 4 * P:(t % 4 + 1) * P], WTT[0:E, t * P:(t + 1) * P], b2_sb[0:E, :],
                                    start=True, stop=True)
                ins.then_inc(bo_full, 1)
            pe.wait_ge(wtt_rdy, 4)
            pe.wait_ge(bo_used, 4)

            def hidden(i, j):
                p, tb = j // TB, j % TB
                if tb == 0:
                    pe.wait_ge(ew_in[p], i * 32 + 32)
                for c in range(FC):
                    k = (i * 2 * TB + j) * FC
                    if isinstance(i, int) and i == 0 and j == 0:
                        pass
                    else:
                        pe.wait_ge(h_rdy, k + c - FC + 1)
                    pe.matmul(slot[c // 2][:, c % 2, :], W1[:, p, c * P:(c + 1) * P], xnTf[:, tb * 512:(tb + 1) * 512],
                              start=True, stop=True).then_inc(h_full, 1)

            def outputs(i, j):
                p, tb = j // TB, j % TB
                k = i * 2 * TB + j
                pe.wait_ge(h_rdy, (k + 1) * FC)
                if not (isinstance(i, int) and i == 0 and j < 2):
                    pe.wait_ge(y_used, (k - 1) * 4)
                for tt in range(4):
                    for c in range(FC):
                        ins = pe.matmul(tps[j % 2][:, tt * P:(tt + 1) * P], HB[:, j % 2, c, tt * P:(tt + 1) * P],
                                        W2[:, p, c, :], start=(c == 0), stop=(c == FC - 1))
                ins.then_inc(y_full, 1)

            hidden(0, 0)
            J = 2 * TB
            for j in range(J):
                hidden(0, j + 1) if j + 1 < J else hidden(1, 0)
                outputs(0, j)
            with pe.Fori(1, E // 2 - 1) as i:
                for j in range(J):
                    hidden(i, j + 1) if j + 1 < J else hidden(i + 1, 0)
                    outputs(i, j)
            for j in range(J):
                if j + 1 < J:
                    hidden(E // 2 - 1, j + 1)
                outputs(E // 2 - 1, j)

        @block.vector
        def _(dve):
            ch = Chain(dve, dve_step)
            dve.memset(ops[:, :, :], 0.0).then_inc(b_used, 1)
            dve.wait_ge(x_in, 64)
            dve.wait_ge(cst, 1)
            ln_vector(dve, ch, XN, 0)
            dve.wait_ge(sq_rdy, 1)
            ch.step(dve.tensor_reduce(NRM, SQ.rearrange("p t (h d) -> p (t h) d", d=HD), AX, ALU.add))
            Q, K, V = (QKV[:, :, j * D:(j + 1) * D] for j in range(3))
            ch.step(dve.tensor_copy(HIq[:], Q))
            ch.step(dve.tensor_scalar(HIk[:], K, -2.0, None, ALU.mult))
            ch.step(dve.tensor_copy(VS[:], V))
            ch.sync()
            ch.step(dve.tensor_tensor(LOq[:], Q, HIq[:].bitcast(F32), ALU.subtract))
            ch.step(dve.scalar_tensor_tensor(out=LOk[:], in0=K, scalar=-2.0, in1=HIk[:].bitcast(F32),
                                             op0=ALU.mult, op1=ALU.subtract))
            ch.step(dve.tensor_copy(NH[:], NRM))
            ch.step(dve.tensor_scalar(A0, NRM, -1.0, 1.0, ALU.mult, ALU.add))
            ch.sync()
            ch.step(dve.tensor_tensor(NL[:], NRM, NH[:].bitcast(F32), ALU.subtract))
            ch.link(dve.tensor_scalar(A1, A0, 0.0, None, ALU.is_equal))
            ch.link(dve.tensor_tensor(A2, A0, A1, ALU.add))
            ch.step(dve.tensor_scalar(A1, A1, -1.0, 1.0, ALU.mult, ALU.add))
            ch.link(dve.reciprocal(NRM, A2))
            ch.link(dve.tensor_tensor(A1, A1, NRM, ALU.mult))
            qa, ka = slice(0, H), slice(H, 2 * H)
            ch.step(dve.memset(QG[:], 0.0))
            ch.step(dve.memset(KG[:], 0.0))
            ch.sync()
            ch.step(dve.tensor_copy(QG[:].bitcast(F32R)[:, :, :, 0], A1[:, :, qa]))
            ch.step(dve.tensor_scalar(QG[:, :, :, 3], A0[:, :, qa], 0.0, None, ALU.is_ge))
            ch.step(dve.tensor_scalar(QG[:, :, :, 4], A0[:, :, qa], 0.0, None, ALU.is_le))
            ch.step(dve.tensor_scalar(KG[:].bitcast(F32R)[:, :, :, 0], A1[:, :, ka], 2.0, None, ALU.mult))
            ch.step(dve.tensor_scalar(KG[:, :, :, 3], A0[:, :, ka], 0.0, BIG, ALU.is_le, ALU.mult))
            ch.step(dve.tensor_scalar(KG[:, :, :, 4], A0[:, :, ka], 0.0, BIG, ALU.is_ge, ALU.mult))
            ch.sync()
            ch.step(dve.tensor_copy(QG[:, :, :, 1], QG[:, :, :, 0]))
            ch.step(dve.tensor_tensor(QG[:, :, :, 2], A1[:, :, qa], QG[:, :, :, 0], ALU.subtract))
            ch.step(dve.scalar_tensor_tensor(out=KG[:, :, :, 1], in0=A1[:, :, ka], scalar=2.0, in1=KG[:, :, :, 0],
                                             op0=ALU.mult, op1=ALU.subtract))
            ch.step(dve.tensor_copy(KG[:, :, :, 2], KG[:, :, :, 0]))
            ch.sync()
            dve.sem_inc(s_prep, 1)

            def back_at(b, k):
                if k == 0:
                    ch.enter(b, 1)
                    dve.wait_ge(b_full, b * 4 + 2)
                    o = bps[:, 0:2 * 144].rearrange("p (a n) -> p a n", n=9)
                    ch.link(dve.reciprocal(rec[:].rearrange("p t h -> p (t h)"), o[:, :, 8]))
                    dve.tensor_tensor(On[:].rearrange("p t (h d) -> p (t h) d", d=HD), o[:, :, 0:8],
                                      rec[:].rearrange("p t h -> p (t h)").unsqueeze(2).broadcast_to([P, TN * H, HD]),
                                      ALU.mult).then_inc(b_used, 1)
                elif k == 1:
                    dve.wait_ge(b_full, b * 4 + 3)
                    dve.tensor_copy(OnT[:, :], bps[:, 0:N]).then_inc(b_used, 1)
                else:
                    dve.wait_ge(b_full, b * 4 + 4)
                    xb = X[:, bass.ts(b, TN), :]
                    dve.tensor_tensor(xb, bps[:, 0:N].rearrange("p (t d) -> p t d", t=TN), xb,
                                      ALU.add).then_inc(b_used, 1)
                    ch.leave(b)

            NHf = NH[:].bitcast(F32)

            def norm_features(b):
                bt = bass.ts(b, TN)
                wait(dve, s_tfull, b * STI)
                copies = [(UQ[:, :, :, 24], NHf[:, bt, 0:H]), (UQ[:, :, :, 25], NL[:, bt, 0:H]),
                          (UK[:, :, :, 26], NHf[:, bt, H:2 * H]), (UK[:, :, :, 27], NL[:, bt, H:2 * H])]
                for tt in range(TN):
                    copies.append((GQ[:, tt, :, 0:5], QG[:, bt][:, tt]))
                    copies += [(GK[:, tt, v, v::4, 0:5], KG[:, bt][:, tt, v::4, :]) for v in range(4)]
                for dst, src in copies:
                    dve.tensor_copy(dst, src).then_inc(s_norm, 1)

            def factor(n, h):
                dve.wait_ge(u_full, n + 1)
                wait(dve, u_used, n - 1)
                dve.tensor_scalar(gb[:, h % 2], slot[h % 2][:, 1, :], 2.0 / DENOM_MIN, None,
                                  ALU.min).then_inc(g_rdy, 1)

            def body(b, p, with_front, with_back, with_end):
                for h in range(H):
                    n = b * H + h
                    dve.wait_ge(g_rdy, n + 1)
                    dve.scalar_tensor_tensor(out=Y[:, p, h], in0=slot[h % 2][:, 0, :], scalar=0.0,
                                             in1=gb[:, h % 2], op0=ALU.max, op1=ALU.mult).then_inc(u_used, 1)
                    if h < H - 1 or with_front:
                        factor(n + 1, (h + 1) % 2)
                    dve.wait_ge(u_used, n + 1)
                    wait(dve, f_rdy, n - ZR + 1)
                    dve.scalar_tensor_tensor(out=Zr[:, h % ZR], in0=Y[:, p, h], scalar=2.0, in1=Y[:, p, h],
                                             op0=ALU.add, op1=ALU.mult).then_inc(z_rdy, 1)
                    if h == 2 and with_front:
                        norm_features(b + 1)
                    if with_end and h in (3, 7, 9):
                        back_at(b - 2, (h - 3) // 2 if h == 3 else (h - 5) // 2)

            def back(b, p):
                for e in (b - 1, b):
                    for k in range(3):
                        back_at(e, k)

            norm_features(0)
            factor(0, 0)
            batches(dve, lambda b, p: None, body, back)
            ch.end(B)

            dve.wait_ge(b_used, 3 * B + 1)
            ln_vector(dve, ch, XNx, 1)
            dve.wait_ge(wx_in, 16 * 8)
            for q in range(4):
                dve.wait_ge(qx_full, q + 1)
                dve.tensor_tensor(QX[:, 4 * q:4 * q + 4, :], tps[q % 2][:, :].rearrange("p (t d) -> p t d", d=D),
                                  bq_x[:, :].unsqueeze(1).broadcast_to([P, 4, D]), ALU.add).then_inc(qx_used, 1)
            dve.wait_ge(qx_used, 4)
            dve.wait_ge(xn_rdy, 2 * NT)
            ch.link(dve.tensor_copy(HIq[:], QX[:]))
            ch.step(dve.tensor_tensor(LOq[:], QX[:], HIq[:].bitcast(F32), ALU.subtract))
            ch.step(dve.tensor_tensor(X[:], X[:], bo_x[:, :].unsqueeze(1).broadcast_to([P, NT, D]), ALU.add))
            ch.sync()
            dve.sem_inc(q_prep, 1)
            dve.wait_ge(x_const, 1)

            def keys_values(it):
                n, c = it.n - 1, it.c
                wait(dve, x_tfull, it.k + 1)
                if n == 0:
                    wait(dve, kf_rdy, c * 3)
                    wait(dve, vx_rdy, c)
                src = it.bank[:, :].rearrange("p (t c) -> p t c", c=2 * D)
                dve.tensor_tensor(KV[:, 2 * n:2 * n + 2, :], src[:, :, 0:D],
                                  bkv_x[:, 0:D].unsqueeze(1).broadcast_to([P, 2, D]), ALU.add).then_inc(k_rdy, 1)
                dve.tensor_tensor(VST[:, 2 * n:2 * n + 2, :], src[:, :, D:2 * D],
                                  bkv_x[:, D:2 * D].unsqueeze(1).broadcast_to([P, 2, D]), ALU.add).then_inc(x_tdve, 1)

            def dcount(c, p):
                return 16 * (c // 2 + 1) if isinstance(c, int) else c * 8 + 8 * (2 - p)

            def mask_q(c, p):
                dve.wait_ge(m_in[p], dcount(c, p))
                dve.tensor_scalar(MB[:, p], M8[:, p], 1.0, BIG, ALU.subtract, ALU.mult).then_inc(mb_rdy, 1)

            def mask_k(c, p):
                dve.wait_ge(mt_in[p], dcount(c, p))
                dve.tensor_scalar(MBT[:, p], MT8[:, p], 1.0, BIG, ALU.subtract, ALU.mult).then_inc(mbt_rdy, 1)

            def maximum(c, p, h, t):
                k = (c * H + h) * 2 + t
                if not (isinstance(c, int) and c == 0 and h == 0):
                    dve.wait_ge(mx_rdy, k - 1)
                if h == 0 and t == 0:
                    dve.wait_ge(mb_rdy, c + 1)
                wait(dve, mx_full, k + 1, None if isinstance(k, int) else apart_v)
                dve.tensor_tensor_reduce(out=junk[:, t, :], in0=slot[1][:, t, :], in1=MB[:, p, t, :], scale=1.0,
                                         scalar=-3.0e38, op0=ALU.add, op1=ALU.max,
                                         accum_out=MX[:, t, h:h + 1]).then_inc(mx_rdy, 1)

            def shift(c, half):
                hs = slice(8 * half, 8 * half + 8)
                dve.wait_ge(mx_rdy, c * (2 * H) + H * (half + 1))
                dve.tensor_scalar(QF[:].bitcast(F32R)[:, :, hs, 24], MX[:, :, hs], -1.0, None,
                                  ALU.mult).then_inc(qmax_rdy, 1)
                dve.wait_ge(qmax_rdy, c * 2 + half + 1)
                dve.scalar_tensor_tensor(out=QF[:, :, hs, 25], in0=MX[:, :, hs], scalar=-1.0, in1=QF[:, :, hs, 24],
                                         op0=ALU.mult, op1=ALU.subtract).then_inc(q2_rdy, 1)

            def back_at(b, k):
                if k == 0:
                    dve.wait_ge(xb_full, b * 4 + 2)
                    o = bps[:, 0:2 * 144].rearrange("p (a n) -> p a n", n=9)
                    dve.reciprocal(rec[:].rearrange("p t h -> p (t h)"), o[:, :, 8]).then_inc(rec_rdy, 1)
                    dve.wait_ge(rec_rdy, b + 1)
                    dve.tensor_tensor(On[:].rearrange("p t (h d) -> p (t h) d", d=HD), o[:, :, 0:8],
                                      rec[:].rearrange("p t h -> p (t h)").unsqueeze(2).broadcast_to([P, TN * H, HD]),
                                      ALU.mult).then_inc(xb_used, 1)
                elif k == 1:
                    dve.wait_ge(xb_full, b * 4 + 3)
                    dve.tensor_copy(OnT[:, :], bps[:, 0:N]).then_inc(xb_used, 1)
                else:
                    dve.wait_ge(xb_full, b * 4 + 4)
                    xb = X[:, bass.ts(b, TN), :]
                    dve.tensor_tensor(xb, bps[:, 0:N].rearrange("p (t d) -> p t d", t=TN), xb,
                                      ALU.add).then_inc(xb_used, 1)

            def body(b, p, nxt, nxt2):
                first = isinstance(b, int) and b == 0
                if nxt:
                    if not first:
                        dve.wait_ge(pv_head, b * H)
                    dve.wait_ge(x_tdve, b * XD + X_D0)
                    dve.tensor_copy(VX[:, 1 - p, :, :, 0:8],
                                    VST[:].rearrange("p t (h d) -> p t h d", d=HD)).then_inc(vx_rdy, 1)
                for h in range(H):
                    if nxt:
                        for t in range(TN):
                            maximum(b + 1, 1 - p, h, t)
                        if h == 2:
                            mask_k(b + 1, 1 - p)
                        if h == 7:
                            shift(b + 1, 0)
                        if h == H - 1:
                            shift(b + 1, 1)
                    for i, (n, c, at) in enumerate(X_BODY):
                        if n in (1, 2) and nxt2 and at + 1 == h:
                            keys_values(XItem(i, b, p))
                    if nxt2 and h == 12:
                        mask_q(b + 2, p)
                    if not first and h in (3, 6, 10):
                        back_at(b - 1, (3, 6, 10).index(h))

            keys_values(XItem(1))
            keys_values(XItem(2))
            dve.wait_ge(x_tdve, 2)
            dve.tensor_copy(VX[:, 0, :, :, 0:8], VST[:].rearrange("p t (h d) -> p t h d", d=HD)).then_inc(vx_rdy, 1)
            mask_q(0, 0)
            for h in range(H):
                for t in range(TN):
                    maximum(0, 0, h, t)
                if h == 7:
                    shift(0, 0)
            shift(0, 1)
            for i, (n, c) in enumerate(X_FIRST):
                if c and n in (1, 2):
                    keys_values(XItem(i))
            mask_k(0, 0)
            mask_q(1, 1)
            x_batches(dve, body)
            for k in range(3):
                back_at(B - 1, k)

            dve.wait_ge(xb_used, 3 * B)
            ln_vector(dve, ch, XNf, 2)
            dve.wait_ge(rw_in, 16 * 5)
            dve.scalar_tensor_tensor(out=kw[:, :], in0=keysT[:, :], scalar=2.0, in1=rwT[:, :],
                                     op0=ALU.mult, op1=ALU.add).then_inc(kw_rdy, 1)
            dve.tensor_tensor(ksq[:, :], keysT[:, :], keysT[:, :], ALU.mult).then_inc(kw_rdy, 1)
            dve.wait_ge(ks_full, 1)
            ch.link(dve.tensor_tensor(lc[:, :], rb_b[:, :], tps[0][:, 0:E], ALU.subtract))
            dve.wait_ge(lg_full, 1)
            ch.link(dve.tensor_tensor(LG[:], tps[1][:, 0:NT * E].rearrange("p (t e) -> p t e", e=E),
                                      lc[:, :].unsqueeze(1).broadcast_to([P, NT, E]), ALU.add))
            for t in range(NT):
                ch.step(dve.max(TOP[:, t, :], LG[:, t, :]))
            ch.sync()
            for t in range(NT):
                ch.step(dve.max_index(TOPI[:, t, :], TOP[:, t, :], LG[:, t, :]))
            ch.step(dve.tensor_tensor(EX[:], LG[:], TOP[:, :, 0:1].broadcast_to([P, NT, E]), ALU.subtract))
            ch.sync()
            dve.sem_inc(ex_in, 1)
            ch.link(dve.tensor_copy(TOPF[:], TOPI[:]))
            dve.wait_ge(rt_const, 1)
            iota_b = iota_f[:, :].unsqueeze(1).broadcast_to([P, NT, E])
            for j in range(TOPK):
                dst = EQ if j else PICK
                ch.link(dve.tensor_tensor(dst[:], iota_b, TOPF[:, :, j:j + 1].broadcast_to([P, NT, E]), ALU.is_equal))
                if j:
                    ch.link(dve.tensor_tensor(PICK[:], PICK[:], EQ[:], ALU.add))
            dve.wait_ge(ex_rdy, 1)
            ch.link(dve.tensor_tensor(EX[:], EX[:], PICK[:], ALU.mult))
            ch.link(dve.tensor_reduce(SM[:, :], EX[:], AX, ALU.add))
            ch.link(dve.reciprocal(RS[:, :], SM[:, :]))
            dve.tensor_tensor(WT[:], EX[:], RS[:, :].unsqueeze(2).broadcast_to([P, NT, E]), ALU.mult).then_inc(wt_rdy, 1)
            dve.wait_ge(wt_rdy, 1)
            for q in range(4):
                dve.wait_ge(bo_full, q + 1)
                dve.wait_ge(xn_rdy, 3 * NT)
                xq = X[:, 4 * q:4 * q + 4, :]
                dve.tensor_tensor(xq, tps[q % 2][:, :].rearrange("p (t d) -> p t d", d=D), xq, ALU.add).then_inc(bo_used, 1)
            dve.wait_ge(bo_used, 4)

            def add(e, k, tb, prior):
                dve.wait_ge(y_full, k + 1)
                if prior:
                    dve.wait_ge(y_used, (k - TB) * 4 + 4)
                for tt in range(4):
                    t = tb * 4 + tt
                    dve.scalar_tensor_tensor(out=X[:, t, :], in0=tps[tb % 2][:, tt * P:(tt + 1) * P],
                                             scalar=WT[:, t, bass.ts(e, 1)], in1=X[:, t, :],
                                             op0=ALU.mult, op1=ALU.add).then_inc(y_used, 1)

            for tb in range(TB):
                add(0, tb, tb, False)
            with dve.Fori(1, E) as e:
                for tb in range(TB):
                    add(e, e * TB + tb, tb, True)


_IN = {"x": "x", "wqT_s": "L0_attn_Wq", "wkT_s": "L0_attn_Wk", "wvT_s": "L0_attn_Wv", "woT_s": "L0_attn_Wo",
       "wqT_x": "L0_xattn_Wq", "wkT_x": "L0_xattn_Wk", "wvT_x": "L0_xattn_Wv", "woT_x": "L0_xattn_Wo",
       "bq_x": "L0_xattn_bq", "bk_x": "L0_xattn_bk", "bv_x": "L0_xattn_bv", "bo_x": "L0_xattn_bo",
       "ctx": "ctx_1024", "keysT": "L0_ffn_keys", "rwT": "L0_ffn_rw", "rb": "L0_ffn_rb",
       "w1T": "L0_ffn_w1", "b1": "L0_ffn_b1", "w2T": "L0_ffn_w2", "b2": "L0_ffn_b2"}


def lay_out(inputs):
    a = {k: np.asarray(inputs[v]) for k, v in _IN.items()}
    for k in a:
        if "T_" in k or k.endswith("T"):
            a[k] = a[k].swapaxes(-1, -2)
    mask = np.asarray(inputs["mask_Bx1xSxS2_bf1"]).reshape(B, N, M).view(np.uint8)
    a["b1"] = a["b1"].reshape(E, FC, P).transpose(2, 0, 1)
    a["mask"], a["maskT"] = mask, mask.transpose(0, 2, 1)
    return {k: np.ascontiguousarray(v) for k, v in a.items()}


def kernel(**inputs):
    import concourse.bacc as bacc
    from concourse.bass_utils import run_bass_kernel_spmd
    nc = bacc.Bacc("TRN2", target_bir_lowering=False, num_devices=1)
    arrays = lay_out(inputs)
    a = {k: nc.dram_tensor(k, v.shape, mybir.dt.from_np(v.dtype), kind="ExternalInput").ap()
         for k, v in arrays.items()}
    out = nc.dram_tensor("out", (B, N, D), F32, kind="ExternalOutput").ap()
    decoder_block(nc, a, out)
    r = run_bass_kernel_spmd(nc, [arrays], core_ids=[0])
    return r.results[0]["out"]
```

```python
from contextlib import ExitStack

import numpy as np
import concourse.bass as bass
from concourse import mybir

F32 = mybir.dt.float32
F32R = mybir.dt.float32r
BF16 = mybir.dt.bfloat16
U8 = mybir.dt.uint8
ALU = mybir.AluOpType
ACT = mybir.ActivationFunctionType
AX = mybir.AxisListType.X

P = 128
B, N, D = 8, 256, 128
M = 512
H, HD = 16, 8
TN, TM = N // P, M // P
NT = B * TN
R, G = 4, H // 4
GP = G // 2
E, TOPK, FF = 16, 4, 512
FC = FF // P
EPS = 1e-5
BIG = float(2.0 ** 100)
DENOM_MIN = 1e-6
SCALE = 1.0 / float(np.sqrt(HD))

WEIGHTS = ("wqT_s", "wkT_s", "wvT_s", "woT_s")
WEIGHTS_X = ("wqT_x", "wkT_x", "wvT_x", "woT_x", "bq_x", "bk_x", "bv_x", "bo_x")


def wait(eng, sem, value, apart=None):
    if not isinstance(value, int) or value > 0:
        eng.wait_ge(sem, value)
        if apart is not None:
            eng.sem_inc(apart, 1)


class Chain:

    def __init__(self, eng, sem, apart=None):
        self.apart = apart
        self.eng, self.sem, self.base, self.n, self.loop0, self.per = eng, sem, 0, 0, None, None

    def step(self, ins):
        ins.then_inc(self.sem, 1)
        self.n += 1

    def sync(self):
        wait(self.eng, self.sem, self.base + self.n, None if isinstance(self.base, int) else self.apart)

    def link(self, ins):
        self.step(ins)
        self.sync()

    def enter(self, b, per):
        if self.loop0 is None:
            self.loop0 = self.base + self.n
        self.base, self.n, self.per = b * per + self.loop0, 0, per

    def leave(self, b):
        assert self.n == self.per, (self.n, self.per)
        self.base, self.n = (b + 1) * self.per + self.loop0, 0

    def end(self, batches):
        self.base, self.n, self.loop0 = self.loop0 + batches * self.per, 0, None


def decoder_block(nc, a, out):
    with ExitStack() as ctx:
        def sb(name, shape, dt=F32):
            return ctx.enter_context(nc.sbuf_tensor(name, shape, dt))

        def sem(name):
            return ctx.enter_context(nc.semaphore(name))

        X = sb("X", [P, NT, D])
        ident = sb("ident", [P, P])
        ident_bf = sb("ident_bf", [P, P], BF16)
        ident_r = sb("ident_r", [P, P], F32R)
        halves = sb("halves", [P, 2])
        sel = sb("sel", [P, R * 9])
        bn_st = sb("bn_st", [P, NT, 6])
        bn_mv = sb("bn_mv", [P, NT, 2])
        ln_sd = sb("ln_sd", [P, NT])
        ln_rs = sb("ln_rs", [P, NT])
        eps_c = sb("eps_c", [P, 1])
        rec = sb("rec", [P, TN, H])
        On = sb("On", [P, TN, D])
        OnT = sb("OnT", [P, N])
        OT = sb("OT", [P, 2, N])
        HIq = sb("HIq", [P, NT, D], F32R)
        LOq = sb("LOq", [P, NT, D])

        def arena(phase):
            top = ctx.enter_context(ExitStack())
            return top, lambda name, shape, dt=F32: top.enter_context(
                nc.sbuf_tensor(f"{phase}_{name}", [P] + list(shape), dt))

        def ps(name, shape):
            return ctx.enter_context(nc.psum_tensor(name, [P] + shape, F32))

        slot = [ps(f"slot{i}", [2, 512]) for i in range(2)]
        tps = [ps(f"tps{i}", [512]) for i in range(2)]
        ops = ps("ops", [2, N])
        bps = ps("bps", [512])

        apart_g, apart_a, apart_s, apart_v = sem("apart_g"), sem("apart_a"), sem("apart_s"), sem("apart_v")
        x_in, w_in, cst = sem("x_in"), sem("w_in"), sem("cst")
        dve_step, act_step, pool_step = sem("dve_step"), sem("act_step"), sem("pool_step")
        ln_var, ln_dev, xn_rdy = sem("ln_var"), sem("ln_dev"), sem("xn_rdy")
        xt_full, xt_rdy = sem("xt_full"), sem("xt_rdy")
        qkv_full, qkv_even, qkv_odd = sem("qkv_full"), sem("qkv_even"), sem("qkv_odd")
        hi_rdy, lo_rdy = sem("hi_rdy"), sem("lo_rdy")
        sq_rdy, s_prep, s_const = sem("sq_rdy"), sem("s_prep"), sem("s_const")
        uk_rdy, uq_rdy = sem("uk_rdy"), sem("uq_rdy")
        s_norm, s_tfull, s_tused, s_vf = sem("s_norm"), sem("s_tfull"), sem("s_tused"), sem("s_vf")
        u_full, u_used = sem("u_full"), sem("u_used")
        g_rdy, y_rdy, z_rdy = sem("g_rdy"), sem("y_rdy"), sem("z_rdy")
        root_rdy, f_rdy, w_rdy = sem("root_rdy"), sem("f_rdy"), sem("w_rdy")
        ln_rdy = sem("ln_rdy")
        o_full, o_rdy = sem("o_full"), sem("o_rdy")
        b_full, b_used, s_done = sem("b_full"), sem("b_used"), sem("s_done")

        def ln_vector(dve, ch, XN, k, between=lambda: None):
            for t in range(NT):
                ch.step(dve.bn_stats(bn_st[:, t, :], X[:, t, :]))
            ch.sync()
            for t in range(NT):
                i = dve.bn_aggr(bn_mv[:, t, :], bn_st[:, t, :])
                if t < NT - 1:
                    ch.step(i)
            i.then_inc(ln_var, 1)
            ch.sync()
            between()
            dve.wait_ge(ln_dev, k + 1)
            ch.link(dve.reciprocal(ln_rs[:, :], ln_sd[:, :]))
            for t in range(NT):
                dve.tensor_scalar(XN[:, t, :], X[:, t, :], bn_mv[:, t, 0:1], ln_rs[:, t:t + 1],
                                  ALU.subtract, ALU.mult).then_inc(xn_rdy, 1)

        def ln_scalar(act, k):
            act.wait_ge(ln_var, k + 1)
            act.activation(ln_sd[:, :], bn_mv[:, :, 1], ACT.Sqrt, bias=eps_c[:, 0:1]).then_inc(ln_dev, 1)

        def ln_tensor(pe, XN, k):
            for t in range(NT):
                pe.wait_ge(xn_rdy, k * NT + t + 1)
                i = pe.transpose(slot[t // 8][:, t // 4 % 2, t % 4 * P:(t % 4 + 1) * P], XN[:, t, :], ident[:, :])
                if t % 4 == 3:
                    i.then_inc(xt_full, 1)

        def ln_copy(act, xnT, k):
            for q in range(4):
                act.wait_ge(xt_full, 4 * k + q + 1)
                act.copy(xnT[:, 512 * q:512 * q + 512], slot[q // 2][:, q % 2, :]).then_inc(xt_rdy, 1)

        topS, sS = arena("S")
        Y = sS("Y", [2, H, 2 * N])
        prepS = Y[:, :, :, :].rearrange("p a h n -> p (a h n)")
        at = [0]

        def over_Y(shape, names, **sizes):
            n = int(np.prod(shape))
            at[0] += n
            v = prepS[:, at[0] - n:at[0]]
            return v.rearrange(f"p ({names}) -> p {names}", **sizes) if sizes else v

        XN = over_Y([NT, D], "t d", t=NT)
        xnT = over_Y([NT * P], "")
        QKV = over_Y([NT, 3 * D], "t d", t=NT)
        SQ = over_Y([NT, 2 * D], "t d", t=NT)
        NRM = over_Y([NT, 2 * H], "t h", t=NT)
        A0 = over_Y([NT, 2 * H], "t h", t=NT)
        A1 = over_Y([NT, 2 * H], "t h", t=NT)
        A2 = over_Y([NT, 2 * H], "t h", t=NT)
        ZR = 8
        VW = 16
        Zr = sS("Zr", [ZR, 2 * N])
        gb = sS("gb", [2, 2 * N])
        VS = sS("VS", [NT, D])
        HIk, LOk = sS("HIk", [NT, D], F32R), sS("LOk", [NT, D])
        NH, NL = sS("NH", [NT, 2 * H], F32R), sS("NL", [NT, 2 * H])
        QG, KG = sS("QG", [NT, H, 5]), sS("KG", [NT, H, 5])
        UQ, UK = sS("UQ", [TN, H, 32], F32R), sS("UK", [TN, H, 32], F32R)
        GQ, GK = sS("GQ", [TN, H, 8], F32R), sS("GK", [TN, 4, H, 8], F32R)
        UQT, UKT = sS("UQT", [2, G, N], F32R), sS("UKT", [2, G, N], F32R)
        GQT, GKT = sS("GQT", [2, 2, N], F32R), sS("GKT", [2, 4, N], F32R)
        VF = sS("VF", [2, TN, H, VW])
        wqkv = sS("wqkv", [3 * D])
        wo_s = sS("wo_s", [D])
        S_ITEMS = ("UK01", "UK23", "UQ01", "GQ", "GK01", "GK23", "UQ23")
        STI = len(S_ITEMS)

        topS.close()

        topX, sX = arena("X")
        XNx = sX("XN", [NT, D])
        xnTx = sX("xnT", [NT * P])
        QX = sX("QX", [NT, D])
        wq_x, wkv_x, wo_x = sX("wq", [D]), sX("wkv", [2 * D]), sX("wo", [D])
        bq_x, bkv_x, bo_x = sX("bq", [D]), sX("bkv", [2 * D]), sX("bo", [D])
        CT = sX("CT", [2, TM, D])
        ctxT = sX("ctxT", [M])
        KV = sX("KV", [TM, D])
        QF, KF = sX("QF", [TN, H, 32], F32R), sX("KF", [TM, H, 32], F32R)
        QFT, QFT2 = sX("QFT", [2, G, N], F32R), sX("QFT2", [2, G, N], F32R)
        KFT = sX("KFT", [2, G, M], F32R)
        VX = sX("VX", [2, TM, H, 32])
        M8, MT8 = sX("M8", [2, TN, M], U8), sX("MT8", [2, TM, N], U8)
        MB, MBT = sX("MB", [2, TN, M], BF16), sX("MBT", [2, TM, N], BF16)
        MX = sX("MX", [TN, H])
        W = sX("W", [4, TM, N])
        VST = sX("VST", [TM, D])
        junk = sX("junk", [TN, M], BF16)
        topX.close()
        qx_full, qx_used, q_prep = sem("qx_full"), sem("qx_used"), sem("q_prep")
        wx_in, x_const = sem("wx_in"), sem("x_const")
        c_in, m_in, mt_in = ([sem(f"{n}_in{i}") for i in range(2)] for n in ("c", "m", "mt"))
        x_tfull, x_tact, x_tdve = sem("x_tfull"), sem("x_tact"), sem("x_tdve")
        k_rdy, kf_rdy, qf_rdy, q2_rdy = sem("k_rdy"), sem("kf_rdy"), sem("qf_rdy"), sem("q2_rdy")
        qmax_rdy, rec_rdy = sem("qmax_rdy"), sem("rec_rdy")
        mb_rdy, mbt_rdy, vx_rdy = sem("mb_rdy"), sem("mbt_rdy"), sem("vx_rdy")
        mx_full, mx_rdy, e_full, e_rdy = sem("mx_full"), sem("mx_rdy"), sem("e_full"), sem("e_rdy")
        pv_head, xo_rdy, xb_full, xb_used = sem("pv_head"), sem("xo_rdy"), sem("xb_full"), sem("xb_used")

        topF, sF = arena("F")
        XNf, xnTf = sF("XN", [NT, D]), sF("xnT", [NT * P])
        keysT, rwT, rb_b = sF("keysT", [E]), sF("rwT", [E]), sF("rb", [E])
        kw, ksq, lc = sF("kw", [E]), sF("ksq", [E]), sF("lc", [E])
        ones = sF("ones", [P])
        iota_i, iota_f = sF("iota_i", [E], mybir.dt.int32), sF("iota_f", [E])
        LG, EX, PICK, EQ = (sF(n, [NT, E]) for n in ("LG", "EX", "PICK", "EQ"))
        TOP, TOPI, TOPF = sF("TOP", [NT, 8]), sF("TOPI", [NT, 8], mybir.dt.uint32), sF("TOPF", [NT, 8])
        SM, RS = sF("SM", [NT]), sF("RS", [NT])
        WT, WTT = sF("WT", [NT, E]), sF("WTT", [512])
        B1, b2_sb = sF("B1", [E, FC]), sF("b2", [D])
        W1, W2 = sF("W1", [2, FF]), sF("W2", [2, FC, D])
        W1h, W1l = sF("W1h", [2, FF], F32R), sF("W1l", [2, FF], F32R)
        xTh, xTl = sF("xTh", [NT * P], F32R), sF("xTl", [NT * P], F32R)
        HB = sF("HB", [2, FC, 512])
        TB = NT // 4
        topF.close()
        rw_in, rt_const, kw_rdy, ks_full, lg_full = sem("rw_in"), sem("rt_const"), sem("kw_rdy"), sem("ks_full"), sem("lg_full")
        ex_in, ex_rdy, wt_rdy = sem("ex_in"), sem("ex_rdy"), sem("wt_rdy")
        wtt_full, wtt_rdy, bo_full, bo_used = sem("wtt_full"), sem("wtt_rdy"), sem("bo_full"), sem("bo_used")
        ew_in, ew2_in = ([sem(f"{n}_in{i}") for i in range(2)] for n in ("ew", "ew2"))
        w1_parts, w1_high, xt_high, xt_parts = sem("w1_parts"), sem("w1_high"), sem("xt_high"), sem("xt_parts")
        h_full, h_rdy, y_full, y_used = sem("h_full"), sem("h_rdy"), sem("y_full"), sem("y_used")
        out_done = sem("out_done")

        X_FIRST = [(n, 0) for n in range(9)] + [(0, 1), (1, 1), (2, 1), (9, 0), (3, 1), (4, 1), (7, 1), (5, 1)]
        X_FIRST_AT = (0, 2, 4, 9, 10, 11, 13, 14)
        X_BODY = ((10, 0, 1), (6, 1, 2), (0, 2, 3), (1, 2, 5), (8, 1, 6), (2, 2, 7), (9, 1, 10),
                  (3, 2, 12), (4, 2, 13), (7, 2, 14), (5, 2, 15))
        XI = len(X_BODY)

        def by(items):
            d = sum(it[0] in (1, 2) for it in items)
            return len(items) - d, d

        def x_before(b):
            return X_FIRST + [(n, c + i) for i in range(b) for n, c, _ in X_BODY if c + i < B]

        (X_A0, X_D0), (XA, XD) = by(X_FIRST), by(X_BODY)

        def x_acts(b):
            return by(x_before(b))[0] if isinstance(b, int) else b * XA + X_A0

        class XItem:

            def __init__(self, i, b=None, p=0):
                if b is None:
                    (self.n, self.c), before, base = X_FIRST[i], X_FIRST[:i], (0, 0, 0)
                elif isinstance(b, int):
                    self.n, self.c = X_BODY[i][0], b + X_BODY[i][1]
                    before = x_before(b) + [x for x in X_BODY[:i] if x[1] + b < B]
                    base = (0, 0, 0)
                else:
                    self.n, self.c = X_BODY[i][0], b + X_BODY[i][1]
                    before = X_FIRST + list(X_BODY) * p + list(X_BODY[:i])
                    base = tuple((b - p) * x for x in (XI, XA, XD))
                self.p = self.c % 2 if b is None else (p + X_BODY[i][1]) % 2
                self.bank = tps[len(before) % 2]
                last, (acts, dves) = before[-2:], by(before)
                self.k, self.act = base[0] + len(before), base[1] + acts
                if len(last) < 2:
                    self.bank_free = (x_tact, 0)
                elif last[0][0] in (1, 2):
                    self.bank_free = (x_tdve, base[2] + dves - (last[1][0] in (1, 2)))
                else:
                    self.bank_free = (x_tact, base[1] + acts - (last[1][0] not in (1, 2)))

        def x_items(b, h, nxt, nxt2):
            return [i for i, (n, c, at) in enumerate(X_BODY) if at == h and (c == 0 or (nxt, nxt2)[c - 1])]

        def x_batches(eng, body):
            body(0, 0, True, True)
            with eng.Fori(0, 2) as i:
                for k in (1, 2):
                    body(i * 2 + k, k % 2, True, True)
            body(B - 3, 1, True, True)
            body(B - 2, 0, True, False)
            body(B - 1, 1, False, False)

        block = ctx.enter_context(nc.Block())

        @block.sync
        def _(sp):
            x_t = a["x"].rearrange("b (t p) d -> p (b t) d", p=P)
            for q in range(4):
                sp.dma_start(X[:, 4 * q:4 * q + 4, :], x_t[:, 4 * q:4 * q + 4, :]).then_inc(x_in, 16)
            for j, n in enumerate(WEIGHTS[:3]):
                sp.dma_start(wqkv[:, j * D:(j + 1) * D], a[n]).then_inc(w_in, 16)
            sp.dma_start(wo_s[:, :], a["woT_s"]).then_inc(w_in, 16)
            sp.wait_ge(o_full, GP * (B - 1))
            sp.dma_start(wq_x[:, :], a["wqT_x"]).then_inc(wx_in, 16)
            sp.dma_start(wkv_x[:, 0:D], a["wkT_x"]).then_inc(wx_in, 16)
            sp.dma_start(wkv_x[:, D:2 * D], a["wvT_x"]).then_inc(wx_in, 16)
            sp.dma_start(wo_x[:, :], a["woT_x"]).then_inc(wx_in, 16)
            for dst, n in ((bq_x[:, :], "bq_x"), (bkv_x[:, 0:D], "bk_x"), (bkv_x[:, D:2 * D], "bv_x"),
                           (bo_x[:, :], "bo_x")):
                sp.dma_start(dst, a[n].partition_broadcast(P)).then_inc(wx_in, 16)
            ctx_t = a["ctx"].rearrange("b (t p) d -> b p t d", p=P)
            m_t = a["mask"].rearrange("b (t p) m -> b p t m", p=P)
            mT_t = a["maskT"].rearrange("b (t p) q -> b p t q", p=P)

            for c in range(2):
                sp.dma_start(CT[:, c], ctx_t[c]).then_inc(c_in[c], 16)
            sp.wait_ge(b_used, 3 * B + 1)

            def load(c, p):
                if isinstance(c, int):
                    done = {0: 0, 1: 0, 2: 1, 3: X_FIRST.index((0, 1)) + 1}[c]
                else:
                    done = c * XI + (len(X_FIRST) + 3 - 4 * XI)
                if not (isinstance(c, int) and c < 2):
                    wait(sp, x_tfull, done, apart_s)
                    sp.dma_start(CT[:, p], ctx_t[c]).then_inc(c_in[p], 16)
                wait(sp, mb_rdy, c - 1, apart_s)
                sp.dma_start(M8[:, p], m_t[c]).then_inc(m_in[p], 16)
                wait(sp, mbt_rdy, c - 1, apart_s)
                sp.dma_start(MT8[:, p], mT_t[c]).then_inc(mt_in[p], 16)

            for c in range(4):
                load(c, c % 2)
            with sp.Fori(2, B // 2) as i:
                for p in range(2):
                    load(i * 2 + p, p)
            sp.wait_ge(xb_used, 3 * B)
            for dst, src in ((keysT[:, :], a["keysT"]), (rwT[:, :], a["rwT"]), (rb_b[:, :], a["rb"].partition_broadcast(P)),
                             (B1[:], a["b1"]), (b2_sb[0:E, :], a["b2"])):
                sp.dma_start(dst, src).then_inc(rw_in, 16)
            w2_t = a["w2T"].rearrange("e (c p) d -> e p c d", p=P)

            def load_expert(e, p):
                wait(sp, y_full, (e - 1) * TB, apart_s)
                sp.dma_start(W1[:, p], a["w1T"][e]).then_inc(ew_in[p], 16)
                sp.dma_start(W2[:, p], w2_t[e]).then_inc(ew2_in[p], 16)

            for e in range(2):
                load_expert(e, e)
            with sp.Fori(1, E // 2) as i:
                for p in range(2):
                    load_expert(i * 2 + p, p)
            o_t = out.rearrange("b (t p) d -> p (b t) d", p=P)
            for tb in range(TB):
                sp.wait_ge(y_used, (E - 1) * NT + 4 * (tb + 1))
                sp.dma_start(o_t[:, 4 * tb:4 * tb + 4, :], X[:, 4 * tb:4 * tb + 4, :]).then_inc(out_done, 16)
            sp.wait_ge(out_done, 16 * TB)

        def batches(eng, front, body, back):
            front(0, 0)
            body(0, 0, True, False, False)
            body(1, 1, True, True, False)
            with eng.Fori(1, B // 2 - 1) as i:
                for k in range(2):
                    body(i * 2 + k, k, True, True, True)
            body(B - 2, 0, True, True, True)
            body(B - 1, 1, False, True, True)
            back(B - 1, 1)

        @block.gpsimd
        def _(g):
            ch = Chain(g, pool_step, apart_g)
            ch.step(g.memset(eps_c[:, :], EPS))
            ch.link(g.memset(ident[:, :], 0.0))
            ch.link(g.affine_select(out=ident[:, :], in_=ident[:, :], compare_op=ALU.not_equal, fill=1.0,
                                    base=0, pattern=[[-1, P]], channel_multiplier=1))
            ch.step(g.tensor_copy(ident_bf[:, :], ident[:, :]))
            ch.step(g.tensor_copy(ident_r[:, :], ident[:, :]))
            ch.sync()
            for k in range(4):
                ch.link(g.memset(halves[32 * k:32 * k + 32, k % 2:k % 2 + 1], 1.0))
                ch.link(g.memset(halves[32 * k:32 * k + 32, 1 - k % 2:2 - k % 2], 0.0))
            for r in range(R):
                ch.step(g.tensor_copy(sel[:, 9 * r:9 * r + 9], ident[:, 32 * r:32 * r + 9]))
            for t in (UQ, UK, GQ, GK, VF):
                ch.step(g.memset(t[:].bitcast(F32), 0.0))
            ch.sync()
            ch.step(g.memset(UQ[:].bitcast(F32)[:, :, :, 26:28], 1.0))
            ch.step(g.memset(UK[:].bitcast(F32)[:, :, :, 24:26], 1.0))
            for p in range(2):
                ch.step(g.memset(VF[:, p, :, :, 8:9], 1.0))
            ch.sync()
            g.sem_inc(cst, 1)

            def per_head(x, bt, tt):
                return x[:, bt, :][:, tt].rearrange("p (h d) -> p h d", d=HD)

            HQ, HK = HIq[:].bitcast(F32), HIk[:].bitcast(F32)

            def key_tiles(b):
                wait(g, s_tfull, b * STI - (STI - 2), apart_g)
                for tt in range(TN):
                    for c, src in ((0, HK), (8, LOk), (16, HK)):
                        g.tensor_copy(UK[:, tt, :, c:c + 8], per_head(src, bass.ts(b, TN), tt)).then_inc(uk_rdy, 1)

            def query_tiles(b):
                wait(g, s_tfull, b * STI, apart_g)
                for tt in range(TN):
                    for c, src in ((0, HQ), (8, HQ), (16, LOq)):
                        g.tensor_copy(UQ[:, tt, :, c:c + 8], per_head(src, bass.ts(b, TN), tt)).then_inc(uq_rdy, 1)

            def value_tiles(b, p):
                wait(g, o_full, (b - 1) * GP, apart_g)
                for tt in range(TN):
                    g.tensor_copy(VF[:, p, tt, :, 0:8], per_head(VS, bass.ts(b, TN), tt)).then_inc(s_vf, 1)

            def front(b, p):
                key_tiles(b)
                query_tiles(b)
                value_tiles(b, p)
                key_tiles(b + 1)

            def body(b, p, with_front, with_back, with_end):
                for h in range(H):
                    if with_front and h == 4:
                        query_tiles(b + 1)
                    if with_front and h == 12:
                        if not (isinstance(b, int) and b + 2 >= B):
                            key_tiles(b + 2)
                        value_tiles(b + 1, 1 - p)
                    g.wait_ge(root_rdy, b * H + h + 1)
                    g.tensor_tensor(Y[:, p, h], Y[:, p, h], Zr[:, h % ZR], ALU.add).then_inc(f_rdy, 1)

            g.wait_ge(hi_rdy, 3)
            g.tensor_tensor(LOq[:], QKV[:, :, 0:D], HQ, ALU.subtract).then_inc(lo_rdy, 1)
            g.wait_ge(lo_rdy, 1)
            g.wait_ge(s_prep, 1)
            batches(g, front, body, lambda b, p: None)

            g.wait_ge(b_used, 3 * B + 1)
            for t in (QF, KF, VX):
                ch.step(g.memset(t[:].bitcast(F32), 0.0))
            ch.sync()
            ch.step(g.memset(KF[:].bitcast(F32)[:, :, :, 24:26], 1.0))
            for p in range(2):
                ch.step(g.memset(VX[:, p, :, :, 8:9], 1.0))
            ch.sync()
            g.sem_inc(x_const, 1)

            def heads(x):
                return x.rearrange("p t (h d) -> p t h d", d=HD)

            def q_features(c, half):
                cols, hs = slice(64 * half, 64 * half + 64), slice(8 * half, 8 * half + 8)
                for tt in range(TN):
                    for f, src in ((0, HQ), (8, HQ), (16, LOq)):
                        g.tensor_copy(QF[:, tt, hs, f:f + 8],
                                      src[:, bass.ts(c, TN)][:, tt, cols].rearrange("p (h d) -> p h d", d=HD)
                                      ).then_inc(qf_rdy, 1)

            def k_features(c):
                wait(g, k_rdy, c * 2 + 2, apart_g)
                g.tensor_copy(KF[:, :, :, 0:8], heads(KV[:, :, :])).then_inc(kf_rdy, 1)
                wait(g, kf_rdy, c * 3 + 1, apart_g)
                g.tensor_copy(KF[:, :, :, 16:24], KF[:, :, :, 0:8]).then_inc(kf_rdy, 1)
                g.tensor_tensor(KF[:, :, :, 8:16], heads(KV[:, :, :]), KF[:].bitcast(F32)[:, :, :, 0:8], ALU.subtract).then_inc(kf_rdy, 1)

            k_features(0)
            g.wait_ge(q_prep, 1)
            q_features(0, 0)
            q_features(0, 1)
            g.wait_ge(x_tfull, X_FIRST.index((6, 0)) + 1)
            k_features(1)
            g.wait_ge(x_tfull, X_FIRST.index((9, 0)) + 1)
            q_features(1, 0)

            def body(b, p, nxt, nxt2):
                if nxt:
                    wait(g, x_tfull, XItem(0, b).k + 1, apart_g)
                    q_features(b + 1, 1)
                if nxt2:
                    wait(g, x_tfull, XItem(1, b).k + 1, apart_g)
                    k_features(b + 2)
                    wait(g, x_tfull, XItem(6, b).k + 1, apart_g)
                    q_features(b + 2, 0)

            x_batches(g, body)

            g.wait_ge(xb_used, 3 * B)
            ch.step(g.memset(ones[:, :], 1.0))
            ch.link(g.iota(iota_i[:, :], pattern=[[1, E]], base=0, channel_multiplier=0))
            ch.link(g.tensor_copy(iota_f[:, :], iota_i[:, :]))
            g.sem_inc(rt_const, 1)

        @block.scalar
        def _(act):
            act.wait_ge(cst, 1)
            ln_scalar(act, 0)
            ln_copy(act, xnT, 0)
            for t in range(0, NT, 2):
                act.wait_ge(qkv_full, t + 1)
                act.copy(QKV[:, t, :], tps[0][:, 0:3 * D]).then_inc(qkv_even, 1)
                if t % 4 == 2:
                    q = slice(t - 2, t + 2)
                    act.wait_ge(qkv_odd, t // 2 + 1)
                    act.wait_ge(qkv_even, t // 2 + 1)
                    act.activation(SQ[:, q, :], QKV[:, q, 0:2 * D], ACT.Square).then_inc(sq_rdy, 1)
            act.copy(HIq[:], QKV[:, :, 0:D]).then_inc(hi_rdy, 1)
            act.activation(HIk[:], QKV[:, :, D:2 * D], ACT.Copy, scale=-2.0).then_inc(hi_rdy, 1)
            act.copy(VS[:], QKV[:, :, 2 * D:3 * D]).then_inc(hi_rdy, 1)

            def masked(dst, src, sem):
                for v in range(2):
                    ins = act.activation(dst[:, v], src, ACT.Copy, scale=halves[:, v:v + 1])
                ins.then_inc(sem, 1)

            def front_copy(b, p, n):
                act.wait_ge(s_tfull, b * STI + n + 1)
                if n == 0:
                    wait(act, u_full, (b - 1) * H)
                src = tps[n % 2]
                two = src[:, :].rearrange("p (g n) -> p g n", g=2)
                if S_ITEMS[n] in ("UK01", "UK23"):
                    act.copy(UKT[:, p, 2 * n:2 * n + 2, :], two).then_inc(s_tused, 1)
                elif S_ITEMS[n] in ("UQ01", "UQ23"):
                    g = 0 if S_ITEMS[n] == "UQ01" else 2
                    masked(UQT[:, :, g:g + 2, :], two, s_tused)
                elif S_ITEMS[n] == "GQ":
                    masked(GQT[:, p], src[:, 0:N], s_tused)
                else:
                    v = 0 if S_ITEMS[n] == "GK01" else 2
                    act.copy(GKT[:, p, v:v + 2, :], two).then_inc(s_tused, 1)

            def front(b, p):
                for n in range(STI - 1):
                    front_copy(b, p, n)

            def body(b, p, with_front, with_back, with_end):
                for h in range(H):
                    if h % 8 == 4 and (h > 4 or with_back):
                        act.preload_act_table_set("sqrt_and_others")
                    act.wait_ge(z_rdy, b * H + h + 1)
                    act.activation(Zr[:, h % ZR], Zr[:, h % ZR], ACT.Sqrt).then_inc(root_rdy, 1)
                    if h == 1:
                        front_copy(b, p, STI - 1)
                    if h == 3 and with_back:
                        weights(b - 1, 1 - p, 1, lambda k: None)
                        out_copy(b - 1, 0)
                    if with_front and h in (7, 8, 10, 11):
                        front_copy(b + 1, 1 - p, (7, 8, 10, 11).index(h))
                    if h == 11:
                        weights(b, p, 0, lambda k: (with_back and k == 1 and out_copy(b - 1, 1),
                                                    with_front and k in (0, 2) and front_copy(b + 1, 1 - p, 4 + k // 2)))

            def weights(b, p, half, between):
                act.preload_act_table_set("natural_log_exp_and_others")
                for j in range(2):
                    g = 2 * half + j
                    v = Y[:, p, R * g:R * g + R, :]
                    act.wait_ge(f_rdy, b * H + R * g + R)
                    act.activation(v, v, ACT.Ln, bias=1.0).then_inc(ln_rdy, 1)
                    between(2 * j)
                    act.wait_ge(ln_rdy, b * G + g + 1)
                    act.activation(v, v, ACT.Exp, scale=-1.0).then_inc(w_rdy, 1)
                    between(2 * j + 1)

            def out_copy(b, q):
                act.wait_ge(o_full, b * GP + q + 1)
                wait(act, b_full, b * 4 + 1 if q else b * 4 - 2)
                act.copy(OT[:, :, :], ops[:, :, :]).then_inc(o_rdy, 1)

            def back(b, p):
                weights(b, p, 1, lambda k: None)
                for q in range(GP):
                    out_copy(b, q)

            batches(act, front, body, back)


            def copy_item(it):
                n, p, src = it.n, it.p, it.bank[:, :]
                wait(act, x_tfull, it.k + 1, apart_a)
                if n < 7:
                    act.copy(ctxT[:, :] if n == 0 else KFT[:, p, n - 3, :], src).then_inc(x_tact, 1)
                else:
                    g = (n - 7) % 2 * 2
                    masked((QFT if n < 9 else QFT2)[:, :, g:g + 2, :], src.rearrange("p (g n) -> p g n", g=2), x_tact)

            def out_copy(b, q):
                wait(act, pv_head, b * H + 8 * (q + 1), apart_a)
                wait(act, xb_full, b * 4 + 1 if q else b * 4 - 2, apart_a)
                act.copy(OT[:, :, :], ops[:, :, :]).then_inc(xo_rdy, 1)

            def body(b, p, nxt, nxt2):
                for h in range(H):
                    for j in range(2):
                        k = (b * H + h) * 2 + j
                        wait(act, e_full, k + 1, apart_a)
                        if not (isinstance(b, int) and b == 0 and h < 4):
                            wait(act, pv_head, b * H + h - 3, apart_a)
                        act.activation(W[:, h % 4, 2 * j:2 * j + 2, :].rearrange("p t n -> p (t n)"), slot[0][:, j, :],
                                       ACT.Exp, scale=SCALE).then_inc(e_rdy, 1)
                    if h == 0 and not (isinstance(b, int) and b == 0):
                        out_copy(b - 1, 1)
                    if h == 8:
                        out_copy(b, 0)
                    for i in x_items(b, h, nxt, nxt2):
                        if X_BODY[i][0] not in (1, 2):
                            copy_item(XItem(i, b, p))

            ln_scalar(act, 1)
            for i, (n, c) in enumerate(X_FIRST):
                if i == 3:
                    ln_copy(act, xnTx, 1)
                if n not in (1, 2):
                    copy_item(XItem(i))
            x_batches(act, body)
            out_copy(B - 1, 1)

            ln_scalar(act, 2)
            for q in range(4):
                cols = slice(512 * q, 512 * q + 512)
                act.wait_ge(xt_full, 8 + q + 1)
                act.copy(xnTf[:, cols], slot[q // 2][:, q % 2, :]).then_inc(xt_rdy, 1)
                act.copy(xTh[:, cols], slot[q // 2][:, q % 2, :]).then_inc(xt_high, 1)
            act.wait_ge(ex_in, 1)
            act.activation(EX[:], EX[:], ACT.Exp).then_inc(ex_rdy, 1)
            act.preload_act_table_set("gelu_and_others")

            def weights_copy(q):
                act.wait_ge(wtt_full, q + 1)
                if q:
                    act.wait_ge(bo_full, q)
                act.copy(WTT[0:E, :], bps[0:E, :]).then_inc(wtt_rdy, 1)

            def gelus(e, tb):
                k = e * TB + tb
                for c in range(FC):
                    if c == 0:
                        wait(act, y_full, k - 1)
                    wait(act, h_full, k * FC + c + 1, apart_a)
                    act.activation(HB[:, tb % 2, c, :], slot[c // 2][:, c % 2, :], ACT.Gelu,
                                   bias=B1[:, bass.ts(e, 1), c]).then_inc(h_rdy, 1)

            for tb in range(TB):
                gelus(0, tb)
            for tb in range(TB):
                gelus(1, tb)
                weights_copy(tb)
            with act.Fori(2, E) as e:
                for tb in range(TB):
                    gelus(e, tb)

        @block.tensor
        def _(pe):
            pe.wait_ge(cst, 1)
            ln_tensor(pe, XN, 0)
            pe.wait_ge(w_in, 64)
            for t in range(NT):
                pe.wait_ge(xt_rdy, t // 4 + 1)
                if t >= 2:
                    pe.wait_ge((qkv_even, qkv_odd)[t % 2], t // 2)
                pe.matmul(tps[t % 2][:, 0:3 * D], xnT[:, t * P:(t + 1) * P], wqkv[:, :],
                          start=True, stop=True).then_inc(qkv_full, 1)
            pe.wait_ge(qkv_even, NT // 2)
            pe.wait_ge(qkv_odd, NT // 2)

            def front_item(b, p, n):
                if n == 0:
                    pe.wait_ge(s_norm, (b + 1) * 14)
                if n in (0, 2):
                    pe.wait_ge((uk_rdy, uq_rdy)[n // 2], (b + 1) * 3 * TN)
                wait(pe, s_tused, b * STI + max(n - 1, 0))
                dst, what = tps[n % 2], S_ITEMS[n]
                if what[0] == "U":
                    src = UK if what[1] == "K" else UQ
                    parts = [(j, tt, src[:, tt, R * (int(what[2]) + j):R * (int(what[2]) + j + 1), :])
                             for j in range(2) for tt in range(TN)]
                elif what == "GQ":
                    parts = [(0, tt, GQ[:, tt]) for tt in range(TN)]
                else:
                    parts = [(j, tt, GK[:, tt, int(what[2]) + j]) for j in range(2) for tt in range(TN)]
                for j, tt, src in parts:
                    ins = pe.transpose(dst.bitcast(F32R)[:, j * N + tt * P:j * N + (tt + 1) * P],
                                       src.rearrange("p h f -> p (h f)"), ident_r[:, :])
                ins.then_inc(s_tfull, 1)

            END_AT = (2, 6, 10)
            FRONT_AT = (7, 8, 11, 12, 13)
            BACK_AT = (3, 4, 5, 6, 12, 13, 14, 15)

            def front(b, p):
                for n in range(STI - 2):
                    front_item(b, p, n)

            def scores(b, p, h):
                g, r, v = h // R, h % R // 2 * 64, h % 2
                rg, vg = h // 8 * 64, h // R % 2
                if h in (0, 2, 8):
                    pe.wait_ge(s_tused, b * STI + STI - {0: 2, 2: 1, 8: 0}[h])
                wait(pe, u_used, b * H + h - 1)
                for kt in range(TN):
                    pe.matmul(slot[h % 2][:, 0, kt * N:(kt + 1) * N], UKT[r:r + 64, p, g, kt * P:(kt + 1) * P],
                              UQT[r:r + 64, v, g, :], start=True, stop=True)
                for kt in range(TN):
                    ins = pe.matmul(slot[h % 2][:, 1, kt * N:(kt + 1) * N],
                                    GKT[rg:rg + 64, p, h % 4, kt * P:(kt + 1) * P], GQT[rg:rg + 64, p, vg, :],
                                    start=True, stop=True)
                ins.then_inc(u_full, 1)

            def product(b, p, j):
                g = j // 2
                if j == 0:
                    pe.wait_ge(s_vf, (b + 1) * TN)
                if j % 2 == 0:
                    pe.wait_ge(w_rdy, b * G + g + 1)
                if j % 4 == 0:
                    wait(pe, o_rdy, b * GP + j // 4)
                for r in (j % 2 * 2, j % 2 * 2 + 1):
                    h = R * g + r
                    for kt in range(TN):
                        ins = pe.matmul(ops[32 * r:32 * r + VW, g % 2, :], VF[:, p, kt, h, :],
                                        Y[:, p, h, kt * N:(kt + 1) * N], start=(kt == 0), stop=(kt == TN - 1))
                if j % 4 == 3:
                    ins.then_inc(o_full, 1)

            def turn(b, q):
                if q == 0:
                    pe.wait_ge(b_used, b * 3 + 1)
                pe.wait_ge(o_rdy, b * GP + q + 1)
                for g in (0, 1):
                    for tt in range(TN):
                        ins = pe.matmul(bps[:, tt * 144 + (2 * q + g) * 36:tt * 144 + (2 * q + g + 1) * 36],
                                        OT[:, g, tt * P:(tt + 1) * P], sel[:, :], start=True, stop=True)
                ins.then_inc(b_full, 1)

            def back_at(b, p, k):
                product(b, p, k)
                if k == 5:
                    turn(b, 0)

            def end_at(b, k):
                if k == 0:
                    turn(b, 1)
                if k == 1:
                    pe.wait_ge(b_used, b * 3 + 2)
                    for tt in range(TN):
                        ins = pe.transpose(bps[:, tt * P:(tt + 1) * P], On[:, tt, :], ident[:, :])
                    ins.then_inc(b_full, 1)
                if k == 2:
                    pe.wait_ge(b_used, b * 3 + 3)
                    for tt in range(TN):
                        ins = pe.matmul(bps[:, tt * P:(tt + 1) * P], OnT[:, tt * P:(tt + 1) * P], wo_s[:, :],
                                        start=True, stop=True)
                    ins.then_inc(b_full, 1)

            def body(b, p, with_front, with_back, with_end):
                for h in range(H):
                    scores(b, p, h)
                    if h < 2:
                        front_item(b, p, STI - 2 + h)
                    if with_end and h in END_AT:
                        end_at(b - 2, END_AT.index(h))
                    for k, at in enumerate(BACK_AT):
                        if with_back and h == at:
                            back_at(b - 1, 1 - p, k)
                    if with_front:
                        for n in range(STI - 2):
                            if h == FRONT_AT[n]:
                                front_item(b + 1, 1 - p, n)

            def back(b, p):
                for k in range(3):
                    end_at(b - 1, k)
                for k in range(2 * G):
                    back_at(b, p, k)
                for k in range(3):
                    end_at(b, k)

            batches(pe, front, body, back)

            def data_count(c, p, once):
                return 16 * once * (c // 2 + 1) if isinstance(c, int) else c * (8 * once) + 8 * once * (2 - p)

            def item(it):
                n, p, c, dst = it.n, it.p, it.c, it.bank
                wait(pe, *it.bank_free)
                if n == 0:
                    pe.wait_ge(c_in[p], data_count(c, p, 1))
                    for t in range(TM):
                        ins = pe.transpose(dst[:, t * P:(t + 1) * P], CT[:, p, t, :], ident[:, :])
                elif n < 3:
                    if n == 1:
                        wait(pe, x_tact, it.act)
                    for j in range(2):
                        t = (n - 1) * 2 + j
                        ins = pe.matmul(dst[:, j * N:(j + 1) * N], ctxT[:, t * P:(t + 1) * P], wkv_x[:, :],
                                        start=True, stop=True)
                elif n < 7:
                    if n == 3:
                        pe.wait_ge(kf_rdy, c * 3 + 3)
                    for t in range(TM):
                        ins = pe.transpose(dst.bitcast(F32R)[:, t * P:(t + 1) * P],
                                           KF[:, t, R * (n - 3):R * (n - 2), :].rearrange("p h f -> p (h f)"),
                                           ident_r[:, :])
                else:
                    half = (n - 7) % 2
                    if n < 9:
                        pe.wait_ge(qf_rdy, (c * 2 + half + 1) * 6)
                    else:
                        pe.wait_ge(q2_rdy, c * 2 + half + 1)
                    for j in range(2):
                        for t in range(TN):
                            ins = pe.transpose(dst.bitcast(F32R)[:, j * N + t * P:j * N + (t + 1) * P],
                                               QF[:, t, R * (half * 2 + j):R * (half * 2 + j + 1), :]
                                               .rearrange("p h f -> p (h f)"), ident_r[:, :])
                ins.then_inc(x_tfull, 1)

            def maxima(c, p, h, t):
                g, r, v = h // R, slice(h % R // 2 * 64, h % R // 2 * 64 + 64), h % 2
                k = (c * H + h) * 2 + t
                if not (isinstance(c, int) and c == 0 and h == 0):
                    pe.wait_ge(mx_rdy, k - 1)
                pe.matmul(slot[1][:, t, :], QFT[r, v, g, t * P:(t + 1) * P], KFT[r, p, g, :],
                          start=True, stop=True).then_inc(mx_full, 1)

            def scores(b, p, h, j):
                g, r, v = h // R, slice(h % R // 2 * 64, h % R // 2 * 64 + 64), h % 2
                if not (isinstance(b, int) and b == 0 and h == 0):
                    pe.wait_ge(e_rdy, (b * H + h - 1) * 2 + j + 1)
                for t in (2 * j, 2 * j + 1):
                    cols = slice(t % 2 * N, (t % 2 + 1) * N)
                    pe.matmul(slot[0][:, j, cols], KFT[r, p, g, t * P:(t + 1) * P], QFT2[r, v, g, :],
                              start=True, stop=False)
                    ins = pe.matmul(slot[0][:, j, cols], ident_bf[:, :], MBT[:, p, t, :], start=False, stop=True)
                ins.then_inc(e_full, 1)

            def product(b, p, h):
                pe.wait_ge(e_rdy, (b * H + h + 1) * 2)
                if h == 0:
                    pe.wait_ge(vx_rdy, b + 1)
                if h % 8 == 0:
                    wait(pe, xo_rdy, b * GP + h // 8)
                r, half = slice(32 * (h % R), 32 * (h % R) + 32), h // R % 2
                for t in range(TM):
                    ins = pe.matmul(ops[r, half, :], VX[:, p, t, h, :], W[:, h % 4, t, :],
                                    start=(t == 0), stop=(t == TM - 1))
                ins.then_inc(pv_head, 1)

            def turn(b, q):
                if q == 0:
                    wait(pe, xb_used, b * 3)
                pe.wait_ge(xo_rdy, b * GP + q + 1)
                for g in (0, 1):
                    for tt in range(TN):
                        ins = pe.matmul(bps[:, tt * 144 + (2 * q + g) * 36:tt * 144 + (2 * q + g + 1) * 36],
                                        OT[:, g, tt * P:(tt + 1) * P], sel[:, :], start=True, stop=True)
                ins.then_inc(xb_full, 1)

            def end_at(b, k):
                if k == 0:
                    turn(b, 1)
                if k == 1:
                    pe.wait_ge(xb_used, b * 3 + 1)
                    for tt in range(TN):
                        ins = pe.transpose(bps[:, tt * P:(tt + 1) * P], On[:, tt, :], ident[:, :])
                    ins.then_inc(xb_full, 1)
                if k == 2:
                    pe.wait_ge(xb_used, b * 3 + 2)
                    for tt in range(TN):
                        ins = pe.matmul(bps[:, tt * P:(tt + 1) * P], OnT[:, tt * P:(tt + 1) * P], wo_x[:, :],
                                        start=True, stop=True)
                    ins.then_inc(xb_full, 1)

            def body(b, p, nxt, nxt2):
                first = isinstance(b, int) and b == 0
                for h in range(H):
                    if h == 0:
                        pe.wait_ge(x_tact, x_acts(b))
                        pe.wait_ge(mbt_rdy, b + 1)
                    if h == 8:
                        pe.wait_ge(x_tact, x_acts(b) + (4 if nxt2 else 3 if nxt else 1))
                    for j in range(2):
                        scores(b, p, h, j)
                        if nxt:
                            maxima(b + 1, 1 - p, h, j)
                    if h:
                        product(b, p, h - 1)
                    elif not first:
                        product(b - 1, 1 - p, H - 1)
                    if h == 11:
                        turn(b, 0)
                    if not first and h in (2, 5, 9):
                        end_at(b - 1, (2, 5, 9).index(h))
                    for i in x_items(b, h, nxt, nxt2):
                        item(XItem(i, b, p))

            pe.wait_ge(wx_in, 16 * 8)
            for i in range(3):
                item(XItem(i))
            ln_tensor(pe, XNx, 1)
            pe.wait_ge(x_tdve, 2)
            for q in range(4):
                pe.wait_ge(xt_rdy, 4 + q + 1)
                wait(pe, qx_used, q - 1)
                for t in range(4):
                    ins = pe.matmul(tps[q % 2][:, t * P:(t + 1) * P], xnTx[:, (4 * q + t) * P:(4 * q + t + 1) * P],
                                    wq_x[:, :], start=True, stop=True)
                ins.then_inc(qx_full, 1)
            pe.wait_ge(qx_used, 4)
            for i in range(3, 9):
                item(XItem(i))
            pe.wait_ge(x_tact, 7)
            for h in range(H):
                for t in range(TN):
                    maxima(0, 0, h, t)
                if h in X_FIRST_AT:
                    item(XItem(9 + X_FIRST_AT.index(h)))
            x_batches(pe, body)
            product(B - 1, 1, H - 1)
            for k in range(3):
                end_at(B - 1, k)

            ln_tensor(pe, XNf, 2)
            pe.wait_ge(kw_rdy, 2)
            pe.wait_ge(rt_const, 1)
            pe.matmul(bps[:, 0:E], ones[:, :], ksq[:, :], start=True, stop=True).then_inc(ks_full, 1)
            logits = ops[:, :, :].rearrange("p a n -> p (a n)")
            for t in range(NT):
                pe.wait_ge(xt_rdy, 8 + t // 4 + 1)
                ins = pe.matmul(logits[:, t * E:(t + 1) * E], xnTf[:, t * P:(t + 1) * P], kw[:, :], start=True, stop=True)
            ins.then_inc(lg_full, 1)

            def weights_turn(q):
                pe.wait_ge(wt_rdy, 1)
                wait(pe, wtt_rdy, q)
                for t in range(4 * q, 4 * q + 4):
                    ins = pe.transpose(bps[0:E, t % 4 * P:(t % 4 + 1) * P], WT[:, t, :], ident[:, :])
                ins.then_inc(wtt_full, 1)

            def biases(q):
                pe.wait_ge(rw_in, 16 * 5)
                pe.wait_ge(wtt_rdy, q + 1)
                wait(pe, bo_used, q)
                for t in range(4 * q, 4 * q + 4):
                    ins = pe.matmul(logits[:, t % 4 * P:(t % 4 + 1) * P], WTT[0:E, t % 4 * P:(t % 4 + 1) * P],
                                    b2_sb[0:E, :], start=True, stop=True)
                ins.then_inc(bo_full, 1)

            def hidden(i, j):
                p, tb = j // TB, j % TB
                if tb == 0:
                    pe.wait_ge(w1_parts, i * 2 + (p + 1))
                if isinstance(i, int) and i == 0 and p == 0:
                    pe.wait_ge(xt_parts, tb + 1)
                cols = slice(tb * 512, (tb + 1) * 512)
                for c in range(FC):
                    k = (i * 2 * TB + j) * FC
                    if isinstance(i, int) and i == 0 and j == 0:
                        pe.wait_ge(xt_high, c + 1)
                    else:
                        pe.wait_ge(h_rdy, k + c - FC + 1)
                    for w, x in ((W1h, xTh), (W1h, xTl), (W1l, xTh)):
                        ins = pe.matmul(slot[c // 2][:, c % 2, :], w[:, p, c * P:(c + 1) * P], x[:, cols],
                                        start=(w is W1h and x is xTh), stop=(w is W1l))
                    ins.then_inc(h_full, 1)

            def outputs(i, j):
                p, tb = j // TB, j % TB
                k = i * 2 * TB + j
                if tb == 0:
                    pe.wait_ge(ew2_in[p], i * 16 + 16)
                pe.wait_ge(h_rdy, (k + 1) * FC)
                if not (isinstance(i, int) and i == 0 and j < 2):
                    pe.wait_ge(y_used, (k - 1) * 4)
                for tt in range(4):
                    for c in range(FC):
                        ins = pe.matmul(tps[j % 2][:, tt * P:(tt + 1) * P], HB[:, j % 2, c, tt * P:(tt + 1) * P],
                                        W2[:, p, c, :], start=(c == 0), stop=(c == FC - 1))
                ins.then_inc(y_full, 1)

            hidden(0, 0)
            J = 2 * TB
            for j in range(J):
                hidden(0, j + 1) if j + 1 < J else hidden(1, 0)
                if j >= TB:
                    weights_turn(j - TB)
                outputs(0, j)
                if j >= TB:
                    biases(j - TB)
            with pe.Fori(1, E // 2 - 1) as i:
                for j in range(J):
                    hidden(i, j + 1) if j + 1 < J else hidden(i + 1, 0)
                    outputs(i, j)
            for j in range(J):
                if j + 1 < J:
                    hidden(E // 2 - 1, j + 1)
                outputs(E // 2 - 1, j)

        @block.vector
        def _(dve):
            ch = Chain(dve, dve_step)
            dve.memset(ops[:, :, :], 0.0).then_inc(b_used, 1)
            dve.wait_ge(x_in, 64)
            dve.wait_ge(cst, 1)
            ln_vector(dve, ch, XN, 0)
            Q, K = (QKV[:, :, j * D:(j + 1) * D] for j in range(2))

            def norms(q):
                dve.wait_ge(sq_rdy, q + 1)
                tiles = slice(4 * q, 4 * q + 4)
                ch.step(dve.tensor_reduce(NRM[:, tiles, :].rearrange("p t h -> p (t h)"),
                                          SQ[:, tiles, :].rearrange("p t (h d) -> p (t h) d", d=HD), AX, ALU.add))

            for t in range(1, NT, 2):
                dve.wait_ge(qkv_full, t + 1)
                dve.tensor_copy(QKV[:, t, :], tps[1][:, 0:3 * D]).then_inc(qkv_odd, 1)
                if t % 4 == 1 and t >= 5:
                    norms(t // 4 - 1)
            norms(3)
            ch.sync()
            ch.step(dve.tensor_copy(NH[:], NRM))
            ch.step(dve.tensor_scalar(A0, NRM, -1.0, 1.0, ALU.mult, ALU.add))
            dve.wait_ge(hi_rdy, 2)
            ch.step(dve.scalar_tensor_tensor(out=LOk[:], in0=K, scalar=-2.0, in1=HIk[:].bitcast(F32),
                                             op0=ALU.mult, op1=ALU.subtract))
            ch.sync()
            ch.step(dve.tensor_tensor(NL[:], NRM, NH[:].bitcast(F32), ALU.subtract))
            ch.link(dve.tensor_scalar(A1, A0, 0.0, None, ALU.is_equal))
            ch.link(dve.tensor_tensor(A2, A0, A1, ALU.add))
            ch.step(dve.tensor_scalar(A1, A1, -1.0, 1.0, ALU.mult, ALU.add))
            ch.link(dve.reciprocal(NRM, A2))
            ch.link(dve.tensor_tensor(A1, A1, NRM, ALU.mult))
            qa, ka = slice(0, H), slice(H, 2 * H)
            ch.step(dve.tensor_copy(QG[:].bitcast(F32R)[:, :, :, 0], A1[:, :, qa]))
            ch.step(dve.tensor_scalar(QG[:, :, :, 3], A0[:, :, qa], 0.0, None, ALU.is_ge))
            ch.step(dve.tensor_scalar(QG[:, :, :, 4], A0[:, :, qa], 0.0, None, ALU.is_le))
            ch.step(dve.tensor_scalar(KG[:].bitcast(F32R)[:, :, :, 0], A1[:, :, ka], 2.0, None, ALU.mult))
            ch.step(dve.tensor_scalar(KG[:, :, :, 3], A0[:, :, ka], 0.0, BIG, ALU.is_le, ALU.mult))
            ch.step(dve.tensor_scalar(KG[:, :, :, 4], A0[:, :, ka], 0.0, BIG, ALU.is_ge, ALU.mult))
            ch.sync()
            ch.step(dve.tensor_copy(QG[:, :, :, 1], QG[:, :, :, 0]))
            ch.step(dve.tensor_tensor(QG[:, :, :, 2], A1[:, :, qa], QG[:, :, :, 0], ALU.subtract))
            ch.step(dve.scalar_tensor_tensor(out=KG[:, :, :, 1], in0=A1[:, :, ka], scalar=2.0, in1=KG[:, :, :, 0],
                                             op0=ALU.mult, op1=ALU.subtract))
            ch.step(dve.tensor_copy(KG[:, :, :, 2], KG[:, :, :, 0]))
            ch.sync()
            dve.sem_inc(s_prep, 1)

            def back_at(b, k):
                if k == 0:
                    ch.enter(b, 1)
                    dve.wait_ge(b_full, b * 4 + 2)
                    o = bps[:, 0:2 * 144].rearrange("p (a n) -> p a n", n=9)
                    ch.link(dve.reciprocal(rec[:].rearrange("p t h -> p (t h)"), o[:, :, 8]))
                    dve.tensor_tensor(On[:].rearrange("p t (h d) -> p (t h) d", d=HD), o[:, :, 0:8],
                                      rec[:].rearrange("p t h -> p (t h)").unsqueeze(2).broadcast_to([P, TN * H, HD]),
                                      ALU.mult).then_inc(b_used, 1)
                elif k == 1:
                    dve.wait_ge(b_full, b * 4 + 3)
                    dve.tensor_copy(OnT[:, :], bps[:, 0:N]).then_inc(b_used, 1)
                else:
                    dve.wait_ge(b_full, b * 4 + 4)
                    xb = X[:, bass.ts(b, TN), :]
                    dve.tensor_tensor(xb, bps[:, 0:N].rearrange("p (t d) -> p t d", t=TN), xb,
                                      ALU.add).then_inc(b_used, 1)
                    ch.leave(b)

            NHf = NH[:].bitcast(F32)

            def norm_features(b):
                bt = bass.ts(b, TN)
                wait(dve, s_tfull, b * STI)
                copies = [(UQ[:, :, :, 24], NHf[:, bt, 0:H]), (UQ[:, :, :, 25], NL[:, bt, 0:H]),
                          (UK[:, :, :, 26], NHf[:, bt, H:2 * H]), (UK[:, :, :, 27], NL[:, bt, H:2 * H])]
                for tt in range(TN):
                    copies.append((GQ[:, tt, :, 0:5], QG[:, bt][:, tt]))
                    copies += [(GK[:, tt, v, v::4, 0:5], KG[:, bt][:, tt, v::4, :]) for v in range(4)]
                for dst, src in copies:
                    dve.tensor_copy(dst, src).then_inc(s_norm, 1)

            def factor(n, h):
                dve.wait_ge(u_full, n + 1)
                wait(dve, u_used, n - 1)
                dve.tensor_scalar(gb[:, h % 2], slot[h % 2][:, 1, :], 2.0 / DENOM_MIN, None,
                                  ALU.min).then_inc(g_rdy, 1)

            def body(b, p, with_front, with_back, with_end):
                for h in range(H):
                    n = b * H + h
                    dve.wait_ge(g_rdy, n + 1)
                    dve.scalar_tensor_tensor(out=Y[:, p, h], in0=slot[h % 2][:, 0, :], scalar=0.0,
                                             in1=gb[:, h % 2], op0=ALU.max, op1=ALU.mult).then_inc(u_used, 1)
                    if h < H - 1 or with_front:
                        factor(n + 1, (h + 1) % 2)
                    dve.wait_ge(u_used, n + 1)
                    wait(dve, f_rdy, n - ZR + 1)
                    dve.scalar_tensor_tensor(out=Zr[:, h % ZR], in0=Y[:, p, h], scalar=2.0, in1=Y[:, p, h],
                                             op0=ALU.add, op1=ALU.mult).then_inc(z_rdy, 1)
                    if h == 2 and with_front:
                        norm_features(b + 1)
                    if with_end and h in (3, 7, 11):
                        back_at(b - 2, (h - 3) // 4)

            def back(b, p):
                for e in (b - 1, b):
                    for k in range(3):
                        back_at(e, k)

            norm_features(0)
            factor(0, 0)
            batches(dve, lambda b, p: None, body, back)
            ch.end(B)

            dve.wait_ge(b_used, 3 * B + 1)
            def keys_values(it):
                n, c = it.n - 1, it.c
                wait(dve, x_tfull, it.k + 1)
                if n == 0:
                    wait(dve, kf_rdy, c * 3)
                    wait(dve, vx_rdy, c)
                src = it.bank[:, :].rearrange("p (t c) -> p t c", c=2 * D)
                dve.tensor_tensor(KV[:, 2 * n:2 * n + 2, :], src[:, :, 0:D],
                                  bkv_x[:, 0:D].unsqueeze(1).broadcast_to([P, 2, D]), ALU.add).then_inc(k_rdy, 1)
                dve.tensor_tensor(VST[:, 2 * n:2 * n + 2, :], src[:, :, D:2 * D],
                                  bkv_x[:, D:2 * D].unsqueeze(1).broadcast_to([P, 2, D]), ALU.add).then_inc(x_tdve, 1)

            def dcount(c, p):
                return 16 * (c // 2 + 1) if isinstance(c, int) else c * 8 + 8 * (2 - p)

            def mask_q(c, p):
                dve.wait_ge(m_in[p], dcount(c, p))
                dve.tensor_scalar(MB[:, p], M8[:, p], 1.0, BIG, ALU.subtract, ALU.mult).then_inc(mb_rdy, 1)

            def mask_k(c, p):
                dve.wait_ge(mt_in[p], dcount(c, p))
                dve.tensor_scalar(MBT[:, p], MT8[:, p], 1.0, BIG, ALU.subtract, ALU.mult).then_inc(mbt_rdy, 1)

            def maximum(c, p, h, t):
                k = (c * H + h) * 2 + t
                if not (isinstance(c, int) and c == 0 and h == 0):
                    dve.wait_ge(mx_rdy, k - 1)
                if h == 0 and t == 0:
                    dve.wait_ge(mb_rdy, c + 1)
                wait(dve, mx_full, k + 1, None if isinstance(k, int) else apart_v)
                dve.tensor_tensor_reduce(out=junk[:, t, :], in0=slot[1][:, t, :], in1=MB[:, p, t, :], scale=1.0,
                                         scalar=-3.0e38, op0=ALU.add, op1=ALU.max,
                                         accum_out=MX[:, t, h:h + 1]).then_inc(mx_rdy, 1)

            def shift(c, half):
                hs = slice(8 * half, 8 * half + 8)
                dve.wait_ge(mx_rdy, c * (2 * H) + H * (half + 1))
                dve.tensor_scalar(QF[:, :, hs, 24], MX[:, :, hs], -1.0, None,
                                  ALU.mult).then_inc(qmax_rdy, 1)
                dve.wait_ge(qmax_rdy, c * 2 + half + 1)
                dve.scalar_tensor_tensor(out=QF[:, :, hs, 25], in0=MX[:, :, hs], scalar=-1.0, in1=QF[:].bitcast(F32)[:, :, hs, 24],
                                         op0=ALU.mult, op1=ALU.subtract).then_inc(q2_rdy, 1)

            def back_at(b, k):
                if k == 0:
                    dve.wait_ge(xb_full, b * 4 + 2)
                    o = bps[:, 0:2 * 144].rearrange("p (a n) -> p a n", n=9)
                    dve.reciprocal(rec[:].rearrange("p t h -> p (t h)"), o[:, :, 8]).then_inc(rec_rdy, 1)
                    dve.wait_ge(rec_rdy, b + 1)
                    dve.tensor_tensor(On[:].rearrange("p t (h d) -> p (t h) d", d=HD), o[:, :, 0:8],
                                      rec[:].rearrange("p t h -> p (t h)").unsqueeze(2).broadcast_to([P, TN * H, HD]),
                                      ALU.mult).then_inc(xb_used, 1)
                elif k == 1:
                    dve.wait_ge(xb_full, b * 4 + 3)
                    dve.tensor_copy(OnT[:, :], bps[:, 0:N]).then_inc(xb_used, 1)
                else:
                    dve.wait_ge(xb_full, b * 4 + 4)
                    xb = X[:, bass.ts(b, TN), :]
                    dve.tensor_tensor(xb, bps[:, 0:N].rearrange("p (t d) -> p t d", t=TN), xb,
                                      ALU.add).then_inc(xb_used, 1)

            def body(b, p, nxt, nxt2):
                first = isinstance(b, int) and b == 0
                if nxt:
                    if not first:
                        dve.wait_ge(pv_head, b * H)
                    dve.wait_ge(x_tdve, b * XD + X_D0)
                    dve.tensor_copy(VX[:, 1 - p, :, :, 0:8],
                                    VST[:].rearrange("p t (h d) -> p t h d", d=HD)).then_inc(vx_rdy, 1)
                for h in range(H):
                    if nxt:
                        for t in range(TN):
                            maximum(b + 1, 1 - p, h, t)
                        if h == 2:
                            mask_k(b + 1, 1 - p)
                        if h == 7:
                            shift(b + 1, 0)
                        if h == H - 1:
                            shift(b + 1, 1)
                    for i, (n, c, at) in enumerate(X_BODY):
                        if n in (1, 2) and nxt2 and at + 1 == h:
                            keys_values(XItem(i, b, p))
                    if nxt2 and h == 12:
                        mask_q(b + 2, p)
                    if not first and h in (3, 6, 10):
                        back_at(b - 1, (3, 6, 10).index(h))

            def first_keys_values():
                dve.wait_ge(wx_in, 16 * 8)
                keys_values(XItem(1))
                keys_values(XItem(2))

            ln_vector(dve, ch, XNx, 1, first_keys_values)
            for q in range(4):
                dve.wait_ge(qx_full, q + 1)
                dve.tensor_tensor(QX[:, 4 * q:4 * q + 4, :], tps[q % 2][:, :].rearrange("p (t d) -> p t d", d=D),
                                  bq_x[:, :].unsqueeze(1).broadcast_to([P, 4, D]), ALU.add).then_inc(qx_used, 1)
            dve.wait_ge(qx_used, 4)
            dve.wait_ge(xn_rdy, 2 * NT)
            ch.link(dve.tensor_copy(HIq[:], QX[:]))
            ch.step(dve.tensor_tensor(LOq[:], QX[:], HIq[:].bitcast(F32), ALU.subtract))
            ch.step(dve.tensor_tensor(X[:], X[:], bo_x[:, :].unsqueeze(1).broadcast_to([P, NT, D]), ALU.add))
            ch.sync()
            dve.sem_inc(q_prep, 1)
            dve.wait_ge(x_const, 1)

            dve.wait_ge(x_tdve, 2)
            dve.tensor_copy(VX[:, 0, :, :, 0:8], VST[:].rearrange("p t (h d) -> p t h d", d=HD)).then_inc(vx_rdy, 1)
            mask_q(0, 0)
            for h in range(H):
                for t in range(TN):
                    maximum(0, 0, h, t)
                if h == 7:
                    shift(0, 0)
                if h in (3, 5):
                    keys_values(XItem(10 + h // 5))
                if h == 10:
                    mask_k(0, 0)
                if h == 12:
                    mask_q(1, 1)
            shift(0, 1)
            x_batches(dve, body)
            for k in range(3):
                back_at(B - 1, k)

            dve.wait_ge(xb_used, 3 * B)
            ln_vector(dve, ch, XNf, 2)

            def split(i, p):
                e = i * 2 + p
                dve.wait_ge(ew_in[p], i * 16 + 16)
                wait(dve, y_full, (e - 1) * TB)
                dve.tensor_copy(W1h[:, p], W1[:, p]).then_inc(w1_high, 1)
                dve.wait_ge(w1_high, e + 1)
                dve.tensor_tensor(W1l[:, p], W1[:, p], W1h[:, p].bitcast(F32), ALU.subtract).then_inc(w1_parts, 1)

            split(0, 0)
            dve.wait_ge(rw_in, 16 * 5)
            dve.scalar_tensor_tensor(out=kw[:, :], in0=keysT[:, :], scalar=2.0, in1=rwT[:, :],
                                     op0=ALU.mult, op1=ALU.add).then_inc(kw_rdy, 1)
            dve.tensor_tensor(ksq[:, :], keysT[:, :], keysT[:, :], ALU.mult).then_inc(kw_rdy, 1)
            for q in range(4):
                cols = slice(512 * q, 512 * q + 512)
                dve.wait_ge(xt_rdy, 8 + q + 1)
                dve.wait_ge(xt_high, q + 1)
                dve.tensor_tensor(xTl[:, cols], xnTf[:, cols], xTh[:, cols].bitcast(F32), ALU.subtract).then_inc(xt_parts, 1)
            split(0, 1)
            dve.wait_ge(ks_full, 1)
            ch.link(dve.tensor_tensor(lc[:, :], rb_b[:, :], bps[:, 0:E], ALU.subtract))
            dve.wait_ge(lg_full, 1)
            logits = ops[:, :, :].rearrange("p a n -> p (a n)")
            ch.link(dve.tensor_tensor(LG[:], logits[:, 0:NT * E].rearrange("p (t e) -> p t e", e=E),
                                      lc[:, :].unsqueeze(1).broadcast_to([P, NT, E]), ALU.add))
            for t in range(NT):
                ch.step(dve.max(TOP[:, t, :], LG[:, t, :]))
            ch.sync()
            for t in range(NT):
                ch.step(dve.max_index(TOPI[:, t, :], TOP[:, t, :], LG[:, t, :]))
            ch.step(dve.tensor_tensor(EX[:], LG[:], TOP[:, :, 0:1].broadcast_to([P, NT, E]), ALU.subtract))
            ch.sync()
            dve.sem_inc(ex_in, 1)
            ch.link(dve.tensor_copy(TOPF[:], TOPI[:]))
            dve.wait_ge(rt_const, 1)
            iota_b = iota_f[:, :].unsqueeze(1).broadcast_to([P, NT, E])
            for j in range(TOPK):
                dst = EQ if j else PICK
                ch.link(dve.tensor_tensor(dst[:], iota_b, TOPF[:, :, j:j + 1].broadcast_to([P, NT, E]), ALU.is_equal))
                if j:
                    ch.link(dve.tensor_tensor(PICK[:], PICK[:], EQ[:], ALU.add))
            dve.wait_ge(ex_rdy, 1)
            ch.link(dve.tensor_tensor(EX[:], EX[:], PICK[:], ALU.mult))
            ch.link(dve.tensor_reduce(SM[:, :], EX[:], AX, ALU.add))
            ch.link(dve.reciprocal(RS[:, :], SM[:, :]))
            dve.tensor_tensor(WT[:], EX[:], RS[:, :].unsqueeze(2).broadcast_to([P, NT, E]), ALU.mult).then_inc(wt_rdy, 1)
            dve.wait_ge(wt_rdy, 1)
            dve.wait_ge(xn_rdy, 3 * NT)

            def biases(q):
                dve.wait_ge(bo_full, q + 1)
                dve.wait_ge(y_used, NT + 4 * q + 4)
                xq = X[:, 4 * q:4 * q + 4, :]
                dve.tensor_tensor(xq, logits.rearrange("p (t d) -> p t d", d=D), xq, ALU.add).then_inc(bo_used, 1)

            def add(e, k, tb, prior):
                dve.wait_ge(y_full, k + 1)
                if prior:
                    dve.wait_ge(y_used, (k - TB) * 4 + 4)
                for tt in range(4):
                    t = tb * 4 + tt
                    dve.scalar_tensor_tensor(out=X[:, t, :], in0=tps[tb % 2][:, tt * P:(tt + 1) * P],
                                             scalar=WT[:, t, bass.ts(e, 1)], in1=X[:, t, :],
                                             op0=ALU.mult, op1=ALU.add).then_inc(y_used, 1)

            def expert(i, p):
                e = i * 2 + p
                for tb in range(TB):
                    add(e, e * TB + tb, tb, not (isinstance(i, int) and i == 0 and p == 0))
                    if tb == 1 and not (isinstance(i, int) and (i == 0 and p == 0 or i == E // 2 - 1 and p == 1)):
                        split(i + p, 1 - p)
                    if isinstance(i, int) and i == 0 and p == 1:
                        biases(tb)

            expert(0, 0)
            expert(0, 1)
            dve.wait_ge(bo_used, TB)
            with dve.Fori(1, E // 2 - 1) as i:
                for p in range(2):
                    expert(i, p)
            for p in range(2):
                expert(E // 2 - 1, p)


_IN = {"x": "x", "wqT_s": "L0_attn_Wq", "wkT_s": "L0_attn_Wk", "wvT_s": "L0_attn_Wv", "woT_s": "L0_attn_Wo",
       "wqT_x": "L0_xattn_Wq", "wkT_x": "L0_xattn_Wk", "wvT_x": "L0_xattn_Wv", "woT_x": "L0_xattn_Wo",
       "bq_x": "L0_xattn_bq", "bk_x": "L0_xattn_bk", "bv_x": "L0_xattn_bv", "bo_x": "L0_xattn_bo",
       "ctx": "ctx_1024", "keysT": "L0_ffn_keys", "rwT": "L0_ffn_rw", "rb": "L0_ffn_rb",
       "w1T": "L0_ffn_w1", "b1": "L0_ffn_b1", "w2T": "L0_ffn_w2", "b2": "L0_ffn_b2"}


def lay_out(inputs):
    a = {k: np.asarray(inputs[v]) for k, v in _IN.items()}
    for k in a:
        if "T_" in k or k.endswith("T"):
            a[k] = a[k].swapaxes(-1, -2)
    mask = np.asarray(inputs["mask_Bx1xSxS2_bf1"]).reshape(B, N, M).view(np.uint8)
    a["b1"] = a["b1"].reshape(E, FC, P).transpose(2, 0, 1)
    a["mask"], a["maskT"] = mask, mask.transpose(0, 2, 1)
    return {k: np.ascontiguousarray(v) for k, v in a.items()}


def kernel(**inputs):
    import concourse.bacc as bacc
    from concourse.bass_utils import run_bass_kernel_spmd
    nc = bacc.Bacc("TRN2", target_bir_lowering=False, num_devices=1)
    arrays = lay_out(inputs)
    a = {k: nc.dram_tensor(k, v.shape, mybir.dt.from_np(v.dtype), kind="ExternalInput").ap()
         for k, v in arrays.items()}
    out = nc.dram_tensor("out", (B, N, D), F32, kind="ExternalOutput").ap()
    decoder_block(nc, a, out)
    r = run_bass_kernel_spmd(nc, [arrays], core_ids=[0])
    return r.results[0]["out"]
```
